# Optimizing a Trainium2 kernel written in Bass

```python
import numpy as np
import jax
import jax.numpy as jnp

def _softmax(x, axis=-1):
    return jax.nn.softmax(x, axis=axis)

def _gelu(x):
    return jax.nn.gelu(x, approximate=True)

def _silu(x):
    return jax.nn.silu(x)

def _sigmoid(x):
    return jax.nn.sigmoid(x)

def _layernorm(x, axis=-1, eps=1e-05):
    m = jnp.mean(x, axis=axis, keepdims=True)
    v = jnp.var(x, axis=axis, keepdims=True)
    return (x - m) / jnp.sqrt(v + eps)

def _scatter_add(tgt, idx, src, axis=0):
    return tgt.at[idx].add(src)

def _segment_sum(src, seg, n):
    return jax.ops.segment_sum(src, seg, n)
kernel_name = 'mk_flamingo_gated_d1_seqx_r4_51d8a4'

def setup_inputs(seed: int=0):
    np.random.seed(seed)
    _w = jnp.asarray

    def _rec_inputs():
        import jax
        import jax.numpy as jnp
        _rk = jax.random.key(seed)
        x = -0.0002928 + 1 * jax.random.normal(jax.random.fold_in(_rk, 1), (16, 256, 256), jnp.float32)
        _lenS = 256 - jax.random.randint(jax.random.fold_in(_rk, 7), (16,), 0, max(1, 256 // 4) + 1, jnp.int32)
        _lenS2 = 256 - jax.random.randint(jax.random.fold_in(_rk, 8), (16,), 0, max(1, 256 // 4) + 1, jnp.int32)
        _ctx_1024P = jax.random.normal(jax.random.fold_in(_rk, 11), (16, 16, 256), jnp.float32)
        _ctx_1024c = jax.random.dirichlet(jax.random.fold_in(_rk, 511), 0.3 * jnp.ones((16,), jnp.float32), (16, 256))
        _ctx_1024t = jnp.einsum('bsk,bkd->bsd', _ctx_1024c, _ctx_1024P)
        _ctx_1024t = _ctx_1024t * jax.lax.rsqrt(jnp.mean(jnp.square(_ctx_1024t)) + 1e-12) * 0.953939
        ctx_1024 = -1.39393e-06 + 0.999914 * (_ctx_1024t + 0.3 * jax.random.normal(jax.random.fold_in(_rk, 611), (16, 256, 256), jnp.float32))
        _g = jax.random.normal(jax.random.fold_in(_rk, 9001), (2, 1), jnp.float32)
        _g = jnp.sign(_g) * jnp.maximum(jnp.abs(_g), 1.0) + (_g == 0) * 1.0
        g_xattn = _g[0]
        g_ffn = _g[1]
        return (x, ctx_1024, g_xattn, g_ffn)
    x, ctx_1024, g_xattn, g_ffn = _rec_inputs()

    def _L0_xattn_setup():
        import jax, jax.numpy as jnp
        import numpy as np
        EMBD = 256
        NUM_HEAD = 16
        HEAD = EMBD // NUM_HEAD
        key = jax.random.key(seed)
        ks = jax.random.split(key, 9)
        B, S, D = (2, 512, EMBD)
        s = 1.0 / np.sqrt(D)
        return {'q': jax.random.normal(ks[0], (B, S, D), jnp.float32), 'k': jax.random.normal(ks[1], (B, S, D), jnp.float32), 'v': jax.random.normal(ks[2], (B, S, D), jnp.float32), 'Wq': jax.random.uniform(ks[3], (D, D), jnp.float32, -s, s), 'bq': jax.random.uniform(ks[4], (D,), jnp.float32, -s, s), 'Wk': jax.random.uniform(ks[5], (D, D), jnp.float32, -s, s), 'bk': jax.random.uniform(ks[6], (D,), jnp.float32, -s, s), 'Wv': jax.random.uniform(ks[7], (D, D), jnp.float32, -s, s), 'bv': jax.random.uniform(ks[8], (D,), jnp.float32, -s, s)}
    _L0_xattn_all = _L0_xattn_setup()
    _L0_xattn_in = {k: v for k, v in _L0_xattn_all.items() if k in ('Wq', 'bq', 'Wk', 'bk', 'Wv', 'bv')}
    del _L0_xattn_all

    def _L0_ffn_setup():
        import jax, jax.numpy as jnp
        import numpy as np
        TOP_K = 2
        key = jax.random.key(seed)
        k1, k2, k3, k4, k5 = jax.random.split(key, 5)
        B, S, D, F, E = (2, 256, 256, 512, 8)
        return {'x': jax.random.normal(k1, (B, S, D), dtype=jnp.float32), 'router_kernel_DE': jax.random.normal(k2, (D, E), dtype=jnp.float32) * 0.02, 'kernel_gating_EDF': jax.random.normal(k3, (E, D, F), dtype=jnp.float32) * 0.02, 'kernel_up_EDF': jax.random.normal(k4, (E, D, F), dtype=jnp.float32) * 0.02, 'kernel_down_EFD': jax.random.normal(k5, (E, F, D), dtype=jnp.float32) * 0.02}
    _L0_ffn_all = _L0_ffn_setup()
    _L0_ffn_in = {k: v for k, v in _L0_ffn_all.items() if k in ('router_kernel_DE', 'kernel_gating_EDF', 'kernel_up_EDF', 'kernel_down_EFD')}
    del _L0_ffn_all
    return {'x': x, 'ctx_1024': ctx_1024, 'g_xattn': g_xattn, 'g_ffn': g_ffn, 'L0_xattn_Wq': _L0_xattn_in['Wq'], 'L0_xattn_bq': _L0_xattn_in['bq'], 'L0_xattn_Wk': _L0_xattn_in['Wk'], 'L0_xattn_bk': _L0_xattn_in['bk'], 'L0_xattn_Wv': _L0_xattn_in['Wv'], 'L0_xattn_bv': _L0_xattn_in['bv'], 'L0_ffn_router_kernel_DE': _L0_ffn_in['router_kernel_DE'], 'L0_ffn_kernel_gating_EDF': _L0_ffn_in['kernel_gating_EDF'], 'L0_ffn_kernel_up_EDF': _L0_ffn_in['kernel_up_EDF'], 'L0_ffn_kernel_down_EFD': _L0_ffn_in['kernel_down_EFD']}

def reference(x, ctx_1024, g_xattn, g_ffn, L0_xattn_Wq, L0_xattn_bq, L0_xattn_Wk, L0_xattn_bk, L0_xattn_Wv, L0_xattn_bv, L0_ffn_router_kernel_DE, L0_ffn_kernel_gating_EDF, L0_ffn_kernel_up_EDF, L0_ffn_kernel_down_EFD):
    import jax
    import jax.numpy as jnp

    def _L0_xattn_ref(q, k, v, Wq, bq, Wk, bk, Wv, bv):
        import jax, jax.numpy as jnp
        import numpy as np
        EMBD = 256
        NUM_HEAD = 16
        HEAD = EMBD // NUM_HEAD
        B, S, D = q.shape
        H, Hd = (NUM_HEAD, HEAD)
        qp = jnp.einsum('bsd,ed->bse', q, Wq) + bq
        kp = jnp.einsum('bsd,ed->bse', k, Wk) + bk
        vp = jnp.einsum('bsd,ed->bse', v, Wv) + bv
        qp = qp.reshape(B, S, H, Hd).transpose(0, 2, 1, 3)
        kp = kp.reshape(B, S, H, Hd).transpose(0, 2, 1, 3)
        vp = vp.reshape(B, S, H, Hd).transpose(0, 2, 1, 3)
        score = jnp.einsum('bhqd,bhkd->bhqk', qp, kp) / jnp.sqrt(jnp.float32(Hd))
        attn = jax.nn.softmax(score, axis=-1)
        out = jnp.einsum('bhqk,bhkd->bhqd', attn, vp)
        return out.transpose(0, 2, 1, 3).reshape(B, S, H * Hd)

    def _L0_ffn_ref(x, router_kernel_DE, kernel_gating_EDF, kernel_up_EDF, kernel_down_EFD):
        import jax, jax.numpy as jnp
        import numpy as np
        TOP_K = 2
        E = router_kernel_DE.shape[-1]
        x = x.astype(jnp.float32)
        logits_BSE = jnp.einsum('BSD,DE->BSE', x, router_kernel_DE)
        probs_BSE = jax.nn.softmax(logits_BSE.astype(jnp.float32), axis=-1)
        weights_BSK, indices_BSK = jax.lax.top_k(probs_BSE, TOP_K)
        norm_weights_BSK = jax.nn.softmax(weights_BSK, axis=-1)
        one_hot_BSKE = jax.nn.one_hot(indices_BSK, num_classes=E, dtype=x.dtype)
        full_weights_BSE = jnp.sum(one_hot_BSKE * norm_weights_BSK[..., None], axis=2)
        gating_BSEF = jnp.einsum('BSD,EDF->BSEF', x, kernel_gating_EDF)
        act_BSEF = jax.nn.silu(gating_BSEF)
        up_BSEF = jnp.einsum('BSD,EDF->BSEF', x, kernel_up_EDF)
        fuse_BSEF = act_BSEF * up_BSEF
        down_BSED = jnp.einsum('BSEF,EFD->BSED', fuse_BSEF, kernel_down_EFD)
        out_BSD = jnp.einsum('BSED,BSE->BSD', down_BSED, full_weights_BSE)
        return out_BSD.astype(jnp.float32)
    x = x + jnp.tanh(g_xattn[0]) * _L0_xattn_ref(_layernorm(x, axis=-1), ctx_1024, ctx_1024, L0_xattn_Wq, L0_xattn_bq, L0_xattn_Wk, L0_xattn_bk, L0_xattn_Wv, L0_xattn_bv)
    x = x + jnp.tanh(g_ffn[0]) * _L0_ffn_ref(_layernorm(x, axis=-1), L0_ffn_router_kernel_DE, L0_ffn_kernel_gating_EDF, L0_ffn_kernel_up_EDF, L0_ffn_kernel_down_EFD)
    return x

_drawn_inputs = setup_inputs


def setup_inputs(seed=0):
    import zlib

    import numpy as np

    out = dict(_drawn_inputs(seed))
    spreads = {}
    factors = {'L0_xattn_bq': 8.0,
     'L0_xattn_bk': 8.0,
     'L0_ffn_router_kernel_DE': 4.214,
     'L0_ffn_kernel_gating_EDF': 3.675,
     'L0_ffn_kernel_up_EDF': 3.643,
     'L0_ffn_kernel_down_EFD': 3.638}
    for name, (base, spread) in spreads.items():
        noise = np.random.default_rng([zlib.crc32(name.encode()), seed]).standard_normal(out[name].shape)
        drawn = base * np.exp(spread * noise) if base else spread * noise
        out[name] = jnp.asarray(drawn.astype(out[name].dtype))
    for name, factor in factors.items():
        out[name] = (out[name] * factor).astype(out[name].dtype)
    return out
```

```python
from contextlib import ExitStack

import numpy as np

import concourse.bass as bass
from concourse import mybir

F32 = mybir.dt.float32
BF16 = mybir.dt.bfloat16
I32 = mybir.dt.int32
U32 = mybir.dt.uint32
ACT = mybir.ActivationFunctionType
ALU = mybir.AluOpType
AX = mybir.AxisListType

P = 128
B, S, D = 16, 256, 256
H, HD = 16, 16
E, F = 8, 512
TOKENS = B * S
DT = D // P
FT = F // P
QT = S // P
PARTS = 6
KROWS = PARTS * HD
MROWS = 2
STRIP = 32
VW = HD + 1
GROUP = 4
EPS = 1e-5
K_TOP = 2
TABLE = E * TOKENS
MAX_TILES = TOKENS * K_TOP // P + E
SPARE = P
TABLE_ROWS = TABLE + E * P
ROUTE_STEPS = 21


class Step:

    def __init__(self, i, c):
        self.i, self.c = i, c

    def to(self, k):
        return Step(self.i, self.c + k)

    def live(self):
        return not isinstance(self.i, int) or 0 <= self.c < B

    def count(self, each, more=0):
        return 2 * each * self.i + (each * self.c + more)

    def after_first(self, each, more=0):
        return not isinstance(self.i, int) or each * self.c + more > 0

    def turn(self):
        return self.c % 2

    def landed(self, each=16):
        return each * self.i + each * (self.c // 2 + 1)

    def second(self):
        return not isinstance(self.i, int) or self.c >= 2

    def rows(self):
        return bass.ds((2 * self.i + self.c) * S, S)


def program(nc, x, ctx_t, g_xattn, g_ffn, wq_t, bq, wk_t, bk, wv_t, bv, w_router, w_gate, w_up, w_down, out):
    stack = ExitStack()
    with stack:

        def sb(name, shape, dt=F32):
            return stack.enter_context(nc.sbuf_tensor(name, shape, dt))

        def sem(name):
            return stack.enter_context(nc.semaphore(name))

        def sems(name, n):
            return [sem(f"{name}{k}") for k in range(n)]

        normed = nc.dram_tensor("normed_rows", [TOKENS + SPARE, D], F32, kind="Internal").ap()
        table = nc.dram_tensor("expert_rows", [TABLE_ROWS, 2], F32, kind="Internal").ap()

        ident = sb("ident", [P, P])
        ident_b = sb("ident_b", [P, P], BF16)
        earlier = sb("earlier", [P, P], BF16)
        ones_b = sb("ones_b", [P, P], BF16)
        wq_sb = sb("wq_sb", [P, DT, D])
        wk_sb = sb("wk_sb", [P, DT, D])
        wv_sb = sb("wv_sb", [P, DT, D])
        wr_sb = sb("wr_sb", [P, DT, E])
        bqk = sb("bqk", [P, 2, D])
        bv_sb = sb("bv_sb", [P, D])
        gates = sb("gates", [P, 2])
        tanh_g = sb("tanh_g", [P, 2])
        prefer = sb("prefer", [P, E])
        token_f = sb("token_f", [P, QT])
        base = sb("base", [P, E])
        zeros = sb("zeros", [P, D])
        fill_id = sb("fill_id", [P, TABLE_ROWS // P], I32)
        fill = sb("fill", [P, TABLE_ROWS // P, 2])
        w_gu = sb("w_gu", [P, DT, 2, E, F])

        work = sb("work", [P, 27136])
        at = [0]

        def take(n_f32):
            a = work[:, at[0]:at[0] + n_f32]
            at[0] += n_f32
            return a

        xin = [take(QT * D).rearrange("p (j d) -> p j d", j=QT) for _ in range(2)]
        xres = [take(QT * D).rearrange("p (j d) -> p j d", j=QT) for _ in range(2)]
        ctx_sb = [take(DT * S).rearrange("p (t s) -> p t s", t=DT) for _ in range(2)]
        xhat = take(QT * D).rearrange("p (j d) -> p j d", j=QT)
        xhat_t = take(DT * S).rearrange("p (t s) -> p t s", t=DT)
        qkf = [take(2 * D) for _ in range(QT)]
        rest = [take(2 * D) for _ in range(QT)]
        parts = [take(PARTS * D).bitcast(BF16).rearrange("p (t h r d) -> p t h r d", t=2, h=H, r=PARTS)
                 for _ in range(QT)]
        q_st = [take(H * S // 2).bitcast(BF16).rearrange("p (h s) -> p h s", h=H) for _ in range(2)]
        k_st = [take(H * S // 2).bitcast(BF16).rearrange("p (h s) -> p h s", h=H) for _ in range(2)]
        v_aug = [take(QT * H * STRIP).rearrange("p (j h d) -> p j h d", j=QT, h=H) for _ in range(2)]
        NPROB = 8
        probs = [take(QT * S) for _ in range(NPROB)]
        heads_t = [take(2 * S) for _ in range(2)]
        x1 = [take(QT * D).rearrange("p (j d) -> p j d", j=QT) for _ in range(2)]
        xn = [take(QT * D).rearrange("p (j d) -> p j d", j=QT) for _ in range(2)]
        xn_t = take(DT * S).rearrange("p (t s) -> p t s", t=DT)
        assert at[0] <= 27136, at[0]
        at[0] = 0
        w_dn = take(FT * E * D).rearrange("p (t e d) -> p t e d", t=FT, e=E)
        NX = 4
        rows_in = [take(D) for _ in range(NX)]
        rows_t = [take(DT * P).rearrange("p (t s) -> p t s", t=DT) for _ in range(2)]
        silu = [take(F) for _ in range(2)]
        hid = [take(F) for _ in range(2)]
        hid_t = [take(FT * P).rearrange("p (t s) -> p t s", t=FT) for _ in range(2)]
        y_sb = [take(D) for _ in range(2)]

        maxes = sb("maxes", [P, QT, H])
        max_parts = sb("max_parts", [P, QT, MROWS, H], BF16)
        max_t = [sb(f"max_t{k}", [MROWS * H, S], BF16) for k in range(2)]
        stats = sb("stats", [P, QT, 6])
        mv = sb("mv", [P, QT, 2])
        rstd = sb("rstd", [P, QT])
        stats2 = sb("stats2", [P, QT, 6])
        mv2 = sb("mv2", [P, QT, 2])
        rstd2 = sb("rstd2", [P, QT])
        den = sb("den", [P, QT, H])
        minus_half = sb("minus_half", [P, QT])
        lg = sb("lg", [P, QT, E])
        ex = sb("ex", [P, QT, E])
        pr = sb("pr", [P, QT, E])
        eq = sb("eq", [P, QT, E])
        key = sb("key", [P, QT, E])
        sel = [sb(f"sel{k}", [P, QT, E]) for k in range(K_TOP)]
        routed = sb("routed", [P, QT, E], BF16)
        r1 = sb("r1", [P, QT])
        r2 = sb("r2", [P, QT])
        best = sb("best", [P, QT])
        edge = sb("edge", [P, QT])
        edge_e = sb("edge_e", [P, QT])
        pos = sb("pos", [P, QT, E])
        slot_f = sb("slot_f", [P, K_TOP, QT])
        slots = [sb(f"slots{k}", [P, K_TOP * QT], U32) for k in range(2)]
        entry = [sb(f"entry{k}", [P, K_TOP * QT, 2]) for k in range(2)]
        count_i = sb("count_i", [P, E], I32)
        n_tiles = sb("n_tiles", [P, E])
        cum_a = sb("cum_a", [P, E])
        cum_b = sb("cum_b", [P, E])
        tile_no = sb("tile_no", [P, MAX_TILES])
        past = sb("past", [P, MAX_TILES, E])
        past_n = sb("past_n", [P, MAX_TILES, E])
        t_exp = sb("t_exp", [P, MAX_TILES])
        t_row = sb("t_row", [P, MAX_TILES])
        plan_exp = sb("plan_exp", [P, MAX_TILES], I32)
        plan_row = sb("plan_row", [P, MAX_TILES], I32)
        NW = 4
        U = 4
        assert MAX_TILES % U == 0
        row_info = [sb(f"row_info{k}", [P, 2]) for k in range(NW)]

        bank = [stack.enter_context(nc.psum_tensor(f"bank{k}", [P, 512], F32)) for k in range(8)]
        st_bank = [bank[0], bank[1]]
        s_bank = [bank[2], bank[3]]
        pv_bank = bank[4]
        bank_a, bank_b, bank_c = bank[5], bank[6], bank[7]

        iota_done, const_ready, gate_in = sem("iota_done"), sem("const_ready"), sem("gate_in")
        gate_ready = sem("gate_ready")
        w_in, bias_in, fill_ready, fill_out = sem("w_in"), sem("bias_in"), sem("fill_ready"), sem("fill_out")
        ffn_w_in, down_w_in = sem("ffn_w_in"), sem("down_w_in")
        x_in, xres_in, ctx_in = sems("x_in", 2), sems("xres_in", 2), sems("ctx_in", 2)
        max_in, x1_out, xn_out, table_out = (sems("max_in", 2), sems("x1_out", 2), sems("xn_out", 2),
                                             sems("table_out", 2))
        xhat_t_ps, proj_ps, v_ps, stack_ps = sem("xhat_t_ps"), sem("proj_ps"), sem("v_ps"), sem("stack_ps")
        s_ps, max_t_ps, st_ps, pv_ps = sem("s_ps"), sem("max_t_ps"), sem("st_ps"), sem("pv_ps")
        heads_ps, xn_t_ps, logit_ps, rank_ps = (sem("heads_ps"), sem("xn_t_ps"), sem("logit_ps"),
                                                sem("rank_ps"))
        xhat_t_sb, part1, part2, stack_b_sb = sem("xhat_t_sb"), sem("part1"), sem("part2"), sem("stack_b_sb")
        max_t_sb, exp_done, heads_sb, xn_t_sb = (sem("max_t_sb"), sem("exp_done"), sem("heads_sb"),
                                                 sem("xn_t_sb"))
        route_exp = sem("route_exp")
        var_ready, var2_ready = sem("var_ready"), sem("var2_ready")
        xhat_ready, qkf_ready, parts_ready, v_sb = (sem("xhat_ready"), sem("qkf_ready"), sem("parts_ready"),
                                                    sem("v_sb"))
        stack_a_sb, max_done, max_ready, x1_ready = (sem("stack_a_sb"), sem("max_done"), sem("max_ready"),
                                                     sem("x1_ready"))
        xn_ready, route_in, routed_ready, rank_used = (sem("xn_ready"), sem("route_in"), sem("routed_ready"),
                                                       sem("rank_used"))
        entry_ready, plan_ready = sem("entry_ready"), sem("plan_ready")
        fill_step, norm_step, norm2_step, res_step = (sem("fill_step"), sem("norm_step"), sem("norm2_step"),
                                                      sem("res_step"))
        max_step, route_step, plan_step = sem("max_step"), sem("route_step"), sem("plan_step")
        dve_went_on, pool_went_on, sp_went_on = sem("dve_went_on"), sem("pool_went_on"), sem("sp_went_on")
        rest_ready, part3 = sem("rest_ready"), sem("part3")
        rstd_ready, rstd2_ready = sem("rstd_ready"), sem("rstd2_ready")
        info_in, rows_got, y_out = sems("info_in", NW), sems("rows_got", NX), sem("y_out")
        rows_ps, rows_sb, gate_ps, up_ps = sem("rows_ps"), sem("rows_sb"), sem("gate_ps"), sem("up_ps")
        silu_done, hid_ready, hid_ps, hid_sb = sem("silu_done"), sem("hid_ready"), sem("hid_ps"), sem("hid_sb")
        y_ps, y_ready = sem("y_ps"), sem("y_ready")

        x_rows = x.rearrange("b s d -> (b s) d")

        def token_tiles(dram, step):
            return dram[step.rows(), :].rearrange("(j p) d -> p j d", p=P)

        FIRST, LAST = 2, B - 3
        PAIRS = (LAST - FIRST + 1) // 2

        def steps(eng, one):
            for c in range(-2, FIRST):
                one(Step(0, c))
            with eng.Fori(0, PAIRS) as i:
                for c in range(2):
                    one(Step(i, FIRST + c))
            for c in range(LAST + 1, B + 1):
                one(Step(0, c))

        block = stack.enter_context(nc.Block())

        @block.sync
        def _(sp):
            def load(step):
                k = step.turn()
                if step.second():
                    sp.wait_ge(xhat_ready, step.count(QT, -QT))
                    sp.sem_inc(sp_went_on, 1)
                sp.dma_start(xin[k], token_tiles(x_rows, step)).then_inc(x_in[k], 16)
                if step.second():
                    sp.wait_ge(v_ps, step.count(1, -1))
                    sp.sem_inc(sp_went_on, 1)
                sp.dma_start(ctx_sb[k], ctx_t[:, step.rows()].rearrange("(t p) s -> p t s", p=P)
                             ).then_inc(ctx_in[k], 16)

            sp.dma_start(xin[0], token_tiles(x_rows, Step(0, 0))).then_inc(x_in[0], 16)
            sp.dma_start(wq_sb[:, :, :], wq_t.rearrange("(t p) n -> p t n", p=P)).then_inc(w_in, 16)
            sp.dma_start(ctx_sb[0], ctx_t[:, 0:S].rearrange("(t p) s -> p t s", p=P)).then_inc(ctx_in[0], 16)
            sp.dma_start(wk_sb[:, :, :], wk_t.rearrange("(t p) n -> p t n", p=P)).then_inc(w_in, 16)
            sp.dma_start(bqk[:, 0, :], bq.partition_broadcast(P)).then_inc(bias_in, 16)
            sp.dma_start(bqk[:, 1, :], bk.partition_broadcast(P)).then_inc(bias_in, 16)
            sp.dma_start(wv_sb[:, :, :], wv_t.rearrange("(t p) n -> p t n", p=P)).then_inc(w_in, 16)
            sp.dma_start(bv_sb[:, :], bv.partition_broadcast(P)).then_inc(bias_in, 16)
            sp.dma_start(wr_sb[:, :, :], w_router.rearrange("(t p) e -> p t e", p=P)).then_inc(w_in, 16)
            load(Step(0, 1))
            sp.wait_ge(const_ready, 1)
            sp.dma_start(out[TOKENS:TOKENS + SPARE, :], zeros[:, :]).then_inc(fill_out, 16)
            sp.dma_start(normed[TOKENS:TOKENS + SPARE, :], zeros[:, :]).then_inc(fill_out, 16)
            sp.wait_ge(fill_ready, 1)
            sp.dma_start(table.rearrange("(p a) w -> p a w", p=P), fill[:, :, :]).then_inc(fill_out, 16)

            def one(step):
                prep, nxt, post = step.to(2), step.to(1), step.to(-1)
                if prep.live() and step.c >= 0:
                    load(prep)
                if step.live():
                    k = step.turn()
                    if step.second():
                        sp.wait_ge(x1_ready, step.count(QT, -QT))
                        sp.sem_inc(sp_went_on, 1)
                    sp.dma_start(xres[k], token_tiles(x_rows, step)).then_inc(xres_in[k], 16)
                if post.live():
                    k = post.turn()
                    sp.wait_ge(x1_ready, post.count(QT, QT))
                    sp.sem_inc(sp_went_on, 1)
                    sp.dma_start(token_tiles(out, post), x1[k]).then_inc(x1_out[k], 16)
                    sp.wait_ge(xn_ready, post.count(QT, QT))
                    sp.sem_inc(sp_went_on, 1)
                    sp.dma_start(token_tiles(normed, post), xn[k]).then_inc(xn_out[k], 16)
                if nxt.live():
                    k = nxt.turn()
                    sp.wait_ge(max_t_sb, nxt.count(1, 1))
                    sp.sem_inc(sp_went_on, 1)
                    if nxt.after_first(H, -H):
                        sp.wait_ge(st_ps, nxt.count(H, -H))
                        sp.sem_inc(sp_went_on, 1)
                    for m in range(MROWS):
                        sp.dma_start(q_st[k][KROWS + m:KROWS + m + 1, :, :], max_t[k][m * H:(m + 1) * H, :]
                                     ).then_inc(max_in[k], 16)

            steps(sp, one)
            sp.wait_ge(pv_ps, B * H // GROUP)
            sp.wait_ge(xn_t_ps, B)
            sp.wait_ge(x1_out[0], 16 * B // 2)
            sp.wait_ge(x1_out[1], 16 * B // 2)
            sp.wait_ge(xn_out[0], 16 * B // 2)
            sp.wait_ge(xn_out[1], 16 * B // 2)
            sp.wait_ge(logit_ps, B)
            for t in range(FT):
                sp.dma_start(w_dn[:, t, :, :], w_down[:, t * P:(t + 1) * P, :].rearrange("e p d -> p e d")
                             ).then_inc(down_w_in, 16)
            sp.wait_ge(plan_ready, 1)
            sp.wait_ge(table_out[0], 16 * K_TOP * QT * B // 2)
            sp.wait_ge(table_out[1], 16 * K_TOP * QT * B // 2)
            sp.wait_ge(fill_out, 48)

            def info(k, number, used):
                if used is not None:
                    sp.wait_ge(y_ready, used)
                    sp.sem_inc(sp_went_on, 1)
                    sp.wait_ge(y_out, 16 * used)
                    sp.sem_inc(sp_went_on, 1)
                row = sp.value_load(plan_row[0:1, number], min_val=0, max_val=TABLE_ROWS - P)
                sp.dma_start(row_info[k][:, :], table[bass.ds(row, P), :]).then_inc(info_in[k], 16)

            for k in range(NW):
                info(k, slice(k, k + 1), None)
            with sp.Fori(1, MAX_TILES // NW) as i:
                for k in range(NW):
                    info(k, bass.ds(NW * i + k, 1), NW * i + (k + 1 - NW))
            sp.wait_ge(y_out, 16 * MAX_TILES)

        @block.gpsimd
        def _(pool):
            nc.gpsimd.memset(ident[:, :], 0.0)
            nc.gpsimd.memset(ident_b[:, :], 0.0)
            nc.gpsimd.memset(earlier[:, :], 1.0)
            nc.gpsimd.memset(ones_b[:, :], 1.0).then_inc(iota_done, 1)
            pool.wait_ge(iota_done, 1)
            nc.gpsimd.affine_select(out=ident[:, :], in_=ident[:, :], compare_op=ALU.not_equal, fill=1.0,
                                    base=0, pattern=[[-1, P]], channel_multiplier=1)
            nc.gpsimd.affine_select(out=ident_b[:, :], in_=ident_b[:, :], compare_op=ALU.not_equal, fill=1.0,
                                    base=0, pattern=[[-1, P]], channel_multiplier=1)
            nc.gpsimd.affine_select(out=earlier[:, :], in_=earlier[:, :], compare_op=ALU.is_gt, fill=0.0,
                                    base=0, pattern=[[1, P]], channel_multiplier=-1)
            nc.gpsimd.memset(zeros[:, :], 0.0)
            nc.gpsimd.memset(minus_half[:, :], -0.5)
            for k in range(2):
                nc.gpsimd.memset(v_aug[k][:, :, :, HD:STRIP], 0.0)
            nc.gpsimd.iota(fill_id[:, :], pattern=[[1, TABLE_ROWS // P]], base=0,
                           channel_multiplier=TABLE_ROWS // P)
            nc.gpsimd.iota(token_f[:, :], pattern=[[P, QT]], base=0, channel_multiplier=1,
                           allow_small_or_imprecise_dtypes=True)
            nc.gpsimd.iota(prefer[:, :], pattern=[[-1, E]], base=E, channel_multiplier=0,
                           allow_small_or_imprecise_dtypes=True)
            nc.gpsimd.iota(base[:, :], pattern=[[TOKENS, E]], base=0, channel_multiplier=0,
                           allow_small_or_imprecise_dtypes=True)
            nc.gpsimd.iota(tile_no[:, :], pattern=[[1, MAX_TILES]], base=0, channel_multiplier=0,
                           allow_small_or_imprecise_dtypes=True)
            nc.gpsimd.memset(fill[:, :, 1:2], 0.0).then_inc(iota_done, 1)
            pool.wait_ge(iota_done, 2)
            for k in range(2):
                nc.gpsimd.memset(v_aug[k][:, :, :, HD:VW], 1.0)
            nc.gpsimd.nop().then_inc(const_ready, 1)

            def one(step):
                prep, post = step.to(2), step.to(-1)

                def residue(j):
                    pool.wait_ge(part1, prep.count(QT, j + 1))
                    if prep.after_first(QT, j - 1):
                        pool.wait_ge(part3, prep.count(QT, j - 1))
                    nc.gpsimd.tensor_tensor(
                        rest[j].rearrange("p (t h d) -> p t h d", t=2, h=H),
                        qkf[j].rearrange("p (t h d) -> p t h d", t=2, h=H),
                        parts[j][:, :, :, 0, :], ALU.subtract).then_inc(rest_ready, 1)

                def third(j):
                    pool.wait_ge(part2, prep.count(QT, j + 1))
                    pool.wait_ge(rest_ready, prep.count(QT, j + 1))
                    r = rest[j].rearrange("p (t h d) -> p t h d", t=2, h=H)
                    nc.gpsimd.tensor_tensor(parts[j][:, 0, :, 5, :], r[:, 0, :, :], parts[j][:, 0, :, 3, :],
                                            ALU.subtract)
                    nc.gpsimd.tensor_tensor(parts[j][:, 1, :, 2, :], r[:, 1, :, :], parts[j][:, 1, :, 1, :],
                                            ALU.subtract).then_inc(part3, 1)

                if prep.live():
                    pool.wait_ge(var_ready, prep.count(1, 1))
                    if prep.after_first(QT, 0):
                        pool.wait_ge(xhat_ready, prep.count(QT, 0))
                    nc.gpsimd.tensor_tensor(rstd[:, :], mv[:, :, 1], minus_half[:, :], ALU.pow).then_inc(rstd_ready, 1)
                if post.live():
                    pool.wait_ge(var2_ready, post.count(1, 1))
                    if post.after_first(QT, 0):
                        pool.wait_ge(xn_ready, post.count(QT, 0))
                    nc.gpsimd.tensor_tensor(rstd2[:, :], mv2[:, :, 1], minus_half[:, :], ALU.pow
                                            ).then_inc(rstd2_ready, 1)
                if prep.live():
                    residue(0)
                    third(0)
                    residue(1)
                    third(1)
                if post.live():
                    k = post.turn()
                    if isinstance(post.i, int) and post.c == 0:
                        pool.wait_ge(fill_out, 48)
                    pool.wait_ge(entry_ready, post.count(1, 1))
                    pool.sem_inc(pool_went_on, 1)
                    for n in range(K_TOP * QT):
                        nc.gpsimd.indirect_dma_start(
                            out=table[:, :], out_offset=bass.IndirectOffsetOnAxis(ap=slots[k][:, n:n + 1], axis=0),
                            in_=entry[k][:, n, :], in_offset=None).then_inc(table_out[k], 16)

            steps(pool, one)

            def gather(k, w, landed, used):
                pool.wait_ge(info_in[w], landed)
                if used is not None:
                    pool.wait_ge(rows_ps, used)
                pool.sem_inc(pool_went_on, 1)
                nc.gpsimd.indirect_dma_start(
                    out=rows_in[k], out_offset=None, in_=normed[:, :],
                    in_offset=bass.IndirectOffsetOnAxis(ap=row_info[w][:, 0:1].bitcast(U32), axis=0)
                ).then_inc(rows_got[k], 16)

            def scatter(k, w, number):
                pool.wait_ge(y_ready, number + 1)
                if not isinstance(number, int) or number > 0:
                    pool.wait_ge(y_out, 16 * number)
                pool.sem_inc(pool_went_on, 1)
                nc.gpsimd.indirect_dma_start(
                    out=out[:, :], out_offset=bass.IndirectOffsetOnAxis(ap=row_info[w][:, 0:1].bitcast(U32), axis=0),
                    in_=y_sb[k], in_offset=None, compute_op=ALU.add).then_inc(y_out, 16)

            for k in range(2):
                pool.wait_ge(x1_out[k], 16 * B // 2)
                pool.wait_ge(xn_out[k], 16 * B // 2)
            pool.wait_ge(fill_out, 48)
            pool.wait_ge(pv_ps, B * H // GROUP)
            pool.wait_ge(logit_ps, B)
            for n in range(2):
                gather(n % NX, n % NW, 16, None)

            def turn(i, first, last):
                for n in range(U):
                    if not (last and n >= U - 2):
                        m = n + 2
                        gather(m % NX, m % NW, 16 * (U // NW) * i + 16 * (m // NW + 1),
                               None if first and m < NX else U * i + (m - NX + 1))
                    scatter(n % 2, n % NW, U * i + n)

            turn(0, True, False)
            with pool.Fori(1, MAX_TILES // U - 1) as i:
                turn(i, False, False)
            turn(MAX_TILES // U - 1, False, True)

        @block.scalar
        def _(act):
            act.dma_start(gates[:, 0:1], g_xattn.partition_broadcast(P)).then_inc(gate_in, 16)
            act.dma_start(gates[:, 1:2], g_ffn.partition_broadcast(P)).then_inc(gate_in, 16)
            for dt in range(DT):
                for g, w in enumerate((w_gate, w_up)):
                    act.dma_start(w_gu[:, dt, g, :, :], w[:, dt * P:(dt + 1) * P, :].rearrange("e p f -> p e f")
                                  ).then_inc(ffn_w_in, 16)
            act.wait_ge(gate_in, 32)
            nc.scalar.activation(tanh_g[:, :], gates[:, :], ACT.Tanh).then_inc(gate_ready, 1)

            def one(step):
                nxt, prep, post = step.to(1), step.to(2), step.to(-1)

                def first_part(j):
                    act.wait_ge(qkf_ready, prep.count(QT, j + 1))
                    if prep.after_first(8, 0):
                        act.wait_ge(stack_ps, prep.count(8, 0))
                    nc.scalar.copy(parts[j][:, :, :, 0, :],
                                   qkf[j].rearrange("p (t h d) -> p t h d", t=2, h=H)).then_inc(part1, 1)

                def second_part(j):
                    act.wait_ge(rest_ready, prep.count(QT, j + 1))
                    r = rest[j].rearrange("p (t h d) -> p t h d", t=2, h=H)
                    nc.scalar.copy(parts[j][:, 0, :, 3, :], r[:, 0, :, :])
                    nc.scalar.copy(parts[j][:, 1, :, 1, :], r[:, 1, :, :]).then_inc(part2, 1)

                def stack_out(n):
                    j, h0 = n // 2, 8 * (n % 2)
                    act.wait_ge(stack_ps, nxt.count(8, 2 * n + 2))
                    if nxt.after_first(H, -H):
                        act.wait_ge(st_ps, nxt.count(H, -H))
                    nc.scalar.copy(
                        k_st[nxt.turn()][0:KROWS, h0:h0 + 8, j * P:(j + 1) * P],
                        bank_b[:, :].bitcast(BF16)[0:KROWS, :].rearrange("p (h s) -> p h s", h=8)
                    ).then_inc(stack_b_sb, 1)

                def heads_out(el, half):
                    act.wait_ge(pv_ps, el.count(4, 2 * half + 2))
                    if el.after_first(QT, 0):
                        act.wait_ge(heads_ps, el.count(QT, 0))
                    nc.scalar.copy(heads_t[half], pv_bank[:, :]).then_inc(heads_sb, 1)

                for h in range(H):
                    if step.live():
                        act.wait_ge(st_ps, step.count(H, h + 1))
                        if step.after_first(4, (h - NPROB) // GROUP + 1):
                            act.wait_ge(pv_ps, step.count(4, (h - NPROB) // GROUP + 1))
                        nc.scalar.activation(probs[h % NPROB], st_bank[h % 2][:, :], ACT.Exp,
                                             scale=float(HD) ** -0.5).then_inc(exp_done, 1)
                    if nxt.live() and h < 4:
                        stack_out(h)
                    if post.live() and h == 2:
                        heads_out(post, 1)
                    if prep.live() and h == 6:
                        act.wait_ge(xhat_t_ps, prep.count(1, 1))
                        if prep.after_first(QT, 0):
                            act.wait_ge(proj_ps, prep.count(QT, 0))
                        nc.scalar.copy(xhat_t.rearrange("p t s -> p (t s)"), bank_c[:, :]).then_inc(xhat_t_sb, 1)
                    if post.live() and h == 8:
                        act.wait_ge(xn_t_ps, post.count(1, 1))
                        if post.after_first(1, 0):
                            act.wait_ge(logit_ps, post.count(1, 0))
                        nc.scalar.copy(xn_t.rearrange("p t s -> p (t s)"), bank_c[:, :]).then_inc(xn_t_sb, 1)
                    if prep.live() and h == 9:
                        first_part(0)
                    if step.live() and h == 10:
                        heads_out(step, 0)
                    if prep.live() and h == 11:
                        second_part(0)
                        first_part(1)
                    if post.live() and h == 11:
                        act.wait_ge(route_in, post.count(2, 1))
                        nc.scalar.activation(ex[:, :, :], lg[:, :, :], ACT.Exp).then_inc(route_exp, 1)
                    if prep.live() and h == 13:
                        second_part(1)
                    if nxt.live() and h == 13:
                        act.wait_ge(max_t_ps, nxt.count(1, 1))
                        if nxt.second():
                            act.wait_ge(max_in[nxt.turn()], nxt.to(-2).landed(16 * MROWS))
                        nc.scalar.copy(max_t[nxt.turn()][:, :],
                                       bank_c[:, :].bitcast(BF16)[0:MROWS * H, 0:S]).then_inc(max_t_sb, 1)
                    if post.live() and h == 14:
                        act.wait_ge(route_in, post.count(2, 2))
                        nc.scalar.activation(edge_e[:, :], edge[:, :], ACT.Exp).then_inc(route_exp, 1)

            steps(act, one)

            def tile(k, number):
                act.wait_ge(gate_ps, number + 1)
                nc.scalar.activation(silu[k], bank[1][:, :], ACT.Silu).then_inc(silu_done, 1)
                act.wait_ge(hid_ps, number + 1)
                if not isinstance(number, int) or number >= 2:
                    act.wait_ge(y_ps, number - 1)
                nc.scalar.copy(hid_t[k].rearrange("p t s -> p (t s)"), bank[3][:, :]).then_inc(hid_sb, 1)

            for n in range(2):
                tile(n, n)
            with act.Fori(1, MAX_TILES // 2) as i:
                for k in range(2):
                    tile(k, 2 * i + k)

        @block.vector
        def _(dve):
            dve.wait_ge(const_ready, 1)
            nc.vector.tensor_scalar(fill_id[:, :], fill_id[:, :], P - 1, None, ALU.bitwise_and
                                    ).then_inc(fill_step, 1)
            dve.wait_ge(fill_step, 1)
            nc.vector.tensor_scalar(fill[:, :, 0].bitcast(I32), fill_id[:, :], TOKENS, None, ALU.add
                                    ).then_inc(fill_ready, 1)
            for k in range(2):
                nc.vector.memset(k_st[k][KROWS:P, :, :], -1.0)
            dve.wait_ge(bias_in, 48)

            def by_head(a, d=HD):
                return a.rearrange("p (h d) -> p h d", d=d)

            def norm_stats(el, stats_of, mv_of, source, steps_sem, done):
                for j in range(QT):
                    nc.vector.bn_stats(stats_of[:, j, :], source[:, j, :]).then_inc(steps_sem, 1)
                for j in range(QT):
                    dve.wait_ge(steps_sem, el.count(4, j + 1))
                    dve.sem_inc(dve_went_on, 1)
                    nc.vector.bn_aggr(mv_of[:, j, :], stats_of[:, j, :]).then_inc(steps_sem, 1)
                dve.wait_ge(steps_sem, el.count(4, 4))
                nc.vector.tensor_scalar(mv_of[:, :, 1], mv_of[:, :, 1], EPS, None, ALU.add).then_inc(done, 1)

            def norm_apply(mv_of, rstd_of, source, target, done):
                for j in range(QT):
                    nc.vector.tensor_scalar(target[:, j, :], source[:, j, :], mv_of[:, j, 0:1],
                                            rstd_of[:, j:j + 1], ALU.subtract, ALU.mult).then_inc(done, 1)

            def one(step):
                nxt, prep, post = step.to(1), step.to(2), step.to(-1)

                def replicate(el, j):
                    dve.wait_ge(part3, el.count(QT, j + 1))
                    p = parts[j]
                    nc.vector.tensor_copy(p[:, 0, :, 1:3, :], p[:, 0, :, 0:1, :].to_broadcast([P, H, 2, HD]))
                    nc.vector.tensor_copy(p[:, 1, :, 3:6:2, :], p[:, 1, :, 0:1, :].to_broadcast([P, H, 2, HD]))
                    nc.vector.tensor_copy(p[:, 0, :, 4, :], p[:, 0, :, 3, :])
                    nc.vector.tensor_copy(p[:, 1, :, 4, :], p[:, 1, :, 1, :]).then_inc(parts_ready, 1)

                def project_out(j):
                    dve.wait_ge(proj_ps, prep.count(QT, j + 1))
                    if prep.after_first(QT, j - 1):
                        dve.wait_ge(rest_ready, prep.count(QT, j - 1))
                    nc.vector.tensor_tensor(qkf[j], (bank_a, bank_b)[j][:, :], bqk[:, :, :].rearrange("p t d -> p (t d)"),
                                            ALU.add).then_inc(qkf_ready, 1)

                def stack_out(n):
                    j, h0 = n // 2, 8 * (n % 2)
                    dve.wait_ge(stack_ps, nxt.count(8, 2 * n + 1))
                    if nxt.after_first(H, -H):
                        dve.wait_ge(st_ps, nxt.count(H, -H))
                    nc.vector.tensor_copy(
                        q_st[nxt.turn()][0:KROWS, h0:h0 + 8, j * P:(j + 1) * P],
                        bank_a[:, :].bitcast(BF16)[0:KROWS, :].rearrange("p (h s) -> p h s", h=8)
                    ).then_inc(stack_a_sb, 1)

                def residual(j):
                    k = post.turn()
                    heads = by_head((bank_a, bank_b)[j][:, :], STRIP)
                    dve.wait_ge(heads_ps, post.count(QT, j + 1))
                    nc.vector.reciprocal(den[:, j, :], heads[:, :, HD]).then_inc(res_step, 1)
                    if j == 0:
                        dve.wait_ge(xres_in[k], post.landed())
                        if post.second():
                            dve.wait_ge(x1_out[k], post.to(-2).landed())
                    dve.wait_ge(res_step, post.count(2 * QT, 2 * j + 1))
                    nc.vector.scalar_tensor_tensor(
                        out=by_head(x1[k][:, j, :]), in0=heads[:, :, 0:HD], scalar=tanh_g[:, 0:1],
                        in1=den[:, j, :].unsqueeze(2).to_broadcast([P, H, HD]), op0=ALU.mult, op1=ALU.mult
                    ).then_inc(res_step, 1)
                    dve.wait_ge(res_step, post.count(2 * QT, 2 * j + 2))
                    nc.vector.tensor_tensor(x1[k][:, j, :], x1[k][:, j, :], xres[k][:, j, :], ALU.add
                                            ).then_inc(x1_ready, 1)

                def link(instruction, k):
                    instruction.then_inc(route_step, 1)
                    dve.wait_ge(route_step, post.count(ROUTE_STEPS, k))

                def over_e(a):
                    return a.unsqueeze(2).to_broadcast([P, QT, E])

                def over_j(a):
                    return a.unsqueeze(1).to_broadcast([P, QT, E])

                def route_logits():
                    dve.wait_ge(logit_ps, post.count(1, 1))
                    logits = bank_c[:, 0:QT * E].rearrange("p (j e) -> p j e", e=E)
                    link(nc.vector.tensor_reduce(r1[:, :], logits, AX.X, ALU.max), 1)
                    nc.vector.tensor_tensor(lg[:, :, :], logits, over_e(r1[:, :]), ALU.subtract).then_inc(route_in, 1)

                def choose(chosen, top, k):
                    link(nc.vector.tensor_reduce(top[:, :], pr[:, :, :], AX.X, ALU.max), k)
                    link(nc.vector.tensor_tensor(eq[:, :, :], pr[:, :, :], over_e(top[:, :]), ALU.is_equal), k + 1)
                    link(nc.vector.tensor_tensor(key[:, :, :], eq[:, :, :], over_j(prefer[:, :]), ALU.mult), k + 2)
                    link(nc.vector.tensor_reduce(r1[:, :], key[:, :, :], AX.X, ALU.max), k + 3)
                    link(nc.vector.tensor_tensor(chosen[:, :, :], over_j(prefer[:, :]), over_e(r1[:, :]),
                                                 ALU.is_equal), k + 4)

                def route_choice():
                    dve.wait_ge(route_exp, post.count(2, 1))
                    link(nc.vector.tensor_reduce(r2[:, :], ex[:, :, :], AX.X, ALU.add), 2)
                    link(nc.vector.reciprocal(r1[:, :], r2[:, :]), 3)
                    link(nc.vector.tensor_tensor(pr[:, :, :], ex[:, :, :], over_e(r1[:, :]), ALU.mult), 4)
                    choose(sel[0], best, 5)
                    link(nc.vector.scalar_tensor_tensor(out=pr[:, :, :], in0=sel[0][:, :, :], scalar=-2.0,
                                                        in1=pr[:, :, :], op0=ALU.mult, op1=ALU.add), 10)
                    choose(sel[1], r2, 11)
                    nc.vector.tensor_tensor(routed[:, :, :], sel[0][:, :, :], sel[1][:, :, :], ALU.add
                                            ).then_inc(routed_ready, 1)
                    nc.vector.tensor_tensor(edge[:, :], r2[:, :], best[:, :], ALU.subtract).then_inc(route_in, 1)

                def route_rows():
                    k = post.turn()
                    dve.wait_ge(rank_ps, post.count(1, 1))
                    ranks = bank_c[:, 0:QT * E].rearrange("p (j e) -> p j e", e=E)
                    link(nc.vector.tensor_tensor(pos[:, :, :], ranks, over_j(base[:, :]), ALU.add), 16)
                    nc.vector.tensor_tensor(base[:, :], base[:, :], bank_c[:, QT * E:(QT + 1) * E], ALU.add
                                            ).then_inc(rank_used, 1)
                    nc.vector.tensor_tensor(key[:, :, :], sel[0][:, :, :], pos[:, :, :], ALU.mult)
                    link(nc.vector.tensor_tensor(eq[:, :, :], sel[1][:, :, :], pos[:, :, :], ALU.mult), 17)
                    nc.vector.tensor_reduce(slot_f[:, 0, :], key[:, :, :], AX.X, ALU.add)
                    link(nc.vector.tensor_reduce(slot_f[:, 1, :], eq[:, :, :], AX.X, ALU.add), 18)
                    if post.second():
                        dve.wait_ge(table_out[k], post.to(-2).landed(16 * K_TOP * QT))
                    nc.vector.tensor_copy(slots[k][:, :], slot_f[:, :, :].rearrange("p k j -> p (k j)"))
                    for n in range(K_TOP):
                        nc.vector.tensor_copy(entry[k][:, n * QT:(n + 1) * QT, 0].bitcast(I32), token_f[:, :])
                    dve.wait_ge(route_exp, post.count(2, 2))
                    link(nc.vector.tensor_scalar(r1[:, :], edge_e[:, :], 1.0, None, ALU.add), 19)
                    link(nc.vector.reciprocal(r2[:, :], r1[:, :]), 20)
                    link(nc.vector.tensor_scalar(best[:, :], r2[:, :], tanh_g[:, 1:2], None, ALU.mult), 21)
                    nc.vector.tensor_scalar(token_f[:, :], token_f[:, :], float(S), None, ALU.add)
                    nc.vector.tensor_copy(entry[k][:, 0:QT, 1], best[:, :])
                    nc.vector.tensor_tensor(entry[k][:, QT:2 * QT, 1], best[:, :], edge_e[:, :], ALU.mult
                                            ).then_inc(entry_ready, 1)

                for h in range(H):
                    if nxt.live():
                        if h == 0:
                            replicate(nxt, 1)
                        if h < 4:
                            stack_out(h)
                        if h == 2:
                            dve.wait_ge(v_ps, nxt.count(1, 1))
                            if nxt.after_first(4, -4):
                                dve.wait_ge(pv_ps, nxt.count(4, -4))
                            for j in range(QT):
                                i = nc.vector.tensor_tensor(
                                    v_aug[nxt.turn()][:, j, :, 0:HD], by_head(bank_c[:, j * D:(j + 1) * D]),
                                    by_head(bv_sb[:, :]), ALU.add)
                            i.then_inc(v_sb, 1)
                    if prep.live() and h == 2:
                        dve.wait_ge(x_in[prep.turn()], prep.landed())
                        norm_stats(prep, stats, mv, xin[prep.turn()], norm_step, var_ready)
                    if prep.live() and h == 3:
                        dve.wait_ge(rstd_ready, prep.count(1, 1))
                        if prep.after_first(1, 0):
                            dve.wait_ge(xhat_t_ps, prep.count(1, 0))
                        norm_apply(mv, rstd, xin[prep.turn()], xhat, xhat_ready)
                    if nxt.live() and 4 <= h < 12:
                        for v in (2 * (h - 4), 2 * (h - 4) + 1):
                            dve.wait_ge(s_ps, nxt.count(H, v + 1))
                            if v == 0 and nxt.after_first(1, 0):
                                dve.wait_ge(max_t_ps, nxt.count(1, 0))
                            nc.vector.tensor_reduce(
                                maxes[:, v // 8, 2 * (v % 8):2 * (v % 8) + 2],
                                s_bank[v % 2][:, :].rearrange("p (h s) -> p h s", h=2), AX.X, ALU.max
                            ).then_inc(max_done, 1)
                    if post.live() and h == 5:
                        residual(0)
                        residual(1)
                        dve.wait_ge(x1_ready, post.count(QT, QT))
                        norm_stats(post, stats2, mv2, x1[post.turn()], norm2_step, var2_ready)
                    if post.live() and h == 6:
                        k = post.turn()
                        dve.wait_ge(rstd2_ready, post.count(1, 1))
                        if post.second():
                            dve.wait_ge(xn_out[k], post.to(-2).landed())
                            dve.wait_ge(xn_t_ps, post.count(1, -1))
                        norm_apply(mv2, rstd2, x1[k], xn[k], xn_ready)
                    if prep.live() and h == 8:
                        project_out(0)
                    if prep.live() and h == 10:
                        project_out(1)
                    if post.live() and h == 11:
                        route_logits()
                    if nxt.live() and h == 12:
                        dve.wait_ge(max_done, nxt.count(H, H))
                        nc.vector.tensor_copy(max_parts[:, :, 0, :], maxes[:, :, :]).then_inc(max_step, 1)
                        dve.wait_ge(max_step, nxt.count(1, 1))
                        nc.vector.tensor_tensor(max_parts[:, :, 1, :], maxes[:, :, :], max_parts[:, :, 0, :],
                                                ALU.subtract).then_inc(max_ready, 1)
                    if post.live() and h == 12:
                        route_choice()
                    if prep.live() and h == 13:
                        replicate(prep, 0)
                    if post.live() and h == 14:
                        route_rows()

            steps(dve, one)

            done = [0]

            def plan(instruction):
                done[0] += 1
                instruction.then_inc(plan_step, 1)
                dve.wait_ge(plan_step, done[0])

            dve.wait_ge(rank_used, B)
            plan(nc.vector.tensor_scalar(cum_a[:, :], prefer[:, :], float(TOKENS), float(P - 1 - TOKENS * E),
                                         ALU.mult, ALU.add))
            plan(nc.vector.tensor_tensor(cum_b[:, :], base[:, :], cum_a[:, :], ALU.add))
            plan(nc.vector.tensor_copy(count_i[:, :], cum_b[:, :]))
            plan(nc.vector.tensor_scalar(count_i[:, :], count_i[:, :], P.bit_length() - 1, None,
                                         ALU.arith_shift_right))
            plan(nc.vector.tensor_copy(n_tiles[:, :], count_i[:, :]))
            plan(nc.vector.tensor_copy(cum_a[:, :], n_tiles[:, :]))
            a, b = cum_a, cum_b
            for shift in (1, 2, 4):
                nc.vector.tensor_copy(b[:, 0:shift], a[:, 0:shift])
                plan(nc.vector.tensor_tensor(b[:, shift:E], a[:, shift:E], a[:, 0:E - shift], ALU.add))
                a, b = b, a
            shape = [P, MAX_TILES, E]
            plan(nc.vector.tensor_tensor(past[:, :, :], tile_no[:, :].unsqueeze(2).to_broadcast(shape),
                                         a[:, :].unsqueeze(1).to_broadcast(shape), ALU.is_ge))
            plan(nc.vector.tensor_reduce(t_exp[:, :], past[:, :, :], AX.X, ALU.add))
            plan(nc.vector.tensor_tensor(past_n[:, :, :], past[:, :, :],
                                         n_tiles[:, :].unsqueeze(1).to_broadcast(shape), ALU.mult))
            plan(nc.vector.tensor_reduce(t_row[:, :], past_n[:, :, :], AX.X, ALU.add))
            plan(nc.vector.tensor_tensor(t_row[:, :], tile_no[:, :], t_row[:, :], ALU.subtract))
            plan(nc.vector.tensor_scalar(t_row[:, :], t_row[:, :], float(P), None, ALU.mult))
            plan(nc.vector.scalar_tensor_tensor(out=t_row[:, :], in0=t_exp[:, :], scalar=float(TOKENS),
                                                in1=t_row[:, :], op0=ALU.mult, op1=ALU.add))
            plan(nc.vector.tensor_scalar(t_exp[:, :], t_exp[:, :], float(E - 1), None, ALU.min))
            plan(nc.vector.tensor_copy(plan_exp[:, :], t_exp[:, :]))
            nc.vector.tensor_copy(plan_row[:, :], t_row[:, :]).then_inc(plan_ready, 1)

            def rows_out(n, number):
                dve.wait_ge(rows_ps, number + 1)
                if not isinstance(number, int) or number >= 2:
                    dve.wait_ge(up_ps, number - 1)
                nc.vector.tensor_copy(rows_t[n % 2].rearrange("p t s -> p (t s)"), bank[0][:, 0:DT * P]
                                      ).then_inc(rows_sb, 1)

            def hidden(n, number):
                dve.wait_ge(silu_done, number + 1)
                dve.wait_ge(up_ps, number + 1)
                if not isinstance(number, int) or number >= 2:
                    dve.wait_ge(hid_ps, number - 1)
                nc.vector.tensor_tensor(hid[n % 2], silu[n % 2], bank[2][:, :], ALU.mult).then_inc(hid_ready, 1)

            def weigh(n, number):
                dve.wait_ge(y_ps, number + 1)
                if not isinstance(number, int) or number >= 2:
                    dve.wait_ge(y_out, 16 * (number - 1))
                nc.vector.tensor_scalar(y_sb[n % 2], bank[4][:, 0:D], row_info[n % NW][:, 1:2], None, ALU.mult
                                        ).then_inc(y_ready, 1)

            def turn(i, first, last):
                for n in range(U):
                    number = U * i + n
                    hidden(n, number)
                    if not (last and n == U - 1):
                        rows_out(n + 1, number + 1)
                    if not (first and n == 0):
                        weigh(n - 1, number - 1)

            rows_out(0, 0)
            turn(0, True, False)
            with dve.Fori(1, MAX_TILES // U - 1) as i:
                turn(i, False, False)
            turn(MAX_TILES // U - 1, False, True)
            weigh(U - 1, MAX_TILES - 1)

        @block.tensor
        def _(pe):
            def one(step):
                nxt, prep, post = step.to(1), step.to(2), step.to(-1)

                def stack_unit(n):
                    j, h0 = n // 2, 8 * (n % 2)
                    if n % 2 == 0:
                        pe.wait_ge(parts_ready, nxt.count(QT, j + 1))
                    for t, (to, used) in enumerate(((bank_a, stack_a_sb), (bank_b, stack_b_sb))):
                        if n:
                            pe.wait_ge(used, nxt.count(4, n))
                        for h in range(8):
                            i = nc.tensor.transpose(to[:, :].bitcast(BF16)[0:KROWS, h * P:(h + 1) * P],
                                                    parts[j][:, t, h0 + h, :, :].rearrange("p r d -> p (r d)"),
                                                    ident_b[:, :])
                        i.then_inc(stack_ps, 1)

                def project(lhs, j, w, to, done):
                    for dt in range(DT):
                        i = nc.tensor.matmul(to, lhs[:, dt, j * P:(j + 1) * P], w[:, dt, :],
                                             start=dt == 0, stop=dt == DT - 1)
                    if done is not None:
                        i.then_inc(done, 1)

                def values(el, g):
                    pe.wait_ge(exp_done, el.count(H, GROUP * (g + 1)))
                    if g % 2 == 0 and el.after_first(QT, g // 2):
                        pe.wait_ge(heads_sb, el.count(QT, g // 2))
                    for kt in range(QT):
                        for s in range(GROUP):
                            h = GROUP * g + s
                            i = nc.tensor.matmul(
                                pv_bank[STRIP * s:STRIP * (s + 1), (g % 2) * S:(g % 2 + 1) * S],
                                v_aug[el.turn()][:, kt, h, :], probs[h % NPROB][:, kt * S:(kt + 1) * S],
                                start=kt == 0, stop=kt == QT - 1, tile_position=(0, STRIP * s))
                    i.then_inc(pv_ps, 1)

                def scores(v):
                    k, j, h0 = nxt.turn(), v // 8, 2 * (v % 8)
                    if nxt.after_first(H, v - 1):
                        pe.wait_ge(max_done, nxt.count(H, v - 1))
                    for h in (h0, h0 + 1):
                        i = nc.tensor.matmul(s_bank[v % 2][:, (h - h0) * S:(h - h0 + 1) * S],
                                             q_st[k][0:KROWS, h, j * P:(j + 1) * P], k_st[k][0:KROWS, h, :],
                                             start=True, stop=True)
                    i.then_inc(s_ps, 1)

                for h in range(H):
                    if nxt.live() and h == 0:
                        if step.to(-2).live():
                            pe.wait_ge(rank_used, step.count(1, -1))
                        if step.live():
                            pe.wait_ge(max_t_sb, step.count(1, 1))
                        pe.wait_ge(w_in, 64)
                        pe.wait_ge(ctx_in[nxt.turn()], nxt.landed())
                        for j in range(QT):
                            project(ctx_sb[nxt.turn()], j, wv_sb, bank_c[:, j * D:(j + 1) * D],
                                    v_ps if j == QT - 1 else None)
                    if nxt.live() and h < 4:
                        stack_unit(h)
                    if step.live():
                        k = step.turn()
                        if h == 0:
                            pe.wait_ge(max_in[k], step.landed(16 * MROWS))
                            pe.wait_ge(stack_a_sb, step.count(4, 4))
                            pe.wait_ge(stack_b_sb, step.count(4, 4))
                        if step.after_first(H, h - 1):
                            pe.wait_ge(exp_done, step.count(H, h - 1))
                        for kt in range(QT):
                            i = nc.tensor.matmul(st_bank[h % 2][:, kt * S:(kt + 1) * S],
                                                 k_st[k][0:KROWS + MROWS, h, kt * P:(kt + 1) * P],
                                                 q_st[k][0:KROWS + MROWS, h, :], start=True, stop=True)
                        i.then_inc(st_ps, 1)
                    if step.live() and h in (5, 9, 13):
                        if h == 5:
                            pe.wait_ge(v_sb, step.count(1, 1))
                        values(step, h // 4 - 1)
                    if post.live() and h == 1:
                        values(post, 3)
                    if nxt.live() and 4 <= h < 12:
                        if h == 4:
                            pe.wait_ge(stack_a_sb, nxt.count(4, 4))
                            pe.wait_ge(stack_b_sb, nxt.count(4, 4))
                        scores(2 * (h - 4))
                        scores(2 * (h - 4) + 1)
                    if post.live() and h == 4:
                        pe.wait_ge(heads_sb, post.count(QT, QT))
                        if nxt.live():
                            pe.wait_ge(stack_a_sb, nxt.count(4, 4))
                            pe.wait_ge(stack_b_sb, nxt.count(4, 4))
                        if post.after_first(QT, 0):
                            pe.wait_ge(x1_ready, post.count(QT, 0))
                        for j in range(QT):
                            for n in range(4):
                                i = nc.tensor.transpose(
                                    (bank_a, bank_b)[j][:, n * P:(n + 1) * P],
                                    heads_t[n // 2][:, (n % 2) * S + j * P:(n % 2) * S + (j + 1) * P], ident[:, :])
                            i.then_inc(heads_ps, 1)
                    if prep.live() and h == 5:
                        pe.wait_ge(xhat_ready, prep.count(QT, QT))
                        if nxt.live():
                            pe.wait_ge(v_sb, nxt.count(1, 1))
                        for dt in range(DT):
                            for j in range(QT):
                                i = nc.tensor.transpose(bank_c[:, dt * S + j * P:dt * S + (j + 1) * P],
                                                        xhat[:, j, dt * P:(dt + 1) * P], ident[:, :])
                        i.then_inc(xhat_t_ps, 1)
                    if prep.live() and h in (7, 9):
                        j = (h - 7) // 2
                        to = (bank_a, bank_b)[j]
                        if h == 7:
                            pe.wait_ge(ctx_in[prep.turn()], prep.landed())
                            pe.wait_ge(xhat_t_sb, prep.count(1, 1))
                        if post.live():
                            pe.wait_ge(x1_ready, post.count(QT, j + 1))
                        project(xhat_t, j, wq_sb, to[:, 0:D], None)
                        project(ctx_sb[prep.turn()], j, wk_sb, to[:, D:2 * D], proj_ps)
                    if post.live() and h == 7:
                        pe.wait_ge(xn_ready, post.count(QT, QT))
                        if prep.live():
                            pe.wait_ge(xhat_t_sb, prep.count(1, 1))
                        if nxt.live():
                            pe.wait_ge(v_sb, nxt.count(1, 1))
                        if step.live():
                            pe.wait_ge(max_t_sb, step.count(1, 1))
                        if step.to(-2).live():
                            pe.wait_ge(rank_used, step.count(1, -1))
                        for dt in range(DT):
                            for j in range(QT):
                                i = nc.tensor.transpose(bank_c[:, dt * S + j * P:dt * S + (j + 1) * P],
                                                        xn[post.turn()][:, j, dt * P:(dt + 1) * P], ident[:, :])
                        i.then_inc(xn_t_ps, 1)
                    if post.live() and h == 10:
                        pe.wait_ge(xn_t_sb, post.count(1, 1))
                        for j in range(QT):
                            project(xn_t, j, wr_sb, bank_c[:, j * E:(j + 1) * E], logit_ps if j == QT - 1 else None)
                    if nxt.live() and h == 12:
                        pe.wait_ge(max_ready, nxt.count(1, 1))
                        if post.live():
                            pe.wait_ge(route_in, post.count(2, 1))
                        for j in range(QT):
                            i = nc.tensor.transpose(
                                bank_c[:, :].bitcast(BF16)[0:MROWS * H, j * P:(j + 1) * P],
                                max_parts[:, j, :, :].rearrange("p m h -> p (m h)"), ident_b[:, :])
                        i.then_inc(max_t_ps, 1)
                    if post.live() and h == 13:
                        pe.wait_ge(routed_ready, post.count(1, 1))
                        if nxt.live():
                            pe.wait_ge(max_t_sb, nxt.count(1, 1))
                        nc.tensor.matmul(bank_c[:, 0:E], earlier[:, :], routed[:, 0, :], start=True, stop=True)
                        nc.tensor.matmul(bank_c[:, E:2 * E], earlier[:, :], routed[:, 1, :], start=True, stop=False)
                        nc.tensor.matmul(bank_c[:, E:2 * E], ones_b[:, :], routed[:, 0, :], start=False, stop=True)
                        nc.tensor.matmul(bank_c[:, 2 * E:3 * E], ones_b[:, :], routed[:, 0, :], start=True, stop=False)
                        nc.tensor.matmul(bank_c[:, 2 * E:3 * E], ones_b[:, :], routed[:, 1, :], start=False,
                                         stop=True).then_inc(rank_ps, 1)

            pe.wait_ge(const_ready, 1)
            steps(pe, one)

            w_gu_of = w_gu[:, :, :, :, :].rearrange("p t g e f -> p (t g) (e f)")
            w_dn_of = w_dn.rearrange("p t e d -> p t (e d)")

            def rows_in_t(n, number, landed):
                pe.wait_ge(rows_got[n % NX], landed)
                for dt in range(DT):
                    i = nc.tensor.transpose(bank[0][:, dt * P:(dt + 1) * P], rows_in[n % NX][:, dt * P:(dt + 1) * P],
                                            ident[:, :])
                i.then_inc(rows_ps, 1)

            def gate_up(n, number, expert):
                pe.wait_ge(rows_sb, number + 1)
                if not isinstance(number, int) or number > 0:
                    pe.wait_ge(hid_ready, number)
                for g, done in enumerate((gate_ps, up_ps)):
                    for dt in range(DT):
                        i = nc.tensor.matmul(bank[1 + g][:, :], rows_t[n % 2][:, dt, :],
                                             w_gu_of[:, dt * 2 + g, bass.ds(expert * F, F)],
                                             start=dt == 0, stop=dt == DT - 1)
                    i.then_inc(done, 1)

            def down(n, number, expert):
                pe.wait_ge(hid_sb, number + 1)
                if not isinstance(number, int) or number > 0:
                    pe.wait_ge(y_ready, number)
                for ft in range(FT):
                    i = nc.tensor.matmul(bank[4][:, 0:D], hid_t[n % 2][:, ft, :],
                                         w_dn_of[:, ft, bass.ds(expert * D, D)], start=ft == 0, stop=ft == FT - 1)
                i.then_inc(y_ps, 1)

            def hidden_t(n, number):
                pe.wait_ge(hid_ready, number + 1)
                if not isinstance(number, int) or number > 0:
                    pe.wait_ge(hid_sb, number)
                for ft in range(FT):
                    i = nc.tensor.transpose(bank[3][:, ft * P:(ft + 1) * P], hid[n % 2][:, ft * P:(ft + 1) * P],
                                            ident[:, :])
                i.then_inc(hid_ps, 1)

            def load_expert(number):
                return pe.value_load(plan_exp[0:1, number], min_val=0, max_val=E - 1)

            def turn(i, first, last):
                for n in range(U):
                    number = U * i + n
                    at_n = slice(number, number + 1) if isinstance(number, int) else bass.ds(number, 1)
                    gate_up(n, number, load_expert(at_n))
                    if not (last and n == U - 1):
                        rows_in_t(n + 1, number + 1, 16 * (i + (n + 1) // NX + 1))
                    if not (first and n == 0):
                        before = slice(number - 1, number) if isinstance(number, int) else bass.ds(number - 1, 1)
                        down(n - 1, number - 1, load_expert(before))
                    hidden_t(n, number)

            pe.wait_ge(plan_ready, 1)
            pe.wait_ge(ffn_w_in, 16 * DT * 2)
            pe.wait_ge(down_w_in, 16 * FT)
            rows_in_t(0, 0, 16)
            turn(0, True, False)
            with pe.Fori(1, MAX_TILES // U - 1) as i:
                turn(i, False, False)
            turn(MAX_TILES // U - 1, False, True)
            down(U - 1, MAX_TILES - 1, load_expert(slice(MAX_TILES - 1, MAX_TILES)))


def kernel(x, ctx_1024, g_xattn, g_ffn, L0_xattn_Wq, L0_xattn_bq, L0_xattn_Wk, L0_xattn_bk, L0_xattn_Wv,
           L0_xattn_bv, L0_ffn_router_kernel_DE, L0_ffn_kernel_gating_EDF, L0_ffn_kernel_up_EDF,
           L0_ffn_kernel_down_EFD):
    import concourse.bacc as bacc
    from concourse.bass_utils import run_bass_kernel_spmd

    def laid(a):
        return np.ascontiguousarray(np.asarray(a))

    arrays = {
        "x": laid(x),
        "ctx_t": laid(np.asarray(ctx_1024).reshape(TOKENS, D).T),
        "g_xattn": laid(g_xattn),
        "g_ffn": laid(g_ffn),
        "wq_t": laid(np.asarray(L0_xattn_Wq).T),
        "bq": laid(L0_xattn_bq),
        "wk_t": laid(np.asarray(L0_xattn_Wk).T),
        "bk": laid(L0_xattn_bk),
        "wv_t": laid(np.asarray(L0_xattn_Wv).T),
        "bv": laid(L0_xattn_bv),
        "w_router": laid(L0_ffn_router_kernel_DE),
        "w_gate": laid(L0_ffn_kernel_gating_EDF),
        "w_up": laid(L0_ffn_kernel_up_EDF),
        "w_down": laid(L0_ffn_kernel_down_EFD),
    }
    nc = bacc.Bacc("TRN2", target_bir_lowering=False, num_devices=1)
    args = [nc.dram_tensor(f"in_{n}", a.shape, mybir.dt.from_np(a.dtype), kind="ExternalInput").ap()
            for n, a in arrays.items()]
    out = nc.dram_tensor("out_rows", (TOKENS + SPARE, D), F32, kind="ExternalOutput").ap()
    program(nc, *args, out)
    r = run_bass_kernel_spmd(nc, [{f"in_{n}": a for n, a in arrays.items()}], core_ids=[0])
    return r.results[0]["out_rows"][:TOKENS].reshape(B, S, D)
```

```python
from contextlib import ExitStack

import numpy as np

import concourse.bass as bass
from concourse import mybir

F32 = mybir.dt.float32
BF16 = mybir.dt.bfloat16
I32 = mybir.dt.int32
U32 = mybir.dt.uint32
ACT = mybir.ActivationFunctionType
ALU = mybir.AluOpType
AX = mybir.AxisListType

P = 128
B, S, D = 16, 256, 256
H, HD = 16, 16
E, F = 8, 512
TOKENS = B * S
DT = D // P
FT = F // P
QT = S // P
PARTS = 6
KROWS = PARTS * HD
MROWS = 2
STRIP = 32
VW = HD + 1
GROUP = 4
EPS = 1e-5
K_TOP = 2
TABLE = E * TOKENS
MAX_TILES = TOKENS * K_TOP // P + E
SPARE = P
TABLE_ROWS = TABLE + E * P
HALF = H // 2
ROUTE_STEPS = 21


class Step:

    def __init__(self, i, c):
        self.i, self.c = i, c

    def to(self, k):
        return Step(self.i, self.c + k)

    def live(self):
        return not isinstance(self.i, int) or 0 <= self.c < B

    def count(self, each, more=0):
        assert each * self.c + more > 0
        return 2 * each * self.i + (each * self.c + more)

    def after_first(self, each, more=0):
        return not isinstance(self.i, int) or each * self.c + more > 0

    def turn(self):
        return self.c % 2

    def landed(self, each=16):
        assert self.c >= 0
        return each * self.i + each * (self.c // 2 + 1)

    def second(self):
        return not isinstance(self.i, int) or self.c >= 2

    def rows(self):
        return bass.ds((2 * self.i + self.c) * S, S)


def program(nc, x, ctx_t, g_xattn, g_ffn, wq_t, bq, wk_t, bk, wv_t, bv, w_router, w_gate, w_up, w_down, out):
    stack = ExitStack()
    with stack:

        def sb(name, shape, dt=F32):
            return stack.enter_context(nc.sbuf_tensor(name, shape, dt))

        def sem(name):
            return stack.enter_context(nc.semaphore(name))

        def sems(name, n):
            return [sem(f"{name}{k}") for k in range(n)]

        normed = nc.dram_tensor("normed_rows", [TOKENS + SPARE, D], F32, kind="Internal").ap()
        table = nc.dram_tensor("expert_rows", [TABLE_ROWS, 2], F32, kind="Internal").ap()

        ident = sb("ident", [P, P])
        ident_b = sb("ident_b", [P, P], BF16)
        earlier = sb("earlier", [P, P], BF16)
        ones_b = sb("ones_b", [P, P], BF16)
        wq_sb = sb("wq_sb", [P, DT, D])
        wk_sb = sb("wk_sb", [P, DT, D])
        wv_sb = sb("wv_sb", [P, DT, D])
        wr_sb = sb("wr_sb", [P, DT, E])
        bqk = sb("bqk", [P, 2, D])
        bv_sb = sb("bv_sb", [P, D])
        gates = sb("gates", [P, 2])
        tanh_g = sb("tanh_g", [P, 2])
        prefer = sb("prefer", [P, E])
        token_f = sb("token_f", [P, QT])
        base = sb("base", [P, E])
        zeros = sb("zeros", [P, D])
        fill_id = sb("fill_id", [P, TABLE_ROWS // P], I32)
        fill = sb("fill", [P, TABLE_ROWS // P, 2])
        w_gu = sb("w_gu", [P, DT, 2, E, F])

        work = sb("work", [P, 27136])
        at = [0]

        def take(n_f32):
            a = work[:, at[0]:at[0] + n_f32]
            at[0] += n_f32
            return a

        xin = [take(QT * D).rearrange("p (j d) -> p j d", j=QT) for _ in range(2)]
        ctx_sb = [take(DT * S).rearrange("p (t s) -> p t s", t=DT) for _ in range(2)]
        xhat = take(QT * D).rearrange("p (j d) -> p j d", j=QT)
        xhat_t = take(DT * S).rearrange("p (t s) -> p t s", t=DT)
        qkf = [take(2 * D) for _ in range(QT)]
        rest = [take(2 * D) for _ in range(QT)]
        parts = [take(PARTS * D).bitcast(BF16).rearrange("p (t h r d) -> p t h r d", t=2, h=H, r=PARTS)
                 for _ in range(QT)]
        assert at[0] == FT * E * D
        q_st = [take(H * S // 2).bitcast(BF16).rearrange("p (h s) -> p h s", h=H) for _ in range(2)]
        k_st = [take(H * S // 2).bitcast(BF16).rearrange("p (h s) -> p h s", h=H) for _ in range(2)]
        v_aug = [take(QT * H * STRIP).rearrange("p (j h d) -> p j h d", j=QT, h=H) for _ in range(2)]
        NPROB = 8
        probs = [take(QT * S) for _ in range(NPROB)]
        heads_t = [take(2 * S) for _ in range(2)]
        xres = [take(QT * D).rearrange("p (j d) -> p j d", j=QT) for _ in range(2)]
        x1 = [take(QT * D).rearrange("p (j d) -> p j d", j=QT) for _ in range(2)]
        xn = [take(QT * D).rearrange("p (j d) -> p j d", j=QT) for _ in range(2)]
        xn_t = take(DT * S).rearrange("p (t s) -> p t s", t=DT)
        assert at[0] <= 27136, at[0]
        at[0] = 0
        w_dn = take(FT * E * D).rearrange("p (t e d) -> p t e d", t=FT, e=E)
        NX = 4
        rows_in = [take(D) for _ in range(NX)]
        rows_t = [take(DT * P).rearrange("p (t s) -> p t s", t=DT) for _ in range(2)]
        silu = [take(F) for _ in range(2)]
        hid = [take(F) for _ in range(2)]
        hid_t = [take(FT * P).rearrange("p (t s) -> p t s", t=FT) for _ in range(2)]
        y_sb = [take(D) for _ in range(2)]

        maxes = sb("maxes", [P, 2, QT, HALF])
        max_parts = [sb(f"max_parts{k}", [P, QT, MROWS, HALF], BF16) for k in range(2)]
        max_t = [sb(f"max_t{k}", [MROWS * HALF, S], BF16) for k in range(2)]
        stats = sb("stats", [P, QT, 6])
        mv = sb("mv", [P, QT, 2])
        rstd = sb("rstd", [P, QT])
        stats2 = sb("stats2", [P, QT, 6])
        mv2 = sb("mv2", [P, QT, 2])
        rstd2 = sb("rstd2", [P, QT])
        den = sb("den", [P, QT, H])
        minus_half = sb("minus_half", [P, QT])
        lg = sb("lg", [P, QT, E])
        ex = sb("ex", [P, QT, E])
        pr = sb("pr", [P, QT, E])
        eq = sb("eq", [P, QT, E])
        key = sb("key", [P, QT, E])
        sel = [sb(f"sel{k}", [P, QT, E]) for k in range(K_TOP)]
        routed = sb("routed", [P, QT, E], BF16)
        top_lg = sb("top_lg", [P, QT])
        r1 = sb("r1", [P, QT])
        r2 = sb("r2", [P, QT])
        best = sb("best", [P, QT])
        edge = sb("edge", [P, QT])
        edge_e = sb("edge_e", [P, QT])
        pos = sb("pos", [P, QT, E])
        slot_f = sb("slot_f", [P, K_TOP, QT])
        slots = [sb(f"slots{k}", [P, K_TOP * QT], U32) for k in range(2)]
        entry = [sb(f"entry{k}", [P, K_TOP * QT, 2]) for k in range(2)]
        count_i = sb("count_i", [P, E], I32)
        n_tiles = sb("n_tiles", [P, E])
        cum_a = sb("cum_a", [P, E])
        cum_b = sb("cum_b", [P, E])
        tile_no = sb("tile_no", [P, MAX_TILES])
        past = sb("past", [P, MAX_TILES, E])
        past_n = sb("past_n", [P, MAX_TILES, E])
        t_exp = sb("t_exp", [P, MAX_TILES])
        t_row = sb("t_row", [P, MAX_TILES])
        plan_exp = sb("plan_exp", [P, MAX_TILES], I32)
        plan_row = sb("plan_row", [P, MAX_TILES], I32)
        NW = 8
        AHEAD = 3
        U = 8
        assert MAX_TILES % U == 0
        row_info = [sb(f"row_info{k}", [P, 2]) for k in range(NW)]

        bank = [stack.enter_context(nc.psum_tensor(f"bank{k}", [P, 512], F32)) for k in range(8)]
        st_bank = [bank[0], bank[1]]
        s_bank = [bank[2], bank[3]]
        pv_bank = bank[4]
        bank_a, bank_b, bank_c = bank[5], bank[6], bank[7]
        gu_bank = [(bank[1], bank[2]), (bank[5], bank[6])]

        iota_done, const_ready, gate_in = sem("iota_done"), sem("const_ready"), sem("gate_in")
        gate_ready = sem("gate_ready")
        qk_w_in, v_w_in, r_w_in, bias_in = sem("qk_w_in"), sem("v_w_in"), sem("r_w_in"), sem("bias_in")
        fill_ready, fill_out = sem("fill_ready"), sem("fill_out")
        ffn_w_in, down_w_in = sem("ffn_w_in"), sem("down_w_in")
        x_in, xres_in, ctx_in = sems("x_in", 2), sems("xres_in", 2), sems("ctx_in", 2)
        max_in, x1_out, xn_out, table_out = (sems("max_in", 2), sems("x1_out", 2), sems("xn_out", 2),
                                             sems("table_out", 2))
        xhat_t_ps, proj_ps, v_ps, stack_a_ps = sem("xhat_t_ps"), sem("proj_ps"), sem("v_ps"), sem("stack_a_ps")
        stack_b_ps = sem("stack_b_ps")
        s_ps, max_t_ps, st_ps, pv_ps = sem("s_ps"), sem("max_t_ps"), sem("st_ps"), sem("pv_ps")
        heads_ps, xn_t_ps, logit_ps, rank_ps = (sem("heads_ps"), sem("xn_t_ps"), sem("logit_ps"),
                                                sem("rank_ps"))
        xhat_t_sb, part1, part2, stack_b_sb = sem("xhat_t_sb"), sem("part1"), sem("part2"), sem("stack_b_sb")
        max_t_sb, exp_done, heads_sb, xn_t_sb = (sem("max_t_sb"), sem("exp_done"), sem("heads_sb"),
                                                 sem("xn_t_sb"))
        route_exp = sem("route_exp")
        var_ready, var2_ready = sem("var_ready"), sem("var2_ready")
        xhat_ready, qkf_ready, parts_ready, v_sb = (sem("xhat_ready"), sem("qkf_ready"), sem("parts_ready"),
                                                    sem("v_sb"))
        stack_a_sb, max_done, max_ready, x1_ready = (sem("stack_a_sb"), sem("max_done"), sem("max_ready"),
                                                     sem("x1_ready"))
        xn_ready, route_in, routed_ready, rank_used = (sem("xn_ready"), sem("route_in"), sem("routed_ready"),
                                                       sem("rank_used"))
        entry_ready, plan_ready = sem("entry_ready"), sem("plan_ready")
        fill_step, norm_step, norm2_step, res_step = (sem("fill_step"), sem("norm_step"), sem("norm2_step"),
                                                      sem("res_step"))
        max_step, logit_step = sem("max_step"), sem("logit_step")
        route_step, plan_step = sem("route_step"), sem("plan_step")
        dve_went_on, pool_went_on, sp_went_on = sem("dve_went_on"), sem("pool_went_on"), sem("sp_went_on")
        rest_ready, part3 = sem("rest_ready"), sem("part3")
        rstd_ready, rstd2_ready = sem("rstd_ready"), sem("rstd2_ready")
        info_in, rows_got, y_out = sems("info_in", NW), sems("rows_got", NX), sem("y_out")
        rows_ps, rows_sb, gate_ps, up_ps = sem("rows_ps"), sem("rows_sb"), sem("gate_ps"), sem("up_ps")
        silu_done, hid_ready, hid_ps, hid_sb = sem("silu_done"), sem("hid_ready"), sem("hid_ps"), sem("hid_sb")
        y_ps, y_ready = sem("y_ps"), sem("y_ready")

        x_rows = x.rearrange("b s d -> (b s) d")

        def token_tiles(dram, step):
            return dram[step.rows(), :].rearrange("(j p) d -> p j d", p=P)

        S_UNITS = [(), (), (0,), (1,), (2, 3), (4,), (5,), (6,), (7,), (8,), (9,), (10,), (11,), (12,), (13, 14), (15,)]

        FIRST, LAST = 4, B - 3
        PAIRS = (LAST - FIRST + 1) // 2

        def steps(eng, one):
            for c in range(-2, FIRST):
                one(Step(0, c))
            with eng.Fori(0, PAIRS) as i:
                for c in range(2):
                    one(Step(i, FIRST + c))
            for c in range(LAST + 1, B + 2):
                one(Step(0, c))

        block = stack.enter_context(nc.Block())

        @block.sync
        def _(sp):
            def load(step):
                k = step.turn()
                if step.second():
                    sp.wait_ge(xhat_ready, step.count(QT, -QT))
                    sp.sem_inc(sp_went_on, 1)
                sp.dma_start(xin[k], token_tiles(x_rows, step)).then_inc(x_in[k], 16)
                if step.second():
                    sp.wait_ge(v_ps, step.count(QT, -QT))
                    sp.sem_inc(sp_went_on, 1)
                sp.dma_start(ctx_sb[k], ctx_t[:, step.rows()].rearrange("(t p) s -> p t s", p=P)
                             ).then_inc(ctx_in[k], 16)

            sp.dma_start(xin[0], token_tiles(x_rows, Step(0, 0))).then_inc(x_in[0], 16)
            sp.dma_start(wq_sb[:, :, :], wq_t.rearrange("(t p) n -> p t n", p=P)).then_inc(qk_w_in, 16)
            sp.dma_start(ctx_sb[0], ctx_t[:, 0:S].rearrange("(t p) s -> p t s", p=P)).then_inc(ctx_in[0], 16)
            sp.dma_start(wk_sb[:, :, :], wk_t.rearrange("(t p) n -> p t n", p=P)).then_inc(qk_w_in, 16)
            sp.dma_start(bqk[:, 0, :], bq.partition_broadcast(P)).then_inc(bias_in, 16)
            sp.dma_start(bqk[:, 1, :], bk.partition_broadcast(P)).then_inc(bias_in, 16)
            sp.dma_start(wv_sb[:, :, :], wv_t.rearrange("(t p) n -> p t n", p=P)).then_inc(v_w_in, 16)
            sp.dma_start(bv_sb[:, :], bv.partition_broadcast(P)).then_inc(bias_in, 16)
            sp.dma_start(wr_sb[:, :, :], w_router.rearrange("(t p) e -> p t e", p=P)).then_inc(r_w_in, 16)
            load(Step(0, 1))
            sp.wait_ge(const_ready, 1)
            sp.dma_start(out[TOKENS:TOKENS + SPARE, :], zeros[:, :]).then_inc(fill_out, 16)
            sp.dma_start(normed[TOKENS:TOKENS + SPARE, :], zeros[:, :]).then_inc(fill_out, 16)
            sp.wait_ge(fill_ready, 1)
            sp.dma_start(table.rearrange("(p a) w -> p a w", p=P), fill[:, :, :]).then_inc(fill_out, 16)

            def max_rows(el, half):
                k = el.turn()
                sp.wait_ge(max_t_sb, el.count(2, half + 1))
                sp.sem_inc(sp_went_on, 1)
                if el.after_first(H, -H):
                    sp.wait_ge(st_ps, el.count(H, -H))
                    sp.sem_inc(sp_went_on, 1)
                for m in range(MROWS):
                    sp.dma_start(q_st[k][KROWS + m:KROWS + m + 1, HALF * half:HALF * (half + 1), :],
                                 max_t[half][m * HALF:(m + 1) * HALF, :]).then_inc(max_in[k], 16)

            def one(step):
                prep, nxt, post = step.to(2), step.to(1), step.to(-1)
                if prep.live() and step.c >= 0:
                    load(prep)
                if step.live():
                    k = step.turn()
                    if step.second():
                        sp.wait_ge(x1_ready, step.count(QT, -QT))
                        sp.sem_inc(sp_went_on, 1)
                    sp.dma_start(xres[k], token_tiles(x_rows, step)).then_inc(xres_in[k], 16)
                if step.live():
                    max_rows(step, 1)
                if post.live():
                    k = post.turn()
                    sp.wait_ge(x1_ready, post.count(QT, QT))
                    sp.sem_inc(sp_went_on, 1)
                    sp.dma_start(token_tiles(out, post), x1[k]).then_inc(x1_out[k], 16)
                    sp.wait_ge(xn_ready, post.count(QT, QT))
                    sp.sem_inc(sp_went_on, 1)
                    sp.dma_start(token_tiles(normed, post), xn[k]).then_inc(xn_out[k], 16)
                if nxt.live():
                    max_rows(nxt, 0)
                if isinstance(step.i, int) and -1 <= step.c < 2:
                    for n in ((0,), (1,), (2, 3))[step.c + 1]:
                        dt, g = n // 2, n % 2
                        sp.dma_start(w_gu[:, dt, g, :, :],
                                     (w_gate, w_up)[g][:, dt * P:(dt + 1) * P, :].rearrange("e p f -> p e f")
                                     ).then_inc(ffn_w_in, 16)
                if isinstance(step.i, int) and step.c == B - 2:
                    sp.wait_ge(stack_a_ps, 4 * B)
                    sp.wait_ge(stack_b_ps, 4 * B)
                    sp.wait_ge(v_ps, QT * B)
                    for t in range(FT):
                        sp.dma_start(w_dn[:, t, :, :], w_down[:, t * P:(t + 1) * P, :].rearrange("e p d -> p e d")
                                     ).then_inc(down_w_in, 16)

            steps(sp, one)
            sp.wait_ge(plan_ready, 1)
            sp.wait_ge(table_out[0], 16 * K_TOP * QT * B // 2)
            sp.wait_ge(table_out[1], 16 * K_TOP * QT * B // 2)
            sp.wait_ge(fill_out, 48)

            def info(k, number, used):
                if used is not None:
                    sp.wait_ge(y_ready, used)
                    sp.sem_inc(sp_went_on, 1)
                    sp.wait_ge(y_out, 16 * used)
                    sp.sem_inc(sp_went_on, 1)
                row = sp.value_load(plan_row[0:1, number], min_val=0, max_val=TABLE_ROWS - P)
                sp.dma_start(row_info[k][:, :], table[bass.ds(row, P), :]).then_inc(info_in[k], 16)

            for k in range(NW):
                info(k, slice(k, k + 1), None)
            with sp.Fori(1, MAX_TILES // NW) as i:
                for k in range(NW):
                    info(k, bass.ds(NW * i + k, 1), NW * i + (k + 1 - NW))
            sp.wait_ge(y_out, 16 * MAX_TILES)

        @block.gpsimd
        def _(pool):
            nc.gpsimd.memset(ident[:, :], 0.0)
            nc.gpsimd.memset(ident_b[:, :], 0.0)
            nc.gpsimd.memset(earlier[:, :], 1.0)
            nc.gpsimd.memset(ones_b[:, :], 1.0).then_inc(iota_done, 1)
            pool.wait_ge(iota_done, 1)
            nc.gpsimd.affine_select(out=ident[:, :], in_=ident[:, :], compare_op=ALU.not_equal, fill=1.0,
                                    base=0, pattern=[[-1, P]], channel_multiplier=1)
            nc.gpsimd.affine_select(out=ident_b[:, :], in_=ident_b[:, :], compare_op=ALU.not_equal, fill=1.0,
                                    base=0, pattern=[[-1, P]], channel_multiplier=1)
            nc.gpsimd.affine_select(out=earlier[:, :], in_=earlier[:, :], compare_op=ALU.is_gt, fill=0.0,
                                    base=0, pattern=[[1, P]], channel_multiplier=-1)
            nc.gpsimd.memset(zeros[:, :], 0.0)
            nc.gpsimd.memset(minus_half[:, :], -0.5)
            for k in range(2):
                nc.gpsimd.memset(v_aug[k][:, :, :, HD:STRIP], 0.0)
            nc.gpsimd.iota(fill_id[:, :], pattern=[[1, TABLE_ROWS // P]], base=0,
                           channel_multiplier=TABLE_ROWS // P)
            nc.gpsimd.iota(token_f[:, :], pattern=[[P, QT]], base=0, channel_multiplier=1,
                           allow_small_or_imprecise_dtypes=True)
            nc.gpsimd.iota(prefer[:, :], pattern=[[-1, E]], base=E, channel_multiplier=0,
                           allow_small_or_imprecise_dtypes=True)
            nc.gpsimd.iota(base[:, :], pattern=[[TOKENS, E]], base=0, channel_multiplier=0,
                           allow_small_or_imprecise_dtypes=True)
            nc.gpsimd.iota(tile_no[:, :], pattern=[[1, MAX_TILES]], base=0, channel_multiplier=0,
                           allow_small_or_imprecise_dtypes=True)
            nc.gpsimd.memset(fill[:, :, 1:2], 0.0).then_inc(iota_done, 1)
            pool.wait_ge(iota_done, 2)
            for k in range(2):
                nc.gpsimd.memset(v_aug[k][:, :, :, HD:VW], 1.0)
            nc.gpsimd.nop().then_inc(const_ready, 1)

            def one(step):
                prep, post, route = step.to(2), step.to(-1), step.to(-2)

                def residue(j):
                    pool.wait_ge(part1, prep.count(QT, j + 1))
                    if prep.after_first(QT, j - 1):
                        pool.wait_ge(part3, prep.count(QT, j - 1))
                    nc.gpsimd.tensor_tensor(
                        rest[j].rearrange("p (t h d) -> p t h d", t=2, h=H),
                        qkf[j].rearrange("p (t h d) -> p t h d", t=2, h=H),
                        parts[j][:, :, :, 0, :], ALU.subtract).then_inc(rest_ready, 1)

                def third(j):
                    pool.wait_ge(part2, prep.count(QT, j + 1))
                    pool.wait_ge(rest_ready, prep.count(QT, j + 1))
                    r = rest[j].rearrange("p (t h d) -> p t h d", t=2, h=H)
                    nc.gpsimd.tensor_tensor(parts[j][:, 0, :, 5, :], r[:, 0, :, :], parts[j][:, 0, :, 3, :],
                                            ALU.subtract)
                    nc.gpsimd.tensor_tensor(parts[j][:, 1, :, 2, :], r[:, 1, :, :], parts[j][:, 1, :, 1, :],
                                            ALU.subtract).then_inc(part3, 1)

                if prep.live():
                    pool.wait_ge(var_ready, prep.count(1, 1))
                    if prep.after_first(QT, 0):
                        pool.wait_ge(xhat_ready, prep.count(QT, 0))
                    nc.gpsimd.tensor_tensor(rstd[:, :], mv[:, :, 1], minus_half[:, :], ALU.pow).then_inc(rstd_ready, 1)
                if post.live():
                    pool.wait_ge(var2_ready, post.count(1, 1))
                    if post.after_first(QT, 0):
                        pool.wait_ge(xn_ready, post.count(QT, 0))
                    nc.gpsimd.tensor_tensor(rstd2[:, :], mv2[:, :, 1], minus_half[:, :], ALU.pow
                                            ).then_inc(rstd2_ready, 1)
                if prep.live():
                    residue(0)
                    third(0)
                    residue(1)
                    third(1)
                if isinstance(step.i, int) and step.c == 1:
                    pool.wait_ge(fill_out, 48)
                if route.live():
                    k = route.turn()
                    pool.wait_ge(entry_ready, route.count(1, 1))
                    pool.sem_inc(pool_went_on, 1)
                    for n in range(K_TOP * QT):
                        nc.gpsimd.indirect_dma_start(
                            out=table[:, :], out_offset=bass.IndirectOffsetOnAxis(ap=slots[k][:, n:n + 1], axis=0),
                            in_=entry[k][:, n, :], in_offset=None).then_inc(table_out[k], 16)

            steps(pool, one)

            def gather(k, w, landed, used):
                pool.wait_ge(info_in[w], landed)
                if used is not None:
                    pool.wait_ge(rows_ps, used)
                pool.sem_inc(pool_went_on, 1)
                nc.gpsimd.indirect_dma_start(
                    out=rows_in[k], out_offset=None, in_=normed[:, :],
                    in_offset=bass.IndirectOffsetOnAxis(ap=row_info[w][:, 0:1].bitcast(U32), axis=0)
                ).then_inc(rows_got[k], 16)

            def scatter(k, w, number):
                pool.wait_ge(y_ready, number + 1)
                if not isinstance(number, int) or number > 0:
                    pool.wait_ge(y_out, 16 * number)
                pool.sem_inc(pool_went_on, 1)
                nc.gpsimd.indirect_dma_start(
                    out=out[:, :], out_offset=bass.IndirectOffsetOnAxis(ap=row_info[w][:, 0:1].bitcast(U32), axis=0),
                    in_=y_sb[k], in_offset=None, compute_op=ALU.add).then_inc(y_out, 16)

            for k in range(2):
                pool.wait_ge(x1_out[k], 16 * B // 2)
                pool.wait_ge(xn_out[k], 16 * B // 2)
            pool.wait_ge(fill_out, 48)
            pool.wait_ge(pv_ps, B * H // GROUP)
            pool.wait_ge(logit_ps, B)
            for n in range(AHEAD):
                gather(n % NX, n % NW, 16, None)

            def turn(i, first, last):
                for n in range(U):
                    if not (last and n >= U - AHEAD):
                        m = n + AHEAD
                        gather(m % NX, m % NW, 16 * (U // NW) * i + 16 * (m // NW + 1),
                               None if first and m < NX else U * i + (m - NX + 1))
                    scatter(n % 2, n % NW, U * i + n)

            turn(0, True, False)
            with pool.Fori(1, MAX_TILES // U - 1) as i:
                turn(i, False, False)
            turn(MAX_TILES // U - 1, False, True)

        @block.scalar
        def _(act):
            act.dma_start(gates[:, 0:1], g_xattn.partition_broadcast(P)).then_inc(gate_in, 16)
            act.dma_start(gates[:, 1:2], g_ffn.partition_broadcast(P)).then_inc(gate_in, 16)
            act.wait_ge(gate_in, 32)
            nc.scalar.activation(tanh_g[:, :], gates[:, :], ACT.Tanh).then_inc(gate_ready, 1)

            def one(step):
                nxt, prep, post, route = step.to(1), step.to(2), step.to(-1), step.to(-2)

                def first_part(j):
                    act.wait_ge(qkf_ready, prep.count(QT, j + 1))
                    if prep.after_first(4, 0):
                        act.wait_ge(stack_a_ps, prep.count(4, 0))
                        act.wait_ge(stack_b_ps, prep.count(4, 0))
                    nc.scalar.copy(parts[j][:, :, :, 0, :],
                                   qkf[j].rearrange("p (t h d) -> p t h d", t=2, h=H)).then_inc(part1, 1)

                def second_part(j):
                    act.wait_ge(rest_ready, prep.count(QT, j + 1))
                    r = rest[j].rearrange("p (t h d) -> p t h d", t=2, h=H)
                    nc.scalar.copy(parts[j][:, 0, :, 3, :], r[:, 0, :, :])
                    nc.scalar.copy(parts[j][:, 1, :, 1, :], r[:, 1, :, :]).then_inc(part2, 1)

                def stack_out(n):
                    j, h0 = n % 2, HALF * (n // 2)
                    act.wait_ge(stack_b_ps, nxt.count(4, n + 1))
                    if nxt.after_first(H, -H):
                        act.wait_ge(st_ps, nxt.count(H, -H))
                    nc.scalar.copy(
                        k_st[nxt.turn()][0:KROWS, h0:h0 + 8, j * P:(j + 1) * P],
                        bank_b[:, :].bitcast(BF16)[0:KROWS, :].rearrange("p (h s) -> p h s", h=8)
                    ).then_inc(stack_b_sb, 1)

                def heads_out(el, half):
                    act.wait_ge(pv_ps, el.count(4, 2 * half + 2))
                    if el.after_first(QT, 0):
                        act.wait_ge(heads_ps, el.count(QT, 0))
                    nc.scalar.copy(heads_t[half], pv_bank[:, :]).then_inc(heads_sb, 1)

                def max_out(el, half):
                    act.wait_ge(max_t_ps, el.count(2, half + 1))
                    if el.after_first(1, 0):
                        act.wait_ge(max_in[el.to(-1).turn()], el.to(-1).landed(32 * MROWS) - 16 * MROWS * (1 - half))
                    nc.scalar.copy(max_t[half][:, :], bank_c[:, :].bitcast(BF16)[0:MROWS * HALF, 0:S]
                                   ).then_inc(max_t_sb, 1)

                for h in range(H):
                    if nxt.live() and h < 4:
                        stack_out(h)
                    if step.live():
                        act.wait_ge(st_ps, step.count(H, h + 1))
                        if step.after_first(4, (h - NPROB) // GROUP + 1):
                            act.wait_ge(pv_ps, step.count(4, (h - NPROB) // GROUP + 1))
                        nc.scalar.activation(probs[h % NPROB], st_bank[h % 2][:, :], ACT.Exp,
                                             scale=float(HD) ** -0.5).then_inc(exp_done, 1)
                    if post.live() and h == 2:
                        heads_out(post, 1)
                    if step.live() and h == 4:
                        max_out(step, 1)
                    if prep.live() and h == 5:
                        act.wait_ge(xhat_t_ps, prep.count(1, 1))
                        if prep.after_first(QT, 0):
                            act.wait_ge(proj_ps, prep.count(QT, 0))
                        nc.scalar.copy(xhat_t.rearrange("p t s -> p (t s)"), bank_c[:, :]).then_inc(xhat_t_sb, 1)
                    if prep.live() and h == 8:
                        first_part(0)
                    if route.live() and h == 8:
                        act.wait_ge(route_in, route.count(2, 2))
                        nc.scalar.activation(edge_e[:, :], edge[:, :], ACT.Exp).then_inc(route_exp, 1)
                    if post.live() and h == 9:
                        act.wait_ge(xn_t_ps, post.count(1, 1))
                        if post.after_first(1, 0):
                            act.wait_ge(logit_ps, post.count(1, 0))
                        nc.scalar.copy(xn_t.rearrange("p t s -> p (t s)"), bank_c[:, :]).then_inc(xn_t_sb, 1)
                    if prep.live() and h == 10:
                        second_part(0)
                        first_part(1)
                    if step.live() and h == 11:
                        heads_out(step, 0)
                    if nxt.live() and h == 11:
                        max_out(nxt, 0)
                    if prep.live() and h == 12:
                        second_part(1)
                    if post.live() and h == 13:
                        act.wait_ge(route_in, post.count(2, 1))
                        nc.scalar.activation(ex[:, :, :], lg[:, :, :], ACT.Exp).then_inc(route_exp, 1)

            steps(act, one)

            def tile(k, number):
                act.wait_ge(gate_ps, number + 1)
                nc.scalar.activation(silu[k], gu_bank[k][0][:, :], ACT.Silu).then_inc(silu_done, 1)
                act.wait_ge(hid_ps, number + 1)
                if not isinstance(number, int) or number >= 2:
                    act.wait_ge(y_ps, number - 1)
                nc.scalar.copy(hid_t[k].rearrange("p t s -> p (t s)"), bank[3][:, :]).then_inc(hid_sb, 1)

            for n in range(2):
                tile(n, n)
            with act.Fori(1, MAX_TILES // 2) as i:
                for k in range(2):
                    tile(k, 2 * i + k)

        @block.vector
        def _(dve):
            dve.wait_ge(const_ready, 1)
            nc.vector.tensor_scalar(fill_id[:, :], fill_id[:, :], P - 1, None, ALU.bitwise_and
                                    ).then_inc(fill_step, 1)
            dve.wait_ge(fill_step, 1)
            nc.vector.tensor_scalar(fill[:, :, 0].bitcast(I32), fill_id[:, :], TOKENS, None, ALU.add
                                    ).then_inc(fill_ready, 1)

            def by_head(a, d=HD):
                return a.rearrange("p (h d) -> p h d", d=d)

            def norm_stats(el, stats_of, mv_of, source, steps_sem, done):
                for j in range(QT):
                    nc.vector.bn_stats(stats_of[:, j, :], source[:, j, :]).then_inc(steps_sem, 1)
                for j in range(QT):
                    dve.wait_ge(steps_sem, el.count(4, j + 1))
                    dve.sem_inc(dve_went_on, 1)
                    nc.vector.bn_aggr(mv_of[:, j, :], stats_of[:, j, :]).then_inc(steps_sem, 1)
                dve.wait_ge(steps_sem, el.count(4, 4))
                nc.vector.tensor_scalar(mv_of[:, :, 1], mv_of[:, :, 1], EPS, None, ALU.add).then_inc(done, 1)

            def norm_apply(mv_of, rstd_of, source, target, done):
                for j in range(QT):
                    nc.vector.tensor_scalar(target[:, j, :], source[:, j, :], mv_of[:, j, 0:1],
                                            rstd_of[:, j:j + 1], ALU.subtract, ALU.mult).then_inc(done, 1)

            def one(step):
                nxt, prep, post, route = step.to(1), step.to(2), step.to(-1), step.to(-2)

                def replicate(el, j):
                    dve.wait_ge(part3, el.count(QT, j + 1))
                    p = parts[j]
                    nc.vector.tensor_copy(p[:, 0, :, 1:3, :], p[:, 0, :, 0:1, :].to_broadcast([P, H, 2, HD]))
                    nc.vector.tensor_copy(p[:, 1, :, 3:6:2, :], p[:, 1, :, 0:1, :].to_broadcast([P, H, 2, HD]))
                    nc.vector.tensor_copy(p[:, 0, :, 4, :], p[:, 0, :, 3, :])
                    nc.vector.tensor_copy(p[:, 1, :, 4, :], p[:, 1, :, 1, :]).then_inc(parts_ready, 1)

                def project_out(j):
                    if j == 0:
                        dve.wait_ge(bias_in, 48)
                    dve.wait_ge(proj_ps, prep.count(QT, j + 1))
                    if prep.after_first(QT, j - 1):
                        dve.wait_ge(rest_ready, prep.count(QT, j - 1))
                    nc.vector.tensor_tensor(qkf[j], (bank_a, bank_b)[j][:, :], bqk[:, :, :].rearrange("p t d -> p (t d)"),
                                            ALU.add).then_inc(qkf_ready, 1)

                def stack_out(n):
                    j, h0 = n % 2, HALF * (n // 2)
                    dve.wait_ge(stack_a_ps, nxt.count(4, n + 1))
                    if nxt.after_first(H, -H):
                        dve.wait_ge(st_ps, nxt.count(H, -H))
                    nc.vector.tensor_copy(
                        q_st[nxt.turn()][0:KROWS, h0:h0 + 8, j * P:(j + 1) * P],
                        bank_a[:, :].bitcast(BF16)[0:KROWS, :].rearrange("p (h s) -> p h s", h=8)
                    ).then_inc(stack_a_sb, 1)

                def residual(j):
                    k = post.turn()
                    heads = by_head((bank_a, bank_b)[j][:, :], STRIP)
                    dve.wait_ge(heads_ps, post.count(QT, j + 1))
                    nc.vector.reciprocal(den[:, j, :], heads[:, :, HD]).then_inc(res_step, 1)
                    if j == 0:
                        dve.wait_ge(xres_in[k], post.landed())
                        if post.second():
                            dve.wait_ge(x1_out[k], post.to(-2).landed())
                    dve.wait_ge(res_step, post.count(2 * QT, 2 * j + 1))
                    nc.vector.scalar_tensor_tensor(
                        out=by_head(x1[k][:, j, :]), in0=heads[:, :, 0:HD], scalar=tanh_g[:, 0:1],
                        in1=den[:, j, :].unsqueeze(2).to_broadcast([P, H, HD]), op0=ALU.mult, op1=ALU.mult
                    ).then_inc(res_step, 1)
                    dve.wait_ge(res_step, post.count(2 * QT, 2 * j + 2))
                    nc.vector.tensor_tensor(x1[k][:, j, :], x1[k][:, j, :], xres[k][:, j, :], ALU.add
                                            ).then_inc(x1_ready, 1)

                def step_done(k):
                    dve.wait_ge(route_step, route.count(ROUTE_STEPS, k))

                def over_e(a):
                    return a.unsqueeze(2).to_broadcast([P, QT, E])

                def over_j(a):
                    return a.unsqueeze(1).to_broadcast([P, QT, E])

                def route_logits():
                    dve.wait_ge(logit_ps, post.count(1, 1))
                    logits = bank_a[:, 0:QT * E].rearrange("p (j e) -> p j e", e=E)
                    nc.vector.tensor_reduce(top_lg[:, :], logits, AX.X, ALU.max).then_inc(logit_step, 1)
                    dve.wait_ge(logit_step, post.count(1, 1))
                    nc.vector.tensor_tensor(lg[:, :, :], logits, over_e(top_lg[:, :]), ALU.subtract
                                            ).then_inc(route_in, 1)

                def choose(n, chosen, top, k):
                    step_done(k + n)
                    if n == 0:
                        i = nc.vector.tensor_reduce(top[:, :], pr[:, :, :], AX.X, ALU.max)
                    elif n == 1:
                        i = nc.vector.tensor_tensor(eq[:, :, :], pr[:, :, :], over_e(top[:, :]), ALU.is_equal)
                    elif n == 2:
                        i = nc.vector.tensor_tensor(key[:, :, :], eq[:, :, :], over_j(prefer[:, :]), ALU.mult)
                    elif n == 3:
                        i = nc.vector.tensor_reduce(r1[:, :], key[:, :, :], AX.X, ALU.max)
                    else:
                        i = nc.vector.tensor_tensor(chosen[:, :, :], over_j(prefer[:, :]), over_e(r1[:, :]), ALU.is_equal)
                    i.then_inc(route_step, 1)

                def route_choice(n):
                    if n == 0:
                        dve.wait_ge(route_exp, route.count(2, 1))
                        nc.vector.tensor_reduce(r2[:, :], ex[:, :, :], AX.X, ALU.add).then_inc(route_step, 1)
                    elif n == 1:
                        step_done(1)
                        nc.vector.reciprocal(r1[:, :], r2[:, :]).then_inc(route_step, 1)
                    elif n == 2:
                        step_done(2)
                        nc.vector.tensor_tensor(pr[:, :, :], ex[:, :, :], over_e(r1[:, :]), ALU.mult
                                                ).then_inc(route_step, 1)
                    elif n < 8:
                        choose(n - 3, sel[0], best, 3)
                    elif n == 8:
                        step_done(8)
                        nc.vector.scalar_tensor_tensor(out=pr[:, :, :], in0=sel[0][:, :, :], scalar=-2.0,
                                                       in1=pr[:, :, :], op0=ALU.mult, op1=ALU.add
                                                       ).then_inc(route_step, 1)
                    elif n < 14:
                        choose(n - 9, sel[1], r2, 9)
                    elif n == 14:
                        step_done(14)
                        nc.vector.tensor_tensor(routed[:, :, :], sel[0][:, :, :], sel[1][:, :, :], ALU.add
                                                ).then_inc(routed_ready, 1)
                        nc.vector.tensor_tensor(edge[:, :], r2[:, :], best[:, :], ALU.subtract).then_inc(route_in, 1)

                def route_weights(n):
                    if n == 0:
                        dve.wait_ge(route_exp, route.count(2, 2))
                        nc.vector.tensor_scalar(r1[:, :], edge_e[:, :], 1.0, None, ALU.add).then_inc(route_step, 1)
                    elif n == 1:
                        step_done(15)
                        nc.vector.reciprocal(r2[:, :], r1[:, :]).then_inc(route_step, 1)
                    elif n == 2:
                        step_done(16)
                        nc.vector.tensor_scalar(best[:, :], r2[:, :], tanh_g[:, 1:2], None, ALU.mult
                                                ).then_inc(route_step, 1)

                def route_rows(n):
                    k = route.turn()
                    if n == 0:
                        dve.wait_ge(rank_ps, route.count(1, 1))
                        ranks = bank_b[:, 0:QT * E].rearrange("p (j e) -> p j e", e=E)
                        nc.vector.tensor_tensor(pos[:, :, :], ranks, over_j(base[:, :]), ALU.add
                                                ).then_inc(route_step, 1)
                    elif n == 1:
                        step_done(18)
                        nc.vector.tensor_tensor(base[:, :], base[:, :], bank_b[:, QT * E:(QT + 1) * E], ALU.add
                                                ).then_inc(rank_used, 1)
                        nc.vector.tensor_tensor(key[:, :, :], sel[0][:, :, :], pos[:, :, :], ALU.mult)
                        nc.vector.tensor_tensor(eq[:, :, :], sel[1][:, :, :], pos[:, :, :], ALU.mult
                                                ).then_inc(route_step, 1)
                    elif n == 2:
                        step_done(19)
                        nc.vector.tensor_reduce(slot_f[:, 0, :], key[:, :, :], AX.X, ALU.add)
                        nc.vector.tensor_reduce(slot_f[:, 1, :], eq[:, :, :], AX.X, ALU.add).then_inc(route_step, 1)
                    else:
                        step_done(20)
                        if route.second():
                            dve.wait_ge(table_out[k], route.to(-2).landed(16 * K_TOP * QT))
                        nc.vector.tensor_copy(slots[k][:, :], slot_f[:, :, :].rearrange("p k j -> p (k j)"))
                        for m in range(K_TOP):
                            i = nc.vector.tensor_copy(entry[k][:, m * QT:(m + 1) * QT, 0].bitcast(I32), token_f[:, :])
                        i.then_inc(route_step, 1)
                        nc.vector.tensor_copy(entry[k][:, 0:QT, 1], best[:, :])
                        nc.vector.tensor_tensor(entry[k][:, QT:2 * QT, 1], best[:, :], edge_e[:, :], ALU.mult
                                                ).then_inc(entry_ready, 1)
                        step_done(21)
                        nc.vector.tensor_scalar(token_f[:, :], token_f[:, :], float(S), None, ALU.add)

                def values_out(j):
                    if j == 0:
                        dve.wait_ge(bias_in, 48)
                        if nxt.after_first(4, -4):
                            dve.wait_ge(pv_ps, nxt.count(4, -4))
                    dve.wait_ge(v_ps, nxt.count(QT, QT))
                    nc.vector.tensor_tensor(
                        v_aug[nxt.turn()][:, j, :, 0:HD], by_head(bank_c[:, j * D:(j + 1) * D]),
                        by_head(bv_sb[:, :]), ALU.add).then_inc(v_sb, 1)

                def heads_maxima(v):
                    dve.wait_ge(s_ps, nxt.count(H, v + 1))
                    nc.vector.tensor_reduce(
                        maxes[:, v // 8, (v // 4) % 2, 2 * (v % 4):2 * (v % 4) + 2],
                        s_bank[v % 2][:, :].rearrange("p (h s) -> p h s", h=2), AX.X, ALU.max
                    ).then_inc(max_done, 1)

                def split_maxima(el, half):
                    dve.wait_ge(max_done, el.count(H, 8 * (half + 1)))
                    if el.after_first(2, half - 1):
                        dve.wait_ge(max_t_ps, el.count(2, half - 1))
                    nc.vector.tensor_copy(max_parts[half][:, :, 0, :], maxes[:, half, :, :]).then_inc(max_step, 1)
                    dve.wait_ge(max_step, el.count(2, half + 1))
                    nc.vector.tensor_tensor(max_parts[half][:, :, 1, :], maxes[:, half, :, :],
                                            max_parts[half][:, :, 0, :], ALU.subtract).then_inc(max_ready, 1)

                for h in range(H):
                    if route.live() and h < 8:
                        route_choice(2 * h)
                    if step.live() and h == 0:
                        split_maxima(step, 1)
                    if route.live() and 9 <= h < 12:
                        route_weights(h - 9)
                    if nxt.live():
                        if h < 4:
                            stack_out(h)
                        if h in (2, 3):
                            values_out(h - 2)
                        for v in S_UNITS[h]:
                            heads_maxima(v)
                    if isinstance(step.i, int) and step.c in (-2, -1) and h == 1:
                        nc.vector.memset(k_st[step.c + 2][KROWS:P, :, :], -1.0)
                    if prep.live() and h == 0:
                        dve.wait_ge(x_in[prep.turn()], prep.landed())
                        norm_stats(prep, stats, mv, xin[prep.turn()], norm_step, var_ready)
                    if route.live() and h < 7:
                        route_choice(2 * h + 1)
                    if prep.live() and h == 3:
                        dve.wait_ge(rstd_ready, prep.count(1, 1))
                        if prep.after_first(1, 0):
                            dve.wait_ge(xhat_t_ps, prep.count(1, 0))
                        norm_apply(mv, rstd, xin[prep.turn()], xhat, xhat_ready)
                    if post.live() and h == 5:
                        residual(0)
                    if post.live() and h == 6:
                        residual(1)
                        dve.wait_ge(x1_ready, post.count(QT, QT))
                        norm_stats(post, stats2, mv2, x1[post.turn()], norm2_step, var2_ready)
                    if post.live() and h == 7:
                        k = post.turn()
                        dve.wait_ge(rstd2_ready, post.count(1, 1))
                        if post.second():
                            dve.wait_ge(xn_out[k], post.to(-2).landed())
                            dve.wait_ge(xn_t_ps, post.count(1, -1))
                        norm_apply(mv2, rstd2, x1[k], xn[k], xn_ready)
                    if nxt.live() and h == 8:
                        split_maxima(nxt, 0)
                    if prep.live() and h == 8:
                        project_out(0)
                    if prep.live() and h == 10:
                        project_out(1)
                    if prep.live() and h == 12:
                        replicate(prep, 0)
                    if post.live() and h == 12:
                        route_logits()
                    if route.live() and h == 14:
                        route_rows(0)
                        route_rows(1)
                    if route.live() and h == 15:
                        route_rows(2)
                    if prep.live() and h == 15:
                        replicate(prep, 1)
                    if route.live() and h == 15:
                        route_rows(3)

            steps(dve, one)

            done = [0]

            def plan(instruction):
                done[0] += 1
                instruction.then_inc(plan_step, 1)
                dve.wait_ge(plan_step, done[0])

            dve.wait_ge(rank_used, B)
            plan(nc.vector.tensor_scalar(cum_a[:, :], prefer[:, :], float(TOKENS), float(P - 1 - TOKENS * E),
                                         ALU.mult, ALU.add))
            plan(nc.vector.tensor_tensor(cum_b[:, :], base[:, :], cum_a[:, :], ALU.add))
            plan(nc.vector.tensor_copy(count_i[:, :], cum_b[:, :]))
            plan(nc.vector.tensor_scalar(count_i[:, :], count_i[:, :], P.bit_length() - 1, None,
                                         ALU.arith_shift_right))
            plan(nc.vector.tensor_copy(n_tiles[:, :], count_i[:, :]))
            plan(nc.vector.tensor_copy(cum_a[:, :], n_tiles[:, :]))
            a, b = cum_a, cum_b
            for shift in (1, 2, 4):
                nc.vector.tensor_copy(b[:, 0:shift], a[:, 0:shift])
                plan(nc.vector.tensor_tensor(b[:, shift:E], a[:, shift:E], a[:, 0:E - shift], ALU.add))
                a, b = b, a
            shape = [P, MAX_TILES, E]
            plan(nc.vector.tensor_tensor(past[:, :, :], tile_no[:, :].unsqueeze(2).to_broadcast(shape),
                                         a[:, :].unsqueeze(1).to_broadcast(shape), ALU.is_ge))
            plan(nc.vector.tensor_reduce(t_exp[:, :], past[:, :, :], AX.X, ALU.add))
            plan(nc.vector.tensor_tensor(past_n[:, :, :], past[:, :, :],
                                         n_tiles[:, :].unsqueeze(1).to_broadcast(shape), ALU.mult))
            plan(nc.vector.tensor_reduce(t_row[:, :], past_n[:, :, :], AX.X, ALU.add))
            plan(nc.vector.tensor_tensor(t_row[:, :], tile_no[:, :], t_row[:, :], ALU.subtract))
            plan(nc.vector.tensor_scalar(t_row[:, :], t_row[:, :], float(P), None, ALU.mult))
            plan(nc.vector.scalar_tensor_tensor(out=t_row[:, :], in0=t_exp[:, :], scalar=float(TOKENS),
                                                in1=t_row[:, :], op0=ALU.mult, op1=ALU.add))
            plan(nc.vector.tensor_scalar(t_exp[:, :], t_exp[:, :], float(E - 1), None, ALU.min))
            plan(nc.vector.tensor_copy(plan_exp[:, :], t_exp[:, :]))
            nc.vector.tensor_copy(plan_row[:, :], t_row[:, :]).then_inc(plan_ready, 1)

            def rows_out(n, number):
                dve.wait_ge(rows_ps, number + 1)
                if not isinstance(number, int) or number >= 2:
                    dve.wait_ge(up_ps, number - 1)
                nc.vector.tensor_copy(rows_t[n % 2].rearrange("p t s -> p (t s)"), bank[0][:, 0:DT * P]
                                      ).then_inc(rows_sb, 1)

            def hidden(n, number):
                dve.wait_ge(silu_done, number + 1)
                dve.wait_ge(up_ps, number + 1)
                if not isinstance(number, int) or number >= 2:
                    dve.wait_ge(hid_ps, number - 1)
                nc.vector.tensor_tensor(hid[n % 2], silu[n % 2], gu_bank[n % 2][1][:, :], ALU.mult).then_inc(hid_ready, 1)

            def weigh(n, number):
                dve.wait_ge(y_ps, number + 1)
                if not isinstance(number, int) or number >= 2:
                    dve.wait_ge(y_out, 16 * (number - 1))
                nc.vector.tensor_scalar(y_sb[n % 2], bank[4][:, 0:D], row_info[n % NW][:, 1:2], None, ALU.mult
                                        ).then_inc(y_ready, 1)

            def turn(i, first, last):
                for n in range(U):
                    number = U * i + n
                    hidden(n, number)
                    if not (last and n == U - 1):
                        rows_out(n + 1, number + 1)
                    if not (first and n == 0):
                        weigh(n - 1, number - 1)

            rows_out(0, 0)
            turn(0, True, False)
            with dve.Fori(1, MAX_TILES // U - 1) as i:
                turn(i, False, False)
            turn(MAX_TILES // U - 1, False, True)
            weigh(U - 1, MAX_TILES - 1)

        @block.tensor
        def _(pe):
            def one(step):
                nxt, prep, post, route = step.to(1), step.to(2), step.to(-1), step.to(-2)

                def stack(n, t):
                    j, h0 = n % 2, HALF * (n // 2)
                    to, used = ((bank_a, stack_a_sb), (bank_b, stack_b_sb))[t]
                    pe.wait_ge(parts_ready, nxt.count(QT, j + 1))
                    if n:
                        pe.wait_ge(used, nxt.count(4, n))
                    elif t == 0 and route.live():
                        pe.wait_ge(route_in, route.count(2, 1))
                    elif t == 1 and step.to(-3).live():
                        pe.wait_ge(rank_used, step.to(-3).count(1, 1))
                    for h in range(8):
                        i = nc.tensor.transpose(to[:, :].bitcast(BF16)[0:KROWS, h * P:(h + 1) * P],
                                                parts[j][:, t, h0 + h, :, :].rearrange("p r d -> p (r d)"),
                                                ident_b[:, :])
                    i.then_inc((stack_a_ps, stack_b_ps)[t], 1)

                def project(lhs, j, w, to, done):
                    for dt in range(DT):
                        i = nc.tensor.matmul(to, lhs[:, dt, j * P:(j + 1) * P], w[:, dt, :],
                                             start=dt == 0, stop=dt == DT - 1)
                    if done is not None:
                        i.then_inc(done, 1)

                def values(el, g):
                    pe.wait_ge(exp_done, el.count(H, GROUP * (g + 1)))
                    if g == 0:
                        pe.wait_ge(v_sb, el.count(QT, QT))
                    if g % 2 == 0 and el.after_first(QT, g // 2):
                        pe.wait_ge(heads_sb, el.count(QT, g // 2))
                    for kt in range(QT):
                        for s in range(GROUP):
                            h = GROUP * g + s
                            i = nc.tensor.matmul(
                                pv_bank[STRIP * s:STRIP * (s + 1), (g % 2) * S:(g % 2 + 1) * S],
                                v_aug[el.turn()][:, kt, h, :], probs[h % NPROB][:, kt * S:(kt + 1) * S],
                                start=kt == 0, stop=kt == QT - 1, tile_position=(0, STRIP * s))
                    i.then_inc(pv_ps, 1)

                def scores(v):
                    k, j, h0 = nxt.turn(), (v // 4) % 2, HALF * (v // 8) + 2 * (v % 4)
                    if v % 8 == 0:
                        pe.wait_ge(stack_a_sb, nxt.count(4, v // 4 + 2))
                        pe.wait_ge(stack_b_sb, nxt.count(4, v // 4 + 2))
                    if nxt.after_first(H, v - 1):
                        pe.wait_ge(max_done, nxt.count(H, v - 1))
                    for h in (h0, h0 + 1):
                        i = nc.tensor.matmul(s_bank[v % 2][:, (h - h0) * S:(h - h0 + 1) * S],
                                             q_st[k][0:KROWS, h, j * P:(j + 1) * P], k_st[k][0:KROWS, h, :],
                                             start=True, stop=True)
                    i.then_inc(s_ps, 1)

                def maxima_t(el, half):
                    pe.wait_ge(max_ready, el.count(2, half + 1))
                    for j in range(QT):
                        i = nc.tensor.transpose(
                            bank_c[:, :].bitcast(BF16)[0:MROWS * HALF, j * P:(j + 1) * P],
                            max_parts[half][:, j, :, :].rearrange("p m h -> p (m h)"), ident_b[:, :])
                    i.then_inc(max_t_ps, 1)

                for h in range(H):
                    if nxt.live() and h < 4:
                        stack(h, 1)
                    if step.live():
                        k = step.turn()
                        if h == 0:
                            pe.wait_ge(max_in[k], step.landed(32 * MROWS) - 16 * MROWS)
                            pe.wait_ge(stack_a_sb, step.count(4, 4))
                            pe.wait_ge(stack_b_sb, step.count(4, 4))
                        if h == HALF:
                            pe.wait_ge(max_in[k], step.landed(32 * MROWS))
                        if step.after_first(H, h - 1):
                            pe.wait_ge(exp_done, step.count(H, h - 1))
                        for kt in range(QT):
                            i = nc.tensor.matmul(st_bank[h % 2][:, kt * S:(kt + 1) * S],
                                                 k_st[k][0:KROWS + MROWS, h, kt * P:(kt + 1) * P],
                                                 q_st[k][0:KROWS + MROWS, h, :], start=True, stop=True)
                        i.then_inc(st_ps, 1)
                    if nxt.live() and h < 4:
                        stack(h, 0)
                    if nxt.live() and h < 2:
                        if h == 0:
                            pe.wait_ge(xhat_t_sb, nxt.count(1, 1))
                            if step.live():
                                pe.wait_ge(max_t_sb, step.count(2, 1))
                            pe.wait_ge(v_w_in, 16)
                            pe.wait_ge(ctx_in[nxt.turn()], nxt.landed())
                        project(ctx_sb[nxt.turn()], h, wv_sb, bank_c[:, h * D:(h + 1) * D], v_ps)
                    if nxt.live():
                        for v in S_UNITS[h]:
                            scores(v)
                    if step.live() and h in (5, 9, 13):
                        values(step, h // 4 - 1)
                    if post.live() and h == 1:
                        values(post, 3)
                    if step.live() and h == 4:
                        if nxt.live():
                            pe.wait_ge(v_sb, nxt.count(QT, QT))
                        maxima_t(step, 1)
                    if post.live() and h == 4:
                        pe.wait_ge(heads_sb, post.count(QT, QT))
                        if nxt.live():
                            pe.wait_ge(stack_a_sb, nxt.count(4, 4))
                            pe.wait_ge(stack_b_sb, nxt.count(4, 4))
                        if route.live():
                            pe.wait_ge(route_in, route.count(2, 1))
                        if step.to(-3).live():
                            pe.wait_ge(rank_used, step.to(-3).count(1, 1))
                        for j in range(QT):
                            for n in range(4):
                                i = nc.tensor.transpose(
                                    (bank_a, bank_b)[j][:, n * P:(n + 1) * P],
                                    heads_t[n // 2][:, (n % 2) * S + j * P:(n % 2) * S + (j + 1) * P], ident[:, :])
                            i.then_inc(heads_ps, 1)
                    if prep.live() and h == 5:
                        pe.wait_ge(xhat_ready, prep.count(QT, QT))
                        if nxt.live():
                            pe.wait_ge(v_sb, nxt.count(QT, QT))
                        if step.live():
                            pe.wait_ge(max_t_sb, step.count(2, 2))
                        for dt in range(DT):
                            for j in range(QT):
                                i = nc.tensor.transpose(bank_c[:, dt * S + j * P:dt * S + (j + 1) * P],
                                                        xhat[:, j, dt * P:(dt + 1) * P], ident[:, :])
                        i.then_inc(xhat_t_ps, 1)
                    if prep.live() and h in (7, 9):
                        j = (h - 7) // 2
                        to = (bank_a, bank_b)[j]
                        if h == 7:
                            pe.wait_ge(qk_w_in, 32)
                            pe.wait_ge(ctx_in[prep.turn()], prep.landed())
                            pe.wait_ge(xhat_t_sb, prep.count(1, 1))
                        if post.live():
                            pe.wait_ge(x1_ready, post.count(QT, j + 1))
                        elif nxt.live():
                            pe.wait_ge((stack_a_sb, stack_b_sb)[j], nxt.count(4, 4))
                        project(xhat_t, j, wq_sb, to[:, 0:D], None)
                        project(ctx_sb[prep.turn()], j, wk_sb, to[:, D:2 * D], proj_ps)
                    if post.live() and h == 8:
                        pe.wait_ge(xn_ready, post.count(QT, QT))
                        if prep.live():
                            pe.wait_ge(xhat_t_sb, prep.count(1, 1))
                        if step.live():
                            pe.wait_ge(max_t_sb, step.count(2, 2))
                        if nxt.live():
                            pe.wait_ge(v_sb, nxt.count(QT, QT))
                        if route.live():
                            pe.wait_ge(xn_t_sb, route.count(1, 1))
                        for dt in range(DT):
                            for j in range(QT):
                                i = nc.tensor.transpose(bank_c[:, dt * S + j * P:dt * S + (j + 1) * P],
                                                        xn[post.turn()][:, j, dt * P:(dt + 1) * P], ident[:, :])
                        i.then_inc(xn_t_ps, 1)
                    if nxt.live() and h == 10:
                        if post.live():
                            pe.wait_ge(xn_t_sb, post.count(1, 1))
                        if prep.live():
                            pe.wait_ge(xhat_t_sb, prep.count(1, 1))
                        if step.live():
                            pe.wait_ge(max_t_sb, step.count(2, 2))
                        pe.wait_ge(v_sb, nxt.count(QT, QT))
                        maxima_t(nxt, 0)
                    if post.live() and h == 11:
                        pe.wait_ge(xn_t_sb, post.count(1, 1))
                        pe.wait_ge(x1_ready, post.count(QT, QT))
                        pe.wait_ge(r_w_in, 16)
                        if prep.live():
                            pe.wait_ge(qkf_ready, prep.count(QT, 1))
                        for j in range(QT):
                            project(xn_t, j, wr_sb, bank_a[:, j * E:(j + 1) * E], logit_ps if j == QT - 1 else None)
                    if route.live() and h == 12:
                        pe.wait_ge(routed_ready, route.count(1, 1))
                        if prep.live():
                            pe.wait_ge(qkf_ready, prep.count(QT, QT))
                        if nxt.live():
                            pe.wait_ge(stack_b_sb, nxt.count(4, 4))
                        if post.live():
                            pe.wait_ge(x1_ready, post.count(QT, QT))
                        if step.to(-3).live():
                            pe.wait_ge(rank_used, step.to(-3).count(1, 1))
                        nc.tensor.matmul(bank_b[:, 0:E], earlier[:, :], routed[:, 0, :], start=True, stop=True)
                        nc.tensor.matmul(bank_b[:, E:2 * E], earlier[:, :], routed[:, 1, :], start=True, stop=False)
                        nc.tensor.matmul(bank_b[:, E:2 * E], ones_b[:, :], routed[:, 0, :], start=False, stop=True)
                        nc.tensor.matmul(bank_b[:, 2 * E:3 * E], ones_b[:, :], routed[:, 0, :], start=True, stop=False)
                        nc.tensor.matmul(bank_b[:, 2 * E:3 * E], ones_b[:, :], routed[:, 1, :], start=False,
                                         stop=True).then_inc(rank_ps, 1)

            pe.wait_ge(const_ready, 1)
            steps(pe, one)

            w_gu_of = w_gu[:, :, :, :, :].rearrange("p t g e f -> p (t g) (e f)")
            w_dn_of = w_dn.rearrange("p t e d -> p t (e d)")

            def rows_in_t(n, number, landed):
                pe.wait_ge(rows_got[n % NX], landed)
                for dt in range(DT):
                    i = nc.tensor.transpose(bank[0][:, dt * P:(dt + 1) * P], rows_in[n % NX][:, dt * P:(dt + 1) * P],
                                            ident[:, :])
                i.then_inc(rows_ps, 1)

            def gate_up(n, number, expert):
                pe.wait_ge(rows_sb, number + 1)
                if not isinstance(number, int) or number > 1:
                    pe.wait_ge(hid_ready, number - 1)
                for g, done in enumerate((gate_ps, up_ps)):
                    for dt in range(DT):
                        i = nc.tensor.matmul(gu_bank[n % 2][g][:, :], rows_t[n % 2][:, dt, :],
                                             w_gu_of[:, dt * 2 + g, bass.ds(expert * F, F)],
                                             start=dt == 0, stop=dt == DT - 1)
                    i.then_inc(done, 1)

            def down(n, number, expert):
                pe.wait_ge(hid_sb, number + 1)
                if not isinstance(number, int) or number > 0:
                    pe.wait_ge(y_ready, number)
                for ft in range(FT):
                    i = nc.tensor.matmul(bank[4][:, 0:D], hid_t[n % 2][:, ft, :],
                                         w_dn_of[:, ft, bass.ds(expert * D, D)], start=ft == 0, stop=ft == FT - 1)
                i.then_inc(y_ps, 1)

            def hidden_t(n, number):
                pe.wait_ge(hid_ready, number + 1)
                if not isinstance(number, int) or number > 0:
                    pe.wait_ge(hid_sb, number)
                for ft in range(FT):
                    i = nc.tensor.transpose(bank[3][:, ft * P:(ft + 1) * P], hid[n % 2][:, ft * P:(ft + 1) * P],
                                            ident[:, :])
                i.then_inc(hid_ps, 1)

            def load_expert(number):
                return pe.value_load(plan_exp[0:1, number], min_val=0, max_val=E - 1)

            def turn(i, first, last):
                expert = None if first else load_expert(bass.ds(U * i - 1, 1) if not isinstance(i, int) else
                                                        slice(U * i - 1, U * i))
                for n in range(U):
                    number = U * i + n
                    before = expert
                    expert = load_expert(slice(number, number + 1) if isinstance(number, int) else bass.ds(number, 1))
                    gate_up(n, number, expert)
                    if not (last and n == U - 1):
                        rows_in_t(n + 1, number + 1, 16 * ((U // NX) * i + (n + 1) // NX + 1))
                    if not (first and n == 0):
                        down(n - 1, number - 1, before)
                    hidden_t(n, number)

            pe.wait_ge(plan_ready, 1)
            pe.wait_ge(ffn_w_in, 16 * DT * 2)
            pe.wait_ge(down_w_in, 16 * FT)
            rows_in_t(0, 0, 16)
            turn(0, True, False)
            with pe.Fori(1, MAX_TILES // U - 1) as i:
                turn(i, False, False)
            turn(MAX_TILES // U - 1, False, True)
            down(U - 1, MAX_TILES - 1, load_expert(slice(MAX_TILES - 1, MAX_TILES)))


def kernel(x, ctx_1024, g_xattn, g_ffn, L0_xattn_Wq, L0_xattn_bq, L0_xattn_Wk, L0_xattn_bk, L0_xattn_Wv,
           L0_xattn_bv, L0_ffn_router_kernel_DE, L0_ffn_kernel_gating_EDF, L0_ffn_kernel_up_EDF,
           L0_ffn_kernel_down_EFD):
    import concourse.bacc as bacc
    from concourse.bass_utils import run_bass_kernel_spmd

    def laid(a):
        return np.ascontiguousarray(np.asarray(a))

    arrays = {
        "x": laid(x),
        "ctx_t": laid(np.asarray(ctx_1024).reshape(TOKENS, D).T),
        "g_xattn": laid(g_xattn),
        "g_ffn": laid(g_ffn),
        "wq_t": laid(np.asarray(L0_xattn_Wq).T),
        "bq": laid(L0_xattn_bq),
        "wk_t": laid(np.asarray(L0_xattn_Wk).T),
        "bk": laid(L0_xattn_bk),
        "wv_t": laid(np.asarray(L0_xattn_Wv).T),
        "bv": laid(L0_xattn_bv),
        "w_router": laid(L0_ffn_router_kernel_DE),
        "w_gate": laid(L0_ffn_kernel_gating_EDF),
        "w_up": laid(L0_ffn_kernel_up_EDF),
        "w_down": laid(L0_ffn_kernel_down_EFD),
    }
    nc = bacc.Bacc("TRN2", target_bir_lowering=False, num_devices=1)
    args = [nc.dram_tensor(f"in_{n}", a.shape, mybir.dt.from_np(a.dtype), kind="ExternalInput").ap()
            for n, a in arrays.items()]
    out = nc.dram_tensor("out_rows", (TOKENS + SPARE, D), F32, kind="ExternalOutput").ap()
    program(nc, *args, out)
    r = run_bass_kernel_spmd(nc, [{f"in_{n}": a for n, a in arrays.items()}], core_ids=[0])
    return r.results[0]["out_rows"][:TOKENS].reshape(B, S, D)
```

```python
from contextlib import ExitStack

import numpy as np

import concourse.bass as bass
from concourse import mybir

F32 = mybir.dt.float32
F32R = mybir.dt.float32r
BF16 = mybir.dt.bfloat16
I32 = mybir.dt.int32
U32 = mybir.dt.uint32
ACT = mybir.ActivationFunctionType
ALU = mybir.AluOpType
AX = mybir.AxisListType

P = 128
B, S, D = 16, 256, 256
H, HD = 16, 16
E, F = 8, 512
TOKENS = B * S
DT = D // P
FT = F // P
QT = S // P
PARTS = 6
KROWS = PARTS * HD
MROWS = 2
STRIP = 32
VW = HD + 1
GROUP = 4
EPS = 1e-5
K_TOP = 2
TABLE = E * TOKENS
MAX_TILES = TOKENS * K_TOP // P + E - 1
SPARE = P
TABLE_ROWS = TABLE + E * P
HALF = H // 2
ROUTE_STEPS = 21


class Step:

    def __init__(self, i, c):
        self.i, self.c = i, c

    def to(self, k):
        return Step(self.i, self.c + k)

    def live(self):
        return not isinstance(self.i, int) or 0 <= self.c < B

    def count(self, each, more=0):
        assert each * self.c + more > 0
        return 2 * each * self.i + (each * self.c + more)

    def after_first(self, each, more=0):
        return not isinstance(self.i, int) or each * self.c + more > 0

    def turn(self):
        return self.c % 2

    def landed(self, each=16):
        assert self.c >= 0
        return each * self.i + each * (self.c // 2 + 1)

    def second(self):
        return not isinstance(self.i, int) or self.c >= 2

    def rows(self):
        return bass.ds((2 * self.i + self.c) * S, S)


def program(nc, x, ctx_t, g_xattn, g_ffn, wq_t, bq, wk_t, bk, wv_t, bv, w_router, w_gate, w_up, w_down, out):
    stack = ExitStack()
    with stack:

        def sb(name, shape, dt=F32):
            return stack.enter_context(nc.sbuf_tensor(name, shape, dt))

        def sem(name):
            return stack.enter_context(nc.semaphore(name))

        def sems(name, n):
            return [sem(f"{name}{k}") for k in range(n)]

        normed = nc.dram_tensor("normed_rows", [TOKENS + SPARE, D], F32, kind="Internal").ap()
        table = nc.dram_tensor("expert_rows", [TABLE_ROWS, 2], F32, kind="Internal").ap()

        ident = sb("ident", [P, P])
        ident_b = sb("ident_b", [P, P], BF16)
        earlier = sb("earlier", [P, P], BF16)
        ones_b = sb("ones_b", [P, P], BF16)
        wr_sb = sb("wr_sb", [P, DT, E])
        gates = sb("gates", [P, 2])
        tanh_g = sb("tanh_g", [P, 2])
        prefer = sb("prefer", [P, E])
        token_f = sb("token_f", [P, QT])
        base = sb("base", [P, E])

        maxes = sb("maxes", [P, 2, QT, HALF])
        max_parts = [sb(f"max_parts{k}", [P, QT, MROWS, HALF], BF16) for k in range(2)]
        max_t = [sb(f"max_t{k}", [MROWS * HALF, S], BF16) for k in range(2)]
        stats = sb("stats", [P, QT, 6])
        mv = sb("mv", [P, QT, 2])
        rstd = sb("rstd", [P, QT])
        stats2 = sb("stats2", [P, QT, 6])
        mv2 = sb("mv2", [P, QT, 2])
        rstd2 = sb("rstd2", [P, QT])
        den = sb("den", [P, QT, H])
        shift, shift2 = sb("shift", [P, QT]), sb("shift2", [P, QT])
        minus_half = sb("minus_half", [P, QT])
        lg = sb("lg", [P, QT, E])
        ex = sb("ex", [P, QT, E])
        pr = sb("pr", [P, QT, E])
        eq = sb("eq", [P, QT, E])
        key = sb("key", [P, QT, E])
        sel = [sb(f"sel{k}", [P, QT, E]) for k in range(K_TOP)]
        routed = sb("routed", [P, QT, E], BF16)
        top_lg = sb("top_lg", [P, QT])
        r1 = sb("r1", [P, QT])
        r2 = sb("r2", [P, QT])
        best = sb("best", [P, QT])
        edge = sb("edge", [P, QT])
        edge_e = sb("edge_e", [P, QT])
        pos = sb("pos", [P, QT, E])
        slot_f = sb("slot_f", [P, K_TOP, QT])
        slots = [sb(f"slots{k}", [P, K_TOP * QT], U32) for k in range(2)]
        entry = [sb(f"entry{k}", [P, K_TOP * QT, 2]) for k in range(2)]
        count_i = sb("count_i", [P, E], I32)
        n_tiles = sb("n_tiles", [P, E])
        cum_a = sb("cum_a", [P, E])
        cum_b = sb("cum_b", [P, E])
        tile_no = sb("tile_no", [P, MAX_TILES])
        past = sb("past", [P, MAX_TILES, E])
        past_n = sb("past_n", [P, MAX_TILES, E])
        t_exp = sb("t_exp", [P, MAX_TILES])
        t_row = sb("t_row", [P, MAX_TILES])
        plan_exp = sb("plan_exp", [P, MAX_TILES], I32)
        plan_row = sb("plan_row", [P, MAX_TILES], I32)
        NW = 8
        AHEAD = 3
        U = 8
        TURNS = -(-MAX_TILES // U)
        LAST_TILES = MAX_TILES - U * (TURNS - 1)
        row_info = [sb(f"row_info{k}", [P, 2]) for k in range(NW)]

        attention_stack = ExitStack()
        w_gu = attention_stack.enter_context(nc.sbuf_tensor("w_gu", [P, DT, 2, E, F], F32))
        WORK = 31232
        work = attention_stack.enter_context(nc.sbuf_tensor("work", [P, WORK], F32))
        at = [0]
        PART = 2 * E * F

        def take(n_f32):
            a = work[:, at[0]:at[0] + n_f32]
            at[0] += n_f32
            return a

        xin = [take(QT * D).rearrange("p (j d) -> p j d", j=QT) for _ in range(2)]
        ctx_sb = [take(DT * S).rearrange("p (t s) -> p t s", t=DT) for _ in range(2)]
        xhat = take(QT * D).rearrange("p (j d) -> p j d", j=QT)
        xhat_t = take(DT * S).rearrange("p (t s) -> p t s", t=DT)
        qkf = [take(2 * D) for _ in range(QT)]
        rest = [take(2 * D) for _ in range(QT)]
        parts = [take(PARTS * D).bitcast(BF16).rearrange("p (t h r d) -> p t h r d", t=2, h=H, r=PARTS)
                 for _ in range(QT)]
        assert at[0] == PART
        wq_sb = take(DT * D).rearrange("p (t d) -> p t d", t=DT)
        wk_sb = take(DT * D).rearrange("p (t d) -> p t d", t=DT)
        wv_sb = take(DT * D).rearrange("p (t d) -> p t d", t=DT)
        bqk = take(2 * D)
        bv_sb = take(D)
        zeros = take(D)
        fill_id = take(TABLE_ROWS // P).bitcast(I32)
        fill = take(TABLE_ROWS // P * 2).rearrange("p (a w) -> p a w", w=2)
        assert at[0] <= PART + PART // 2
        at[0] = PART + PART // 2
        q_st = [take(H * S // 2).bitcast(BF16).rearrange("p (h s) -> p h s", h=H) for _ in range(2)]
        k_st = [take(H * S // 2).bitcast(BF16).rearrange("p (h s) -> p h s", h=H) for _ in range(2)]
        v_aug = [take(QT * H * STRIP).rearrange("p (j h d) -> p j h d", j=QT, h=H) for _ in range(2)]
        NPROB = 8
        probs = [take(QT * S) for _ in range(NPROB)]
        heads_t = [take(2 * S) for _ in range(2)]
        xres = [take(QT * D).rearrange("p (j d) -> p j d", j=QT) for _ in range(2)]
        x1 = [take(QT * D).rearrange("p (j d) -> p j d", j=QT) for _ in range(2)]
        xn = [take(QT * D).rearrange("p (j d) -> p j d", j=QT) for _ in range(2)]
        xn_t = take(DT * S).rearrange("p (t s) -> p t s", t=DT)
        assert at[0] <= WORK, at[0]
        attention_stack.close()

        w_lo = sb("w_lo", [P, DT, 2, E * F], F32R)
        hi_0 = sb("hi_0", [P, 2, E * F], F32R)
        hi_10 = sb("hi_10", [P, E * F], F32R)
        w_dn = sb("w_dn", [P, FT, E * D])
        hi_11 = sb("hi_11", [P, E * F], F32R)
        hi = [[hi_0[:, 0, :], hi_0[:, 1, :]], [hi_10[:, :], hi_11[:, :]]]
        NX = 4
        rows_in = [sb(f"rows_in{k}", [P, D]) for k in range(NX)]
        rows_hi = [sb(f"rows_hi{k}", [P, DT, P], F32R) for k in range(2)]
        rows_lo = [sb(f"rows_lo{k}", [P, DT, P], F32R) for k in range(2)]
        silu = [sb(f"silu{k}", [P, F]) for k in range(2)]
        hid = [sb(f"hid{k}", [P, F]) for k in range(2)]
        hid_t = [sb(f"hid_t{k}", [P, FT, P]) for k in range(2)]
        y_sb = [sb(f"y_sb{k}", [P, D]) for k in range(2)]

        bank = [stack.enter_context(nc.psum_tensor(f"bank{k}", [P, 512], F32)) for k in range(8)]
        st_bank = [bank[0], bank[1]]
        s_bank = [bank[2], bank[3]]
        pv_bank = bank[4]
        bank_a, bank_b, bank_c = bank[5], bank[6], bank[7]
        stack_b_bank = [bank_b, bank_b, bank_b, bank_c]
        gu_bank = [(bank[1], bank[2]), (bank[5], bank[6])]

        iota_done, const_ready, gate_in = sem("iota_done"), sem("const_ready"), sem("gate_in")
        gate_ready = sem("gate_ready")
        qk_w_in, v_w_in, r_w_in, bias_in = sem("qk_w_in"), sem("v_w_in"), sem("r_w_in"), sem("bias_in")
        fill_ready, fill_out = sem("fill_ready"), sem("fill_out")
        ffn_w_in, down_w_in = sem("ffn_w_in"), sem("down_w_in")
        x_in, xres_in, ctx_in = sems("x_in", 2), sems("xres_in", 2), sems("ctx_in", 2)
        max_in, x1_out, xn_out, table_out = (sems("max_in", 2), sems("x1_out", 2), sems("xn_out", 2),
                                             sems("table_out", 2))
        xhat_t_ps, proj_ps, v_ps, stack_a_ps = sem("xhat_t_ps"), sem("proj_ps"), sem("v_ps"), sem("stack_a_ps")
        stack_b_ps = sem("stack_b_ps")
        s_ps, max_t_ps, st_ps, pv_ps = sem("s_ps"), sem("max_t_ps"), sem("st_ps"), sem("pv_ps")
        heads_ps, xn_t_ps, logit_ps, rank_ps = (sem("heads_ps"), sem("xn_t_ps"), sem("logit_ps"),
                                                sem("rank_ps"))
        xhat_t_sb, part1, part2, stack_b_sb = sem("xhat_t_sb"), sem("part1"), sem("part2"), sem("stack_b_sb")
        max_t_sb, exp_done, heads_sb, xn_t_sb = (sem("max_t_sb"), sem("exp_done"), sem("heads_sb"),
                                                 sem("xn_t_sb"))
        route_exp = sem("route_exp")
        var_ready, var2_ready = sem("var_ready"), sem("var2_ready")
        xhat_ready, qkf_ready, parts_ready, v_sb = (sem("xhat_ready"), sem("qkf_ready"), sem("parts_ready"),
                                                    sem("v_sb"))
        stack_a_sb, max_done, max_ready, x1_ready = (sem("stack_a_sb"), sem("max_done"), sem("max_ready"),
                                                     sem("x1_ready"))
        xn_ready, route_in, routed_ready, rank_used = (sem("xn_ready"), sem("route_in"), sem("routed_ready"),
                                                       sem("rank_used"))
        entry_ready, plan_ready = sem("entry_ready"), sem("plan_ready")
        fill_step, norm_step, norm2_step, res_step = (sem("fill_step"), sem("norm_step"), sem("norm2_step"),
                                                      sem("res_step"))
        heads_gated = sem("heads_gated")
        max_step, logit_step = sem("max_step"), sem("logit_step")
        route_step, plan_step = sem("route_step"), sem("plan_step")
        dve_went_on, pool_went_on, sp_went_on = sem("dve_went_on"), sem("pool_went_on"), sem("sp_went_on")
        rest_ready, part3 = sem("rest_ready"), sem("part3")
        rstd_ready, rstd2_ready = sem("rstd_ready"), sem("rstd2_ready")
        rstd_step, rstd2_step = sem("rstd_step"), sem("rstd2_step")
        info_in, rows_got, y_out = sems("info_in", NW), sems("rows_got", NX), sem("y_out")
        rows_ps, rows_sb, gate_ps, up_ps = sem("rows_ps"), sem("rows_sb"), sem("gate_ps"), sem("up_ps")
        silu_done, hid_ready, hid_ps, hid_sb = sem("silu_done"), sem("hid_ready"), sem("hid_ps"), sem("hid_sb")
        y_ps, y_ready = sem("y_ps"), sem("y_ready")
        rows_hi_sb, hi_ready, lo_ready = sem("rows_hi_sb"), sem("hi_ready"), sem("lo_ready")
        pool_lo_ready = sem("pool_lo_ready")

        x_rows = x.rearrange("b s d -> (b s) d")

        def token_tiles(dram, step):
            return dram[step.rows(), :].rearrange("(j p) d -> p j d", p=P)

        S_UNITS = [(), (), (0,), (1,), (2,), (3,), (4,), (5,), (6,), (7,), (8,), (9,), (10,), (11, 12), (13,), (14,)]
        S_LAST = H - 1

        FIRST, LAST = 4, B - 3
        PAIRS = (LAST - FIRST + 1) // 2

        def steps(eng, one):
            for c in range(-2, FIRST):
                one(Step(0, c))
            with eng.Fori(0, PAIRS) as i:
                for c in range(2):
                    one(Step(i, FIRST + c))
            for c in range(LAST + 1, B + 2):
                one(Step(0, c))

        PIECES = DT * 2 * 2

        def piece(n):
            return n // 4, n // 2 % 2, slice(n % 2 * E // 2, (n % 2 + 1) * E // 2)

        def piece_hi(n):
            dt, g, e = piece(n)
            return hi[dt][g][:, e.start * F:e.stop * F]

        def piece_raw(n):
            dt, g, e = piece(n)
            return w_gu[:, dt, g, e, :].rearrange("p e f -> p (e f)")

        def last_element(el):
            return isinstance(el.i, int) and el.c == B - 1

        def lower_part(engine, n):
            dt, g, e = piece(n)
            return engine.tensor_tensor(w_lo[:, dt, g, e.start * F:e.stop * F], piece_raw(n),
                                        piece_hi(n).bitcast(F32), ALU.subtract)

        block = stack.enter_context(nc.Block())

        @block.sync
        def _(sp):
            def load(step):
                k = step.turn()
                if step.second():
                    sp.wait_ge(xhat_ready, step.count(QT, -QT))
                    sp.sem_inc(sp_went_on, 1)
                sp.dma_start(xin[k], token_tiles(x_rows, step)).then_inc(x_in[k], 16)
                if step.second():
                    sp.wait_ge(v_ps, step.count(QT, -QT))
                    sp.sem_inc(sp_went_on, 1)
                sp.dma_start(ctx_sb[k], ctx_t[:, step.rows()].rearrange("(t p) s -> p t s", p=P)
                             ).then_inc(ctx_in[k], 16)

            sp.dma_start(xin[0], token_tiles(x_rows, Step(0, 0))).then_inc(x_in[0], 16)
            sp.dma_start(wq_sb, wq_t.rearrange("(t p) n -> p t n", p=P)).then_inc(qk_w_in, 16)
            sp.dma_start(ctx_sb[0], ctx_t[:, 0:S].rearrange("(t p) s -> p t s", p=P)).then_inc(ctx_in[0], 16)
            sp.dma_start(wk_sb, wk_t.rearrange("(t p) n -> p t n", p=P)).then_inc(qk_w_in, 16)
            sp.dma_start(bqk[:, 0:D], bq.partition_broadcast(P)).then_inc(bias_in, 16)
            sp.dma_start(bqk[:, D:2 * D], bk.partition_broadcast(P)).then_inc(bias_in, 16)
            sp.dma_start(wv_sb, wv_t.rearrange("(t p) n -> p t n", p=P)).then_inc(v_w_in, 16)
            sp.dma_start(bv_sb, bv.partition_broadcast(P)).then_inc(bias_in, 16)
            sp.dma_start(wr_sb[:, :, :], w_router.rearrange("(t p) e -> p t e", p=P)).then_inc(r_w_in, 16)
            load(Step(0, 1))
            sp.wait_ge(const_ready, 1)
            sp.dma_start(out[TOKENS:TOKENS + SPARE, :], zeros).then_inc(fill_out, 16)
            sp.dma_start(normed[TOKENS:TOKENS + SPARE, :], zeros).then_inc(fill_out, 16)
            sp.wait_ge(fill_ready, 1)
            sp.dma_start(table.rearrange("(p a) w -> p a w", p=P), fill[:, :, :]).then_inc(fill_out, 16)

            def max_rows(el, half):
                k = el.turn()
                sp.wait_ge(max_t_sb, el.count(2, half + 1))
                sp.sem_inc(sp_went_on, 1)
                if el.after_first(H, -H):
                    sp.wait_ge(st_ps, el.count(H, -H))
                    sp.sem_inc(sp_went_on, 1)
                for m in range(MROWS):
                    sp.dma_start(q_st[k][KROWS + m:KROWS + m + 1, HALF * half:HALF * (half + 1), :],
                                 max_t[half][m * HALF:(m + 1) * HALF, :]).then_inc(max_in[k], 16)

            def one(step):
                prep, nxt, post = step.to(2), step.to(1), step.to(-1)
                if prep.live() and step.c >= 0:
                    load(prep)
                if step.live():
                    k = step.turn()
                    if step.second():
                        sp.wait_ge(x1_ready, step.count(QT, -QT))
                        sp.sem_inc(sp_went_on, 1)
                    sp.dma_start(xres[k], token_tiles(x_rows, step)).then_inc(xres_in[k], 16)
                if step.live():
                    max_rows(step, 1)
                if isinstance(step.i, int) and -1 <= step.c < 4:
                    for n in ((0,), (1,), (2, 3), (4, 5), (6, 7))[step.c + 1]:
                        dt, g, e = piece(n)
                        sp.dma_start(w_gu[:, dt, g, e, :],
                                     (w_gate, w_up)[g][e, dt * P:(dt + 1) * P, :].rearrange("e p f -> p e f")
                                     ).then_inc(ffn_w_in, 16)
                if post.live():
                    k = post.turn()
                    sp.wait_ge(x1_ready, post.count(QT, QT))
                    sp.sem_inc(sp_went_on, 1)
                    sp.dma_start(token_tiles(out, post), x1[k]).then_inc(x1_out[k], 16)
                    sp.wait_ge(xn_ready, post.count(QT, QT))
                    sp.sem_inc(sp_went_on, 1)
                    sp.dma_start(token_tiles(normed, post), xn[k]).then_inc(xn_out[k], 16)
                if nxt.live():
                    max_rows(nxt, 0)

                if isinstance(step.i, int) and step.c == B - 1:
                    sp.wait_ge(st_ps, H * B)
                    for t in range(FT):
                        sp.dma_start(w_dn[:, t, :].rearrange("p (e d) -> p e d", e=E), w_down[:, t * P:(t + 1) * P, :].rearrange("e p d -> p e d")
                                     ).then_inc(down_w_in, 16)

            steps(sp, one)
            sp.wait_ge(plan_ready, 1)
            sp.wait_ge(table_out[0], 16 * K_TOP * QT * B // 2)
            sp.wait_ge(table_out[1], 16 * K_TOP * QT * B // 2)
            sp.wait_ge(fill_out, 48)

            def info(k, number, used):
                if used is not None:
                    sp.wait_ge(y_ready, used)
                    sp.sem_inc(sp_went_on, 1)
                    sp.wait_ge(y_out, 16 * used)
                    sp.sem_inc(sp_went_on, 1)
                row = sp.value_load(plan_row[0:1, number], min_val=0, max_val=TABLE_ROWS - P)
                sp.dma_start(row_info[k][:, :], table[bass.ds(row, P), :]).then_inc(info_in[k], 16)

            for k in range(NW):
                info(k, slice(k, k + 1), None)
            with sp.Fori(1, MAX_TILES // NW) as i:
                for k in range(NW):
                    info(k, bass.ds(NW * i + k, 1), NW * i + (k + 1 - NW))
            for n in range(MAX_TILES // NW * NW, MAX_TILES):
                info(n % NW, slice(n, n + 1), n + 1 - NW)
            sp.wait_ge(y_out, 16 * MAX_TILES)

        @block.gpsimd
        def _(pool):
            nc.gpsimd.memset(ident[:, :], 0.0)
            nc.gpsimd.memset(ident_b[:, :], 0.0)
            nc.gpsimd.memset(earlier[:, :], 1.0)
            nc.gpsimd.memset(ones_b[:, :], 1.0).then_inc(iota_done, 1)
            pool.wait_ge(iota_done, 1)
            nc.gpsimd.affine_select(out=ident[:, :], in_=ident[:, :], compare_op=ALU.not_equal, fill=1.0,
                                    base=0, pattern=[[-1, P]], channel_multiplier=1)
            nc.gpsimd.affine_select(out=ident_b[:, :], in_=ident_b[:, :], compare_op=ALU.not_equal, fill=1.0,
                                    base=0, pattern=[[-1, P]], channel_multiplier=1)
            nc.gpsimd.affine_select(out=earlier[:, :], in_=earlier[:, :], compare_op=ALU.is_gt, fill=0.0,
                                    base=0, pattern=[[1, P]], channel_multiplier=-1)
            nc.gpsimd.memset(zeros, 0.0)
            nc.gpsimd.memset(minus_half[:, :], -0.5)
            for k in range(2):
                nc.gpsimd.memset(v_aug[k][:, :, :, HD:STRIP], 0.0)
            nc.gpsimd.iota(fill_id, pattern=[[1, TABLE_ROWS // P]], base=0,
                           channel_multiplier=TABLE_ROWS // P)
            nc.gpsimd.iota(token_f[:, :], pattern=[[P, QT]], base=0, channel_multiplier=1,
                           allow_small_or_imprecise_dtypes=True)
            nc.gpsimd.iota(prefer[:, :], pattern=[[-1, E]], base=E, channel_multiplier=0,
                           allow_small_or_imprecise_dtypes=True)
            nc.gpsimd.iota(base[:, :], pattern=[[TOKENS, E]], base=0, channel_multiplier=0,
                           allow_small_or_imprecise_dtypes=True)
            nc.gpsimd.iota(tile_no[:, :], pattern=[[1, MAX_TILES]], base=0, channel_multiplier=0,
                           allow_small_or_imprecise_dtypes=True)
            nc.gpsimd.memset(fill[:, :, 1:2], 0.0).then_inc(iota_done, 1)
            pool.wait_ge(iota_done, 2)
            for k in range(2):
                nc.gpsimd.memset(v_aug[k][:, :, :, HD:VW], 1.0)
            nc.gpsimd.nop().then_inc(const_ready, 1)

            def one(step):
                prep, post, route = step.to(2), step.to(-1), step.to(-2)

                def residue(j):
                    pool.wait_ge(part1, prep.count(QT, j + 1))
                    if prep.after_first(QT, j - 1):
                        pool.wait_ge(part3, prep.count(QT, j - 1))
                    nc.gpsimd.tensor_tensor(
                        rest[j].rearrange("p (t h d) -> p t h d", t=2, h=H),
                        qkf[j].rearrange("p (t h d) -> p t h d", t=2, h=H),
                        parts[j][:, :, :, 0, :], ALU.subtract).then_inc(rest_ready, 1)

                def third(j):
                    pool.wait_ge(part2, prep.count(QT, j + 1))
                    pool.wait_ge(rest_ready, prep.count(QT, j + 1))
                    r = rest[j].rearrange("p (t h d) -> p t h d", t=2, h=H)
                    nc.gpsimd.tensor_tensor(parts[j][:, 0, :, 5, :], r[:, 0, :, :], parts[j][:, 0, :, 3, :],
                                            ALU.subtract)
                    nc.gpsimd.tensor_tensor(parts[j][:, 1, :, 2, :], r[:, 1, :, :], parts[j][:, 1, :, 1, :],
                                            ALU.subtract).then_inc(part3, 1)

                def norm_scale(el, mv_of, rstd_of, shift_of, step_sem, done):
                    nc.gpsimd.tensor_tensor(rstd_of[:, :], mv_of[:, :, 1], minus_half[:, :], ALU.pow).then_inc(step_sem, 1)
                    pool.wait_ge(step_sem, el.count(1, 1))
                    nc.gpsimd.tensor_tensor(shift_of[:, :], mv_of[:, :, 0], rstd_of[:, :], ALU.mult).then_inc(done, 1)

                def add_x(j):
                    k = post.turn()
                    if j == 0:
                        pool.wait_ge(xres_in[k], post.landed())
                    pool.wait_ge(heads_gated, post.count(QT, j + 1))
                    nc.gpsimd.tensor_tensor(x1[k][:, j, :], x1[k][:, j, :], xres[k][:, j, :], ALU.add
                                            ).then_inc(x1_ready, 1)

                if prep.live():
                    pool.wait_ge(var_ready, prep.count(1, 1))
                    if prep.after_first(QT, 0):
                        pool.wait_ge(xhat_ready, prep.count(QT, 0))
                    norm_scale(prep, mv, rstd, shift, rstd_step, rstd_ready)
                if post.live():
                    if not last_element(post):
                        add_x(0)
                        add_x(1)
                    pool.wait_ge(var2_ready, post.count(1, 1))
                    if post.after_first(QT, 0):
                        pool.wait_ge(xn_ready, post.count(QT, 0))
                    norm_scale(post, mv2, rstd2, shift2, rstd2_step, rstd2_ready)
                if prep.live():
                    residue(0)
                    third(0)
                    residue(1)
                    third(1)
                if isinstance(step.i, int) and step.c in (B - 1, B):
                    n = PIECES - 3 if step.c == B - 1 else PIECES - 1
                    pool.wait_ge(hi_ready, n + 1)
                    lower_part(nc.gpsimd, n).then_inc(pool_lo_ready, 1)
                if isinstance(step.i, int) and step.c == 1:
                    pool.wait_ge(fill_out, 48)
                if route.live():
                    k = route.turn()
                    pool.wait_ge(entry_ready, route.count(1, 1))
                    pool.sem_inc(pool_went_on, 1)
                    for n in range(K_TOP * QT):
                        nc.gpsimd.indirect_dma_start(
                            out=table[:, :], out_offset=bass.IndirectOffsetOnAxis(ap=slots[k][:, n:n + 1], axis=0),
                            in_=entry[k][:, n, :], in_offset=None).then_inc(table_out[k], 16)

            steps(pool, one)

            def gather(k, w, landed, used):
                pool.wait_ge(info_in[w], landed)
                if used is not None:
                    pool.wait_ge(rows_ps, used)
                pool.sem_inc(pool_went_on, 1)
                nc.gpsimd.indirect_dma_start(
                    out=rows_in[k][:, :], out_offset=None, in_=normed[:, :],
                    in_offset=bass.IndirectOffsetOnAxis(ap=row_info[w][:, 0:1].bitcast(U32), axis=0)
                ).then_inc(rows_got[k], 16)

            def scatter(k, w, number):
                pool.wait_ge(y_ready, number + 1)
                if not isinstance(number, int) or number > 0:
                    pool.wait_ge(y_out, 16 * number)
                pool.sem_inc(pool_went_on, 1)
                nc.gpsimd.indirect_dma_start(
                    out=out[:, :], out_offset=bass.IndirectOffsetOnAxis(ap=row_info[w][:, 0:1].bitcast(U32), axis=0),
                    in_=y_sb[k][:, :], in_offset=None, compute_op=ALU.add).then_inc(y_out, 16)

            for k in range(2):
                pool.wait_ge(x1_out[k], 16 * B // 2)
                pool.wait_ge(xn_out[k], 16 * B // 2)
            pool.wait_ge(fill_out, 48)
            pool.wait_ge(pv_ps, B * H // GROUP)
            pool.wait_ge(logit_ps, B)
            for n in range(AHEAD):
                gather(n % NX, n % NW, 16, None)

            def turn(i, first, last):
                for n in range(LAST_TILES if last else U):
                    if not (last and n >= LAST_TILES - AHEAD):
                        m = n + AHEAD
                        gather(m % NX, m % NW, 16 * (U // NW) * i + 16 * (m // NW + 1),
                               None if first and m < NX else U * i + (m - NX + 1))
                    scatter(n % 2, n % NW, U * i + n)

            turn(0, True, False)
            with pool.Fori(1, TURNS - 1) as i:
                turn(i, False, False)
            turn(TURNS - 1, False, True)

        @block.scalar
        def _(act):
            act.dma_start(gates[:, 0:1], g_xattn.partition_broadcast(P)).then_inc(gate_in, 16)
            act.dma_start(gates[:, 1:2], g_ffn.partition_broadcast(P)).then_inc(gate_in, 16)
            act.wait_ge(gate_in, 32)
            nc.scalar.activation(tanh_g[:, :], gates[:, :], ACT.Tanh).then_inc(gate_ready, 1)

            def one(step):
                nxt, prep, post, route = step.to(1), step.to(2), step.to(-1), step.to(-2)

                def first_part(j):
                    act.wait_ge(qkf_ready, prep.count(QT, j + 1))
                    if prep.after_first(4, 0):
                        act.wait_ge(stack_a_ps, prep.count(4, 0))
                        act.wait_ge(stack_b_ps, prep.count(4, 0))
                    nc.scalar.copy(parts[j][:, :, :, 0, :],
                                   qkf[j].rearrange("p (t h d) -> p t h d", t=2, h=H)).then_inc(part1, 1)

                def second_part(j):
                    act.wait_ge(rest_ready, prep.count(QT, j + 1))
                    r = rest[j].rearrange("p (t h d) -> p t h d", t=2, h=H)
                    twice = [P, H, 2, HD]
                    nc.scalar.copy(parts[j][:, 0, :, 3:5, :], r[:, 0, :, :].unsqueeze(2).to_broadcast(twice))
                    nc.scalar.copy(parts[j][:, 1, :, 1:5:3, :], r[:, 1, :, :].unsqueeze(2).to_broadcast(twice)
                                   ).then_inc(part2, 1)

                def stack_out(n):
                    j, h0 = n % 2, HALF * (n // 2)
                    act.wait_ge(stack_b_ps, nxt.count(4, n + 1))
                    if nxt.after_first(H, -H):
                        act.wait_ge(st_ps, nxt.count(H, -H))
                    nc.scalar.copy(
                        k_st[nxt.turn()][0:KROWS, h0:h0 + 8, j * P:(j + 1) * P],
                        stack_b_bank[n][:, :].bitcast(BF16)[0:KROWS, :].rearrange("p (h s) -> p h s", h=8)
                    ).then_inc(stack_b_sb, 1)

                def heads_out(el, half):
                    act.wait_ge(pv_ps, el.count(4, 2 * half + 2))
                    if el.after_first(QT, 0):
                        act.wait_ge(heads_ps, el.count(QT, 0))
                    nc.scalar.copy(heads_t[half], pv_bank[:, :]).then_inc(heads_sb, 1)

                def max_out(el, half):
                    act.wait_ge(max_t_ps, el.count(2, half + 1))
                    if el.after_first(1, 0):
                        act.wait_ge(max_in[el.to(-1).turn()], el.to(-1).landed(32 * MROWS) - 16 * MROWS * (1 - half))
                    nc.scalar.copy(max_t[half][:, :], bank_c[:, :].bitcast(BF16)[0:MROWS * HALF, 0:S]
                                   ).then_inc(max_t_sb, 1)

                def leading_bits(n):
                    nc.scalar.copy(piece_hi(n), piece_raw(n)).then_inc(hi_ready, 1)

                def norm_apply(rstd_of, shift_of, source, target, done):
                    for j in range(QT):
                        nc.scalar.activation(target[:, j, :], source[:, j, :], ACT.Identity,
                                             scale=rstd_of[:, j:j + 1], bias=shift_of[:, j:j + 1]).then_inc(done, 1)

                for h in range(H):
                    if isinstance(step.i, int) and step.c == B - 1 and h >= 3 and h % 2 == 1 and (h - 3) // 2 < PIECES - 2:
                        if h == 3:
                            act.wait_ge(v_sb, QT * B)
                            act.wait_ge(fill_out, 48)
                            act.wait_ge(ffn_w_in, 16 * PIECES)
                        leading_bits((h - 3) // 2)
                    if nxt.live() and h < 4:
                        stack_out(h)
                    if step.live():
                        act.wait_ge(st_ps, step.count(H, h + 1))
                        if step.after_first(4, (h - NPROB) // GROUP + 1):
                            act.wait_ge(pv_ps, step.count(4, (h - NPROB) // GROUP + 1))
                        nc.scalar.activation(probs[h % NPROB], st_bank[h % 2][:, :], ACT.Exp,
                                             scale=float(HD) ** -0.5).then_inc(exp_done, 1)
                    if post.live() and h == 3:
                        heads_out(post, 1)
                    if isinstance(step.i, int) and step.c == B and h == 3:
                        leading_bits(PIECES - 2)
                        leading_bits(PIECES - 1)
                    if step.live() and h == 4:
                        max_out(step, 1)
                    if prep.live() and h == 4:
                        act.wait_ge(rstd_ready, prep.count(1, 1))
                        if prep.after_first(1, 0):
                            act.wait_ge(xhat_t_ps, prep.count(1, 0))
                        norm_apply(rstd, shift, xin[prep.turn()], xhat, xhat_ready)
                    if prep.live() and h == 5:
                        act.wait_ge(xhat_t_ps, prep.count(1, 1))
                        if prep.after_first(QT, 0):
                            act.wait_ge(proj_ps, prep.count(QT, 0))
                        nc.scalar.copy(xhat_t.rearrange("p t s -> p (t s)"), bank_c[:, :]).then_inc(xhat_t_sb, 1)
                    if prep.live() and h == 8:
                        first_part(0)
                    if route.live() and h == 8:
                        act.wait_ge(route_in, route.count(2, 2))
                        nc.scalar.activation(edge_e[:, :], edge[:, :], ACT.Exp).then_inc(route_exp, 1)
                    if nxt.live() and h == 11:
                        max_out(nxt, 0)
                    if post.live() and h == 11:
                        act.wait_ge(xn_t_ps, post.count(1, 1))
                        if post.after_first(1, 0):
                            act.wait_ge(logit_ps, post.count(1, 0))
                        nc.scalar.copy(xn_t.rearrange("p t s -> p (t s)"), bank_a[:, :]).then_inc(xn_t_sb, 1)
                    if prep.live() and h == 10:
                        second_part(0)
                    if prep.live() and h == 11:
                        first_part(1)
                    if step.live() and h == 12:
                        heads_out(step, 0)
                    if prep.live() and h == 13:
                        second_part(1)
                    if post.live() and h == 15:
                        act.wait_ge(route_in, post.count(2, 1))
                        nc.scalar.activation(ex[:, :, :], lg[:, :, :], ACT.Exp).then_inc(route_exp, 1)
            steps(act, one)

            def rows_out(n, number):
                act.wait_ge(rows_ps, number + 1)
                if not isinstance(number, int) or number >= 2:
                    act.wait_ge(up_ps, number - 1)
                nc.scalar.copy(rows_hi[n % 2][:, :, :].rearrange("p t s -> p (t s)"), bank[0][:, 0:DT * P]
                               ).then_inc(rows_hi_sb, 1)

            def silu_of(n, number):
                act.wait_ge(gate_ps, number + 1)
                if not isinstance(number, int) or number >= 2:
                    act.wait_ge(hid_ready, number - 1)
                nc.scalar.activation(silu[n % 2][:, :], gu_bank[n % 2][0][:, :], ACT.Silu).then_inc(silu_done, 1)

            def hidden_out(n, number):
                act.wait_ge(hid_ps, number + 1)
                if not isinstance(number, int) or number >= 2:
                    act.wait_ge(y_ps, number - 1)
                nc.scalar.copy(hid_t[n % 2][:, :, :].rearrange("p t s -> p (t s)"), bank[3][:, :]).then_inc(hid_sb, 1)

            def turn(i, last):
                for n in range(LAST_TILES if last else U):
                    number = U * i + n
                    silu_of(n, number)
                    if not (last and n == LAST_TILES - 1):
                        rows_out(n + 1, number + 1)
                    hidden_out(n, number)

            rows_out(0, 0)
            turn(0, False)
            with act.Fori(1, TURNS - 1) as i:
                turn(i, False)
            turn(TURNS - 1, True)

        @block.vector
        def _(dve):
            def spare_entries():
                dve.wait_ge(const_ready, 1)
                nc.vector.tensor_scalar(fill_id, fill_id, P - 1, None, ALU.bitwise_and
                                        ).then_inc(fill_step, 1)
                dve.wait_ge(fill_step, 1)
                nc.vector.tensor_scalar(fill[:, :, 0].bitcast(I32), fill_id, TOKENS, None, ALU.add
                                        ).then_inc(fill_ready, 1)

            def by_head(a, d=HD):
                return a.rearrange("p (h d) -> p h d", d=d)

            def row_stats(el, j, stats_of, source, steps_sem, used):
                if j == 0 and el.after_first(1, 0):
                    dve.wait_ge(used, el.count(1, 0))
                nc.vector.bn_stats(stats_of[:, j, :], source[:, j, :]).then_inc(steps_sem, 1)

            def norm_stats(el, stats_of, mv_of, steps_sem, done):
                for j in range(QT):
                    dve.wait_ge(steps_sem, el.count(4, j + 1))
                    dve.sem_inc(dve_went_on, 1)
                    nc.vector.bn_aggr(mv_of[:, j, :], stats_of[:, j, :]).then_inc(steps_sem, 1)
                dve.wait_ge(steps_sem, el.count(4, 4))
                nc.vector.tensor_scalar(mv_of[:, :, 0], mv_of[:, :, 0], -1.0, None, ALU.mult)
                nc.vector.tensor_scalar(mv_of[:, :, 1], mv_of[:, :, 1], EPS, None, ALU.add).then_inc(done, 1)

            def one(step):
                nxt, prep, post, route = step.to(1), step.to(2), step.to(-1), step.to(-2)

                def replicate(el, j):
                    dve.wait_ge(part3, el.count(QT, j + 1))
                    p = parts[j]
                    nc.vector.tensor_copy(p[:, 0, :, 1:3, :], p[:, 0, :, 0:1, :].to_broadcast([P, H, 2, HD]))
                    nc.vector.tensor_copy(p[:, 1, :, 3:6:2, :], p[:, 1, :, 0:1, :].to_broadcast([P, H, 2, HD])
                                          ).then_inc(parts_ready, 1)

                def project_out(j):
                    if j == 0:
                        dve.wait_ge(bias_in, 48)
                    dve.wait_ge(proj_ps, prep.count(QT, j + 1))
                    if prep.after_first(QT, j - 1):
                        dve.wait_ge(rest_ready, prep.count(QT, j - 1))
                    nc.vector.tensor_tensor(qkf[j], (bank_a, bank_b)[j][:, :], bqk,
                                            ALU.add).then_inc(qkf_ready, 1)

                def stack_out(n):
                    j, h0 = n % 2, HALF * (n // 2)
                    dve.wait_ge(stack_a_ps, nxt.count(4, n + 1))
                    if nxt.after_first(H, -H):
                        dve.wait_ge(st_ps, nxt.count(H, -H))
                    nc.vector.tensor_copy(
                        q_st[nxt.turn()][0:KROWS, h0:h0 + 8, j * P:(j + 1) * P],
                        bank_a[:, :].bitcast(BF16)[0:KROWS, :].rearrange("p (h s) -> p h s", h=8)
                    ).then_inc(stack_a_sb, 1)

                def gated_heads(j):
                    k = post.turn()
                    heads = by_head((bank_a, bank_b)[j][:, :], STRIP)
                    dve.wait_ge(heads_ps, post.count(QT, j + 1))
                    nc.vector.reciprocal(den[:, j, :], heads[:, :, HD]).then_inc(res_step, 1)
                    if j == 0 and post.second():
                        dve.wait_ge(x1_out[k], post.to(-2).landed())
                        dve.wait_ge(xn_ready, post.count(QT, -QT))
                    dve.wait_ge(res_step, post.count(QT, j + 1))
                    nc.vector.scalar_tensor_tensor(
                        out=by_head(x1[k][:, j, :]), in0=heads[:, :, 0:HD], scalar=tanh_g[:, 0:1],
                        in1=den[:, j, :].unsqueeze(2).to_broadcast([P, H, HD]), op0=ALU.mult, op1=ALU.mult
                    ).then_inc(heads_gated, 1)

                def step_done(k):
                    dve.wait_ge(route_step, route.count(ROUTE_STEPS, k))

                def over_e(a):
                    return a.unsqueeze(2).to_broadcast([P, QT, E])

                def over_j(a):
                    return a.unsqueeze(1).to_broadcast([P, QT, E])

                def route_logits():
                    dve.wait_ge(logit_ps, post.count(1, 1))
                    logits = bank_a[:, 0:QT * E].rearrange("p (j e) -> p j e", e=E)
                    nc.vector.tensor_reduce(top_lg[:, :], logits, AX.X, ALU.max).then_inc(logit_step, 1)
                    dve.wait_ge(logit_step, post.count(1, 1))
                    nc.vector.tensor_tensor(lg[:, :, :], logits, over_e(top_lg[:, :]), ALU.subtract
                                            ).then_inc(route_in, 1)

                def choose(n, chosen, top, k):
                    step_done(k + n)
                    if n == 0:
                        i = nc.vector.tensor_reduce(top[:, :], pr[:, :, :], AX.X, ALU.max)
                    elif n == 1:
                        i = nc.vector.tensor_tensor(eq[:, :, :], pr[:, :, :], over_e(top[:, :]), ALU.is_equal)
                    elif n == 2:
                        i = nc.vector.tensor_tensor(key[:, :, :], eq[:, :, :], over_j(prefer[:, :]), ALU.mult)
                    elif n == 3:
                        i = nc.vector.tensor_reduce(r1[:, :], key[:, :, :], AX.X, ALU.max)
                    else:
                        i = nc.vector.tensor_tensor(chosen[:, :, :], over_j(prefer[:, :]), over_e(r1[:, :]), ALU.is_equal)
                    i.then_inc(route_step, 1)

                def route_choice(n):
                    if n == 0:
                        dve.wait_ge(route_exp, route.count(2, 1))
                        nc.vector.tensor_reduce(r2[:, :], ex[:, :, :], AX.X, ALU.add).then_inc(route_step, 1)
                    elif n == 1:
                        step_done(1)
                        nc.vector.reciprocal(r1[:, :], r2[:, :]).then_inc(route_step, 1)
                    elif n == 2:
                        step_done(2)
                        nc.vector.tensor_tensor(pr[:, :, :], ex[:, :, :], over_e(r1[:, :]), ALU.mult
                                                ).then_inc(route_step, 1)
                    elif n < 8:
                        choose(n - 3, sel[0], best, 3)
                    elif n == 8:
                        step_done(8)
                        nc.vector.scalar_tensor_tensor(out=pr[:, :, :], in0=sel[0][:, :, :], scalar=-2.0,
                                                       in1=pr[:, :, :], op0=ALU.mult, op1=ALU.add
                                                       ).then_inc(route_step, 1)
                    elif n < 14:
                        choose(n - 9, sel[1], r2, 9)
                    elif n == 14:
                        step_done(14)
                        nc.vector.tensor_tensor(routed[:, :, :], sel[0][:, :, :], sel[1][:, :, :], ALU.add
                                                ).then_inc(routed_ready, 1)
                        nc.vector.tensor_tensor(edge[:, :], r2[:, :], best[:, :], ALU.subtract).then_inc(route_in, 1)

                def route_weights(n):
                    if n == 0:
                        dve.wait_ge(route_exp, route.count(2, 2))
                        nc.vector.tensor_scalar(r1[:, :], edge_e[:, :], 1.0, None, ALU.add).then_inc(route_step, 1)
                    elif n == 1:
                        step_done(15)
                        nc.vector.reciprocal(r2[:, :], r1[:, :]).then_inc(route_step, 1)
                    elif n == 2:
                        step_done(16)
                        nc.vector.tensor_scalar(best[:, :], r2[:, :], tanh_g[:, 1:2], None, ALU.mult
                                                ).then_inc(route_step, 1)

                def route_rows(n):
                    k = route.turn()
                    if n == 0:
                        dve.wait_ge(rank_ps, route.count(1, 1))
                        ranks = bank_b[:, 0:QT * E].rearrange("p (j e) -> p j e", e=E)
                        nc.vector.tensor_tensor(pos[:, :, :], ranks, over_j(base[:, :]), ALU.add
                                                ).then_inc(route_step, 1)
                    elif n == 1:
                        step_done(18)
                        nc.vector.tensor_tensor(base[:, :], base[:, :], bank_b[:, QT * E:(QT + 1) * E], ALU.add
                                                ).then_inc(rank_used, 1)
                        nc.vector.tensor_tensor(key[:, :, :], sel[0][:, :, :], pos[:, :, :], ALU.mult)
                        nc.vector.tensor_tensor(eq[:, :, :], sel[1][:, :, :], pos[:, :, :], ALU.mult
                                                ).then_inc(route_step, 1)
                    elif n == 2:
                        step_done(19)
                        nc.vector.tensor_reduce(slot_f[:, 0, :], key[:, :, :], AX.X, ALU.add)
                        nc.vector.tensor_reduce(slot_f[:, 1, :], eq[:, :, :], AX.X, ALU.add).then_inc(route_step, 1)
                    else:
                        step_done(20)
                        if route.second():
                            dve.wait_ge(table_out[k], route.to(-2).landed(16 * K_TOP * QT))
                        nc.vector.tensor_copy(slots[k][:, :], slot_f[:, :, :].rearrange("p k j -> p (k j)"))
                        for m in range(K_TOP):
                            i = nc.vector.tensor_copy(entry[k][:, m * QT:(m + 1) * QT, 0].bitcast(I32), token_f[:, :])
                        i.then_inc(route_step, 1)
                        nc.vector.tensor_copy(entry[k][:, 0:QT, 1], best[:, :])
                        nc.vector.tensor_tensor(entry[k][:, QT:2 * QT, 1], best[:, :], edge_e[:, :], ALU.mult
                                                ).then_inc(entry_ready, 1)
                        step_done(21)
                        nc.vector.tensor_scalar(token_f[:, :], token_f[:, :], float(S), None, ALU.add)

                def values_out(j):
                    if j == 0:
                        dve.wait_ge(bias_in, 48)
                        if nxt.after_first(4, -4):
                            dve.wait_ge(pv_ps, nxt.count(4, -4))
                    dve.wait_ge(v_ps, nxt.count(QT, QT))
                    nc.vector.tensor_tensor(
                        v_aug[nxt.turn()][:, j, :, 0:HD], by_head(bank_c[:, j * D:(j + 1) * D]),
                        by_head(bv_sb), ALU.add).then_inc(v_sb, 1)

                def heads_maxima(el, v):
                    dve.wait_ge(s_ps, el.count(H, v + 1))
                    nc.vector.tensor_reduce(
                        maxes[:, v // 8, (v // 4) % 2, 2 * (v % 4):2 * (v % 4) + 2],
                        s_bank[v % 2][:, :].rearrange("p (h s) -> p h s", h=2), AX.X, ALU.max
                    ).then_inc(max_done, 1)

                def split_maxima(el, half):
                    dve.wait_ge(max_done, el.count(H, 8 * (half + 1)))
                    if el.after_first(2, half - 1):
                        dve.wait_ge(max_t_ps, el.count(2, half - 1))
                    nc.vector.tensor_copy(max_parts[half][:, :, 0, :], maxes[:, half, :, :]).then_inc(max_step, 1)
                    dve.wait_ge(max_step, el.count(2, half + 1))
                    nc.vector.tensor_tensor(max_parts[half][:, :, 1, :], maxes[:, half, :, :],
                                            max_parts[half][:, :, 0, :], ALU.subtract).then_inc(max_ready, 1)

                for h in range(H):
                    if nxt.live() and h < 4:
                        stack_out(h)
                    if prep.live() and h == 8:
                        project_out(0)
                    if route.live() and h < 8:
                        route_choice(2 * h)
                    if step.live() and h == 0:
                        heads_maxima(step, S_LAST)
                    if step.live() and h == 2:
                        split_maxima(step, 1)
                    if route.live() and 10 <= h < 13:
                        route_weights(h - 10)
                    if nxt.live():
                        for v in S_UNITS[h]:
                            heads_maxima(nxt, v)
                    if isinstance(step.i, int) and step.c == B - 1 and h >= 16 - (PIECES - 3):
                        n = h - (16 - (PIECES - 3))
                        dve.wait_ge(hi_ready, n + 1)
                        lower_part(nc.vector, n).then_inc(lo_ready, 1)
                    if isinstance(step.i, int) and step.c == -2 and h == 3:
                        spare_entries()
                        for k in range(2):
                            nc.vector.memset(k_st[k][KROWS:P, :, :], -1.0)
                    if prep.live() and h < QT:
                        if h == 0:
                            dve.wait_ge(x_in[prep.turn()], prep.landed())
                        row_stats(prep, h, stats, xin[prep.turn()], norm_step, rstd_ready)
                    if prep.live() and h == 2:
                        norm_stats(prep, stats, mv, norm_step, var_ready)
                    if route.live() and h < 7:
                        route_choice(2 * h + 1)
                    if post.live() and h == 5:
                        gated_heads(0)
                    if post.live() and h == 6:
                        gated_heads(1)
                        if last_element(post):
                            dve.wait_ge(xres_in[post.turn()], post.landed())
                            dve.wait_ge(heads_gated, post.count(QT, QT))
                            for j in range(QT):
                                nc.vector.tensor_tensor(x1[post.turn()][:, j, :], x1[post.turn()][:, j, :],
                                                        xres[post.turn()][:, j, :], ALU.add).then_inc(x1_ready, 1)
                    if post.live() and h == 7:
                        dve.wait_ge(x1_ready, post.count(QT, QT))
                        for j in range(QT):
                            row_stats(post, j, stats2, x1[post.turn()], norm2_step, rstd2_ready)
                        norm_stats(post, stats2, mv2, norm2_step, var2_ready)
                    if post.live() and h == 8:
                        k = post.turn()
                        dve.wait_ge(rstd2_ready, post.count(1, 1))
                        if post.second():
                            dve.wait_ge(xn_out[k], post.to(-2).landed())
                            dve.wait_ge(xn_t_ps, post.count(1, -1))
                        for j in range(QT):
                            nc.vector.tensor_scalar(xn[k][:, j, :], x1[k][:, j, :], rstd2[:, j:j + 1],
                                                    shift2[:, j:j + 1], ALU.mult, ALU.add).then_inc(xn_ready, 1)
                    if nxt.live() and h == 9:
                        values_out(0)
                        values_out(1)
                    if nxt.live() and h == 9:
                        split_maxima(nxt, 0)
                    if prep.live() and h == 10:
                        project_out(1)
                    if prep.live() and h == 12:
                        replicate(prep, 0)
                    if route.live() and h == 13 and not step.live():
                        for n in range(4):
                            route_rows(n)
                    if isinstance(step.i, int) and step.c == B and h == 13:
                        dve.wait_ge(hi_ready, PIECES - 1)
                        lower_part(nc.vector, PIECES - 2).then_inc(lo_ready, 1)
                    if post.live() and h == 14:
                        route_logits()
                    if route.live() and h == 14 and step.live():
                        route_rows(0)
                        route_rows(1)
                    if route.live() and h == 15 and step.live():
                        route_rows(2)
                    if prep.live() and h == 15:
                        replicate(prep, 1)
                    if route.live() and h == 15 and step.live():
                        route_rows(3)

            steps(dve, one)

            done = [0]

            def plan(instruction):
                done[0] += 1
                instruction.then_inc(plan_step, 1)
                dve.wait_ge(plan_step, done[0])

            dve.wait_ge(rank_used, B)
            plan(nc.vector.tensor_scalar(cum_a[:, :], prefer[:, :], float(TOKENS), float(P - 1 - TOKENS * E),
                                         ALU.mult, ALU.add))
            plan(nc.vector.tensor_tensor(cum_b[:, :], base[:, :], cum_a[:, :], ALU.add))
            plan(nc.vector.tensor_copy(count_i[:, :], cum_b[:, :]))
            plan(nc.vector.tensor_scalar(count_i[:, :], count_i[:, :], P.bit_length() - 1, None,
                                         ALU.arith_shift_right))
            plan(nc.vector.tensor_copy(n_tiles[:, :], count_i[:, :]))
            plan(nc.vector.tensor_copy(cum_a[:, :], n_tiles[:, :]))
            a, b = cum_a, cum_b
            for shift in (1, 2, 4):
                nc.vector.tensor_copy(b[:, 0:shift], a[:, 0:shift])
                plan(nc.vector.tensor_tensor(b[:, shift:E], a[:, shift:E], a[:, 0:E - shift], ALU.add))
                a, b = b, a
            shape = [P, MAX_TILES, E]
            plan(nc.vector.tensor_tensor(past[:, :, :], tile_no[:, :].unsqueeze(2).to_broadcast(shape),
                                         a[:, :].unsqueeze(1).to_broadcast(shape), ALU.is_ge))
            plan(nc.vector.tensor_reduce(t_exp[:, :], past[:, :, :], AX.X, ALU.add))
            plan(nc.vector.tensor_tensor(past_n[:, :, :], past[:, :, :],
                                         n_tiles[:, :].unsqueeze(1).to_broadcast(shape), ALU.mult))
            plan(nc.vector.tensor_reduce(t_row[:, :], past_n[:, :, :], AX.X, ALU.add))
            plan(nc.vector.tensor_tensor(t_row[:, :], tile_no[:, :], t_row[:, :], ALU.subtract))
            plan(nc.vector.tensor_scalar(t_row[:, :], t_row[:, :], float(P), None, ALU.mult))
            plan(nc.vector.scalar_tensor_tensor(out=t_row[:, :], in0=t_exp[:, :], scalar=float(TOKENS),
                                                in1=t_row[:, :], op0=ALU.mult, op1=ALU.add))
            plan(nc.vector.tensor_scalar(t_exp[:, :], t_exp[:, :], float(E - 1), None, ALU.min))
            plan(nc.vector.tensor_copy(plan_exp[:, :], t_exp[:, :]))
            nc.vector.tensor_copy(plan_row[:, :], t_row[:, :]).then_inc(plan_ready, 1)

            def rows_out(n, number):
                dve.wait_ge(rows_hi_sb, number + 1)
                if not isinstance(number, int) or number >= 2:
                    dve.wait_ge(up_ps, number - 1)
                nc.vector.tensor_tensor(rows_lo[n % 2][:, :, :].rearrange("p t s -> p (t s)"), bank[0][:, 0:DT * P],
                                        rows_hi[n % 2][:, :, :].rearrange("p t s -> p (t s)").bitcast(F32), ALU.subtract
                                        ).then_inc(rows_sb, 1)

            def hidden(n, number):
                dve.wait_ge(silu_done, number + 1)
                dve.wait_ge(up_ps, number + 1)
                if not isinstance(number, int) or number >= 2:
                    dve.wait_ge(hid_ps, number - 1)
                nc.vector.tensor_tensor(hid[n % 2][:, :], silu[n % 2][:, :], gu_bank[n % 2][1][:, :], ALU.mult).then_inc(hid_ready, 1)

            def weigh(n, number):
                dve.wait_ge(y_ps, number + 1)
                if not isinstance(number, int) or number >= 2:
                    dve.wait_ge(y_out, 16 * (number - 1))
                nc.vector.tensor_scalar(y_sb[n % 2][:, :], bank[4][:, 0:D], row_info[n % NW][:, 1:2], None, ALU.mult
                                        ).then_inc(y_ready, 1)

            def turn(i, first, last):
                for n in range(LAST_TILES if last else U):
                    number = U * i + n
                    hidden(n, number)
                    if not (last and n == LAST_TILES - 1):
                        rows_out(n + 1, number + 1)
                    if not (first and n == 0):
                        weigh(n - 1, number - 1)

            rows_out(0, 0)
            turn(0, True, False)
            with dve.Fori(1, TURNS - 1) as i:
                turn(i, False, False)
            turn(TURNS - 1, False, True)
            weigh(LAST_TILES - 1, MAX_TILES - 1)

        @block.tensor
        def _(pe):
            def one(step):
                nxt, prep, post, route = step.to(1), step.to(2), step.to(-1), step.to(-2)

                def stack(n, t):
                    j, h0 = n % 2, HALF * (n // 2)
                    to, used = ((bank_a, stack_a_sb), (stack_b_bank[n], stack_b_sb))[t]
                    pe.wait_ge(parts_ready, nxt.count(QT, j + 1))
                    if t == 1 and n == 3:
                        if step.live():
                            pe.wait_ge(max_t_sb, step.count(2, 1))
                        else:
                            pe.wait_ge(xhat_t_sb, nxt.count(1, 1))
                    elif n:
                        pe.wait_ge(used, nxt.count(4, n))
                    elif t == 0 and route.live():
                        pe.wait_ge(route_in, route.count(2, 1))
                    elif t == 1 and step.to(-3).live():
                        pe.wait_ge(rank_used, step.to(-3).count(1, 1))
                    for h in range(8):
                        i = nc.tensor.transpose(to[:, :].bitcast(BF16)[0:KROWS, h * P:(h + 1) * P],
                                                parts[j][:, t, h0 + h, :, :].rearrange("p r d -> p (r d)"),
                                                ident_b[:, :])
                    i.then_inc((stack_a_ps, stack_b_ps)[t], 1)

                def project(lhs, j, w, to, done):
                    for dt in range(DT):
                        i = nc.tensor.matmul(to, lhs[:, dt, j * P:(j + 1) * P], w[:, dt, :],
                                             start=dt == 0, stop=dt == DT - 1)
                    if done is not None:
                        i.then_inc(done, 1)

                def values(el, g):
                    pe.wait_ge(exp_done, el.count(H, GROUP * (g + 1)))
                    if g == 0:
                        pe.wait_ge(v_sb, el.count(QT, QT))
                    if g % 2 == 0 and el.after_first(QT, g // 2):
                        pe.wait_ge(heads_sb, el.count(QT, g // 2))
                    for kt in range(QT):
                        for s in range(GROUP):
                            h = GROUP * g + s
                            i = nc.tensor.matmul(
                                pv_bank[STRIP * s:STRIP * (s + 1), (g % 2) * S:(g % 2 + 1) * S],
                                v_aug[el.turn()][:, kt, h, :], probs[h % NPROB][:, kt * S:(kt + 1) * S],
                                start=kt == 0, stop=kt == QT - 1, tile_position=(0, STRIP * s))
                    i.then_inc(pv_ps, 1)

                def scores(el, v):
                    k, j, h0 = el.turn(), (v // 4) % 2, HALF * (v // 8) + 2 * (v % 4)
                    if v % 8 == 0:
                        pe.wait_ge(stack_a_sb, el.count(4, v // 4 + 2))
                        pe.wait_ge(stack_b_sb, el.count(4, v // 4 + 2))
                    if el.after_first(H, v - 1):
                        pe.wait_ge(max_done, el.count(H, v - 1))
                    for h in (h0, h0 + 1):
                        i = nc.tensor.matmul(s_bank[v % 2][:, (h - h0) * S:(h - h0 + 1) * S],
                                             q_st[k][0:KROWS, h, j * P:(j + 1) * P], k_st[k][0:KROWS, h, :],
                                             start=True, stop=True)
                    i.then_inc(s_ps, 1)

                def maxima_t(el, half, to):
                    pe.wait_ge(max_ready, el.count(2, half + 1))
                    for j in range(QT):
                        i = nc.tensor.transpose(
                            to[:, :].bitcast(BF16)[0:MROWS * HALF, j * P:(j + 1) * P],
                            max_parts[half][:, j, :, :].rearrange("p m h -> p (m h)"), ident_b[:, :])
                    i.then_inc(max_t_ps, 1)

                for h in range(H):
                    if nxt.live() and h < 4:
                        stack(h, 1)
                    if step.live():
                        k = step.turn()
                        if h == 0:
                            pe.wait_ge(max_in[k], step.landed(32 * MROWS) - 16 * MROWS)
                            pe.wait_ge(stack_a_sb, step.count(4, 4))
                            pe.wait_ge(stack_b_sb, step.count(4, 4))
                        if h == HALF:
                            pe.wait_ge(max_in[k], step.landed(32 * MROWS))
                        if step.after_first(H, h - 1):
                            pe.wait_ge(exp_done, step.count(H, h - 1))
                        for kt in range(QT):
                            i = nc.tensor.matmul(st_bank[h % 2][:, kt * S:(kt + 1) * S],
                                                 k_st[k][0:KROWS + MROWS, h, kt * P:(kt + 1) * P],
                                                 q_st[k][0:KROWS + MROWS, h, :], start=True, stop=True)
                        i.then_inc(st_ps, 1)
                    if nxt.live() and h < 4:
                        stack(h, 0)
                    if step.live() and h == 0:
                        scores(step, S_LAST)
                    if nxt.live():
                        for v in S_UNITS[h][0:1]:
                            scores(nxt, v)
                    if nxt.live() and h == 11:
                        pe.wait_ge(v_sb, nxt.count(QT, QT))
                        maxima_t(nxt, 0, bank_c)
                    if step.live() and h in (5, 11, 14):
                        values(step, (5, 11, 14).index(h))
                    if post.live() and h == 2:
                        values(post, 3)
                    if post.live() and h == 5:
                        pe.wait_ge(heads_sb, post.count(QT, QT))
                        if nxt.live():
                            pe.wait_ge(stack_a_sb, nxt.count(4, 4))
                            pe.wait_ge(stack_b_sb, nxt.count(4, 3))
                        if route.live():
                            pe.wait_ge(route_in, route.count(2, 1))
                        if step.to(-3).live():
                            pe.wait_ge(rank_used, step.to(-3).count(1, 1))
                        for j in range(QT):
                            for n in range(4):
                                i = nc.tensor.transpose(
                                    (bank_a, bank_b)[j][:, n * P:(n + 1) * P],
                                    heads_t[n // 2][:, (n % 2) * S + j * P:(n % 2) * S + (j + 1) * P], ident[:, :])
                            i.then_inc(heads_ps, 1)
                    if step.live() and h == 4:
                        pe.wait_ge(max_t_sb, step.count(2, 1))
                        if nxt.live():
                            pe.wait_ge(stack_b_sb, nxt.count(4, 4))
                        maxima_t(step, 1, bank_c)
                    if prep.live() and h == 5:
                        pe.wait_ge(xhat_ready, prep.count(QT, QT))
                        if step.live():
                            pe.wait_ge(max_t_sb, step.count(2, 2))
                        elif nxt.live():
                            pe.wait_ge(stack_b_sb, nxt.count(4, 4))
                        for dt in range(DT):
                            for j in range(QT):
                                i = nc.tensor.transpose(bank_c[:, dt * S + j * P:dt * S + (j + 1) * P],
                                                        xhat[:, j, dt * P:(dt + 1) * P], ident[:, :])
                        i.then_inc(xhat_t_ps, 1)
                    if prep.live() and h in (7, 9):
                        j = (h - 7) // 2
                        to = (bank_a, bank_b)[j]
                        if h == 7:
                            pe.wait_ge(qk_w_in, 32)
                            pe.wait_ge(ctx_in[prep.turn()], prep.landed())
                            pe.wait_ge(xhat_t_sb, prep.count(1, 1))
                        if post.live():
                            pe.wait_ge(heads_gated, post.count(QT, j + 1))
                        elif nxt.live():
                            pe.wait_ge((stack_a_sb, stack_b_sb)[j], nxt.count(4, 4 - j))
                        project(xhat_t, j, wq_sb, to[:, 0:D], None)
                        project(ctx_sb[prep.turn()], j, wk_sb, to[:, D:2 * D], proj_ps)
                    if nxt.live() and h == 8:
                        pe.wait_ge(stack_b_sb, nxt.count(4, 4))
                        if step.live():
                            pe.wait_ge(max_t_sb, step.count(2, 2))
                        if prep.live():
                            pe.wait_ge(xhat_t_sb, prep.count(1, 1))
                        pe.wait_ge(v_w_in, 16)
                        pe.wait_ge(ctx_in[nxt.turn()], nxt.landed())
                        for j in range(QT):
                            project(ctx_sb[nxt.turn()], j, wv_sb, bank_c[:, j * D:(j + 1) * D], v_ps)
                    if post.live() and h == 10:
                        pe.wait_ge(xn_ready, post.count(QT, QT))
                        pe.wait_ge(heads_gated, post.count(QT, QT))
                        if nxt.live():
                            pe.wait_ge(stack_a_sb, nxt.count(4, 4))
                        if prep.live():
                            pe.wait_ge(qkf_ready, prep.count(QT, 1))
                        if route.live():
                            pe.wait_ge(route_in, route.count(2, 1))
                        for dt in range(DT):
                            for j in range(QT):
                                i = nc.tensor.transpose(bank_a[:, dt * S + j * P:dt * S + (j + 1) * P],
                                                        xn[post.turn()][:, j, dt * P:(dt + 1) * P], ident[:, :])
                        i.then_inc(xn_t_ps, 1)
                    if post.live() and h in (12, 13):
                        pe.wait_ge(xn_t_sb, post.count(1, 1))
                        pe.wait_ge(r_w_in, 16)
                        j = h - 12
                        project(xn_t, j, wr_sb, bank_a[:, j * E:(j + 1) * E], logit_ps if j == QT - 1 else None)
                    if route.live() and h == (12 if step.live() else 9):
                        pe.wait_ge(routed_ready, route.count(1, 1))
                        if prep.live():
                            pe.wait_ge(qkf_ready, prep.count(QT, QT))
                        if nxt.live():
                            pe.wait_ge(stack_b_sb, nxt.count(4, 4))
                        if post.live():
                            pe.wait_ge(heads_gated, post.count(QT, QT))
                        if step.to(-3).live():
                            pe.wait_ge(rank_used, step.to(-3).count(1, 1))
                        nc.tensor.matmul(bank_b[:, 0:E], earlier[:, :], routed[:, 0, :], start=True, stop=True)
                        nc.tensor.matmul(bank_b[:, E:2 * E], earlier[:, :], routed[:, 1, :], start=True, stop=False)
                        nc.tensor.matmul(bank_b[:, E:2 * E], ones_b[:, :], routed[:, 0, :], start=False, stop=True)
                        nc.tensor.matmul(bank_b[:, 2 * E:3 * E], ones_b[:, :], routed[:, 0, :], start=True, stop=False)
                        nc.tensor.matmul(bank_b[:, 2 * E:3 * E], ones_b[:, :], routed[:, 1, :], start=False,
                                         stop=True).then_inc(rank_ps, 1)
                    if nxt.live():
                        for v in S_UNITS[h][1:]:
                            scores(nxt, v)

            pe.wait_ge(const_ready, 1)
            steps(pe, one)


            def rows_in_t(n, number, landed):
                pe.wait_ge(rows_got[n % NX], landed)
                for dt in range(DT):
                    i = nc.tensor.transpose(bank[0][:, dt * P:(dt + 1) * P], rows_in[n % NX][:, dt * P:(dt + 1) * P],
                                            ident[:, :])
                i.then_inc(rows_ps, 1)

            def gate_up(n, number, expert):
                pe.wait_ge(rows_sb, number + 1)
                if not isinstance(number, int) or number > 1:
                    pe.wait_ge(hid_ready, number - 1)
                for g, done in enumerate((gate_ps, up_ps)):
                    for dt in range(DT):
                        lo = w_lo[:, dt, g, :]
                        for m, (rows, w) in enumerate(((rows_hi, hi[dt][g]), (rows_hi, lo), (rows_lo, hi[dt][g]))):
                            i = nc.tensor.matmul(gu_bank[n % 2][g][:, :], rows[n % 2][:, dt, :],
                                                 w[:, bass.ds(expert * F, F)],
                                                 start=dt == 0 and m == 0, stop=dt == DT - 1 and m == 2)
                    i.then_inc(done, 1)

            def down(n, number, expert):
                pe.wait_ge(hid_sb, number + 1)
                if not isinstance(number, int) or number > 0:
                    pe.wait_ge(y_ready, number)
                for ft in range(FT):
                    i = nc.tensor.matmul(bank[4][:, 0:D], hid_t[n % 2][:, ft, :],
                                         w_dn[:, ft, bass.ds(expert * D, D)], start=ft == 0, stop=ft == FT - 1)
                i.then_inc(y_ps, 1)

            def hidden_t(n, number):
                pe.wait_ge(hid_ready, number + 1)
                if not isinstance(number, int) or number > 0:
                    pe.wait_ge(hid_sb, number)
                for ft in range(FT):
                    i = nc.tensor.transpose(bank[3][:, ft * P:(ft + 1) * P], hid[n % 2][:, ft * P:(ft + 1) * P],
                                            ident[:, :])
                i.then_inc(hid_ps, 1)

            def load_expert(number):
                return pe.value_load(plan_exp[0:1, number], min_val=0, max_val=E - 1)

            def turn(i, first, last):
                expert = None if first else load_expert(bass.ds(U * i - 1, 1) if not isinstance(i, int) else
                                                        slice(U * i - 1, U * i))
                for n in range(LAST_TILES if last else U):
                    number = U * i + n
                    before = expert
                    expert = load_expert(slice(number, number + 1) if isinstance(number, int) else bass.ds(number, 1))
                    gate_up(n, number, expert)
                    if not (last and n == LAST_TILES - 1):
                        rows_in_t(n + 1, number + 1, 16 * ((U // NX) * i + (n + 1) // NX + 1))
                    if not (first and n == 0):
                        down(n - 1, number - 1, before)
                    hidden_t(n, number)

            pe.wait_ge(plan_ready, 1)
            pe.wait_ge(hi_ready, PIECES)
            pe.wait_ge(lo_ready, PIECES - 2)
            pe.wait_ge(pool_lo_ready, 2)
            pe.wait_ge(down_w_in, 16 * FT)
            rows_in_t(0, 0, 16)
            turn(0, True, False)
            with pe.Fori(1, TURNS - 1) as i:
                turn(i, False, False)
            turn(TURNS - 1, False, True)
            down(LAST_TILES - 1, MAX_TILES - 1, load_expert(slice(MAX_TILES - 1, MAX_TILES)))


def kernel(x, ctx_1024, g_xattn, g_ffn, L0_xattn_Wq, L0_xattn_bq, L0_xattn_Wk, L0_xattn_bk, L0_xattn_Wv,
           L0_xattn_bv, L0_ffn_router_kernel_DE, L0_ffn_kernel_gating_EDF, L0_ffn_kernel_up_EDF,
           L0_ffn_kernel_down_EFD):
    import concourse.bacc as bacc
    from concourse.bass_utils import run_bass_kernel_spmd

    def laid(a):
        return np.ascontiguousarray(np.asarray(a))

    arrays = {
        "x": laid(x),
        "ctx_t": laid(np.asarray(ctx_1024).reshape(TOKENS, D).T),
        "g_xattn": laid(g_xattn),
        "g_ffn": laid(g_ffn),
        "wq_t": laid(np.asarray(L0_xattn_Wq).T),
        "bq": laid(L0_xattn_bq),
        "wk_t": laid(np.asarray(L0_xattn_Wk).T),
        "bk": laid(L0_xattn_bk),
        "wv_t": laid(np.asarray(L0_xattn_Wv).T),
        "bv": laid(L0_xattn_bv),
        "w_router": laid(L0_ffn_router_kernel_DE),
        "w_gate": laid(L0_ffn_kernel_gating_EDF),
        "w_up": laid(L0_ffn_kernel_up_EDF),
        "w_down": laid(L0_ffn_kernel_down_EFD),
    }
    nc = bacc.Bacc("TRN2", target_bir_lowering=False, num_devices=1)
    args = [nc.dram_tensor(f"in_{n}", a.shape, mybir.dt.from_np(a.dtype), kind="ExternalInput").ap()
            for n, a in arrays.items()]
    out = nc.dram_tensor("out_rows", (TOKENS + SPARE, D), F32, kind="ExternalOutput").ap()
    program(nc, *args, out)
    r = run_bass_kernel_spmd(nc, [{f"in_{n}": a for n, a in arrays.items()}], core_ids=[0])
    return r.results[0]["out_rows"][:TOKENS].reshape(B, S, D)
```
